# Optimizing a Trainium2 kernel written in Bass

```python
import numpy as np
import jax
import jax.numpy as jnp

def _softmax(x, axis=-1):
    return jax.nn.softmax(x, axis=axis)

def _gelu(x):
    return jax.nn.gelu(x, approximate=True)

def _silu(x):
    return jax.nn.silu(x)

def _sigmoid(x):
    return jax.nn.sigmoid(x)

def _layernorm(x, axis=-1, eps=1e-05):
    m = jnp.mean(x, axis=axis, keepdims=True)
    v = jnp.var(x, axis=axis, keepdims=True)
    return (x - m) / jnp.sqrt(v + eps)

def _scatter_add(tgt, idx, src, axis=0):
    return tgt.at[idx].add(src)

def _segment_sum(src, seg, n):
    return jax.ops.segment_sum(src, seg, n)
kernel_name = 'mk_adj_resnorm_d4_adj_r2_721101'

def setup_inputs(seed: int=0):
    np.random.seed(seed)
    _w = jnp.asarray

    def _rec_inputs():
        import jax
        import jax.numpy as jnp
        _gk = jax.random.key(seed)
        x = -0.0005207 + 1.001 * jax.random.normal(jax.random.fold_in(_gk, 1), (128, 128, 128), jnp.float32)
        _a = jax.random.bernoulli(jax.random.fold_in(_gk, 2), 0.03125, (128, 128, 128))
        _af = _a.astype(jnp.float32)
        adj = _af
        return (x, adj)
    x, adj = _rec_inputs()

    def _L0_gnn_setup():
        import jax, jax.numpy as jnp
        import numpy as np
        DIM = 128
        HEADS = 8
        BS = 8
        N = 512
        NEG = -1000000000.0
        key = jax.random.key(seed)
        ks = jax.random.split(key, 8)
        feats = jax.random.normal(ks[0], (BS, N, DIM), dtype=jnp.float32)
        adj_mat = (jax.random.uniform(ks[1], (BS, N, N)) < 0.1).astype(jnp.float32)
        s = 1.0 / np.sqrt(DIM)
        fc_w = jax.random.normal(ks[2], (DIM, DIM * HEADS), dtype=jnp.float32) * s
        fc_b = jnp.zeros((DIM * HEADS,), dtype=jnp.float32)
        q_w = jax.random.normal(ks[3], (DIM, 1), dtype=jnp.float32) * s
        q_b = jnp.zeros((1,), dtype=jnp.float32)
        k_w = jax.random.normal(ks[4], (DIM, 1), dtype=jnp.float32) * s
        k_b = jnp.zeros((1,), dtype=jnp.float32)
        fp_w = jax.random.normal(ks[5], (DIM * HEADS, DIM), dtype=jnp.float32) * (1.0 / np.sqrt(DIM * HEADS))
        fp_b = jnp.zeros((DIM,), dtype=jnp.float32)
        return {'feats': feats, 'adj_mat': adj_mat, 'fc_w': fc_w, 'fc_b': fc_b, 'q_w': q_w, 'q_b': q_b, 'k_w': k_w, 'k_b': k_b, 'fp_w': fp_w, 'fp_b': fp_b}
    _L0_gnn_all = _L0_gnn_setup()
    _L0_gnn_in = {k: v for k, v in _L0_gnn_all.items() if k in ('fc_w', 'fc_b', 'q_w', 'q_b', 'k_w', 'k_b', 'fp_w', 'fp_b')}
    del _L0_gnn_all

    def _L1_gnn_setup():
        import jax, jax.numpy as jnp
        import numpy as np
        B, N, D, H = (8, 1024, 128, 512)
        RMS_EPS = 1e-06

        def _rmsnorm(h, w, eps=RMS_EPS):
            var = jnp.mean(jnp.square(h), axis=-1, keepdims=True)
            return h * jax.lax.rsqrt(var + eps) * w
        key = jax.random.key(seed)
        ks = jax.random.split(key, 5)
        x = jax.random.normal(ks[0], (B, N, D), dtype=jnp.float32)
        adjacency = jax.random.uniform(ks[1], (B, N, N), dtype=jnp.float32)
        epsilon = jnp.zeros((), dtype=jnp.float32)
        W1 = jax.random.normal(ks[2], (D, H), dtype=jnp.float32) * (1.0 / np.sqrt(D))
        b1 = jnp.zeros((H,), dtype=jnp.float32)
        rms_weight = jnp.ones((H,), dtype=jnp.float32)
        W2 = jax.random.normal(ks[3], (H, D), dtype=jnp.float32) * (1.0 / np.sqrt(H))
        b2 = jnp.zeros((D,), dtype=jnp.float32)
        return {'x': x, 'adjacency': adjacency, 'epsilon': epsilon, 'W1': W1, 'b1': b1, 'rms_weight': rms_weight, 'W2': W2, 'b2': b2}
    _L1_gnn_all = _L1_gnn_setup()
    _L1_gnn_in = {k: v for k, v in _L1_gnn_all.items() if k in ('epsilon', 'W1', 'b1', 'rms_weight', 'W2', 'b2')}
    del _L1_gnn_all

    def _L2_gnn_setup():
        import jax, jax.numpy as jnp
        import numpy as np
        D_IN = 128
        D_HID = 256
        key = jax.random.key(seed)
        k1, k2, k3, k4, k5, k6 = jax.random.split(key, 6)
        x = jax.random.normal(k1, (8, 2048, D_IN), dtype=jnp.float32)
        adj = jax.random.uniform(k2, (8, 2048, 2048), dtype=jnp.float32)
        s1 = 1.0 / np.sqrt(D_IN)
        s2 = 1.0 / np.sqrt(D_HID)
        W1 = jax.random.uniform(k3, (D_IN, D_HID), dtype=jnp.float32, minval=-s1, maxval=s1)
        b1 = jax.random.uniform(k4, (D_HID,), dtype=jnp.float32, minval=-s1, maxval=s1)
        W2 = jax.random.uniform(k5, (D_HID, D_IN), dtype=jnp.float32, minval=-s2, maxval=s2)
        b2 = jax.random.uniform(k6, (D_IN,), dtype=jnp.float32, minval=-s2, maxval=s2)
        eps = jnp.zeros((1,), dtype=jnp.float32)
        return {'x': x, 'adj': adj, 'eps': eps, 'W1': W1, 'b1': b1, 'W2': W2, 'b2': b2}
    _L2_gnn_all = _L2_gnn_setup()
    _L2_gnn_in = {k: v for k, v in _L2_gnn_all.items() if k in ('eps', 'W1', 'b1', 'W2', 'b2')}
    del _L2_gnn_all

    def _L3_gnn_setup():
        import jax, jax.numpy as jnp
        import numpy as np
        B, N, D = (4, 2048, 128)
        DENSITY = 0.02
        key = jax.random.key(seed)
        kx, ka1, ka2, kwt, kbt, kwh, kth = jax.random.split(key, 7)
        x = jax.random.normal(kx, (B, N, D), dtype=jnp.float32)
        mask = jax.random.uniform(ka1, (B, N, N)) < DENSITY
        vals = jax.random.uniform(ka2, (B, N, N), dtype=jnp.float32)
        adj = jnp.where(mask, vals, 0.0).astype(jnp.float32)
        s = 0.02
        W_t = s * jax.random.normal(kwt, (D, D), dtype=jnp.float32)
        b_t = s * jax.random.normal(kbt, (D,), dtype=jnp.float32)
        W_h = s * jax.random.normal(kwh, (D, D), dtype=jnp.float32)
        theta = s * jax.random.normal(kth, (D, D), dtype=jnp.float32)
        return {'x': x, 'adj': adj, 'W_t': W_t, 'b_t': b_t, 'W_h': W_h, 'theta': theta}
    _L3_gnn_all = _L3_gnn_setup()
    _L3_gnn_in = {k: v for k, v in _L3_gnn_all.items() if k in ('W_t', 'b_t', 'W_h', 'theta')}
    del _L3_gnn_all
    return {'x': x, 'adj': adj, 'L0_gnn_fc_w': _L0_gnn_in['fc_w'], 'L0_gnn_fc_b': _L0_gnn_in['fc_b'], 'L0_gnn_q_w': _L0_gnn_in['q_w'], 'L0_gnn_q_b': _L0_gnn_in['q_b'], 'L0_gnn_k_w': _L0_gnn_in['k_w'], 'L0_gnn_k_b': _L0_gnn_in['k_b'], 'L0_gnn_fp_w': _L0_gnn_in['fp_w'], 'L0_gnn_fp_b': _L0_gnn_in['fp_b'], 'L1_gnn_epsilon': _L1_gnn_in['epsilon'], 'L1_gnn_W1': _L1_gnn_in['W1'], 'L1_gnn_b1': _L1_gnn_in['b1'], 'L1_gnn_rms_weight': _L1_gnn_in['rms_weight'], 'L1_gnn_W2': _L1_gnn_in['W2'], 'L1_gnn_b2': _L1_gnn_in['b2'], 'L2_gnn_eps': _L2_gnn_in['eps'], 'L2_gnn_W1': _L2_gnn_in['W1'], 'L2_gnn_b1': _L2_gnn_in['b1'], 'L2_gnn_W2': _L2_gnn_in['W2'], 'L2_gnn_b2': _L2_gnn_in['b2'], 'L3_gnn_W_t': _L3_gnn_in['W_t'], 'L3_gnn_b_t': _L3_gnn_in['b_t'], 'L3_gnn_W_h': _L3_gnn_in['W_h'], 'L3_gnn_theta': _L3_gnn_in['theta']}

def reference(x, adj, L0_gnn_fc_w, L0_gnn_fc_b, L0_gnn_q_w, L0_gnn_q_b, L0_gnn_k_w, L0_gnn_k_b, L0_gnn_fp_w, L0_gnn_fp_b, L1_gnn_epsilon, L1_gnn_W1, L1_gnn_b1, L1_gnn_rms_weight, L1_gnn_W2, L1_gnn_b2, L2_gnn_eps, L2_gnn_W1, L2_gnn_b1, L2_gnn_W2, L2_gnn_b2, L3_gnn_W_t, L3_gnn_b_t, L3_gnn_W_h, L3_gnn_theta):
    import jax
    import jax.numpy as jnp

    def _L0_gnn_ref(feats, adj_mat, fc_w, fc_b, q_w, q_b, k_w, k_b, fp_w, fp_b):
        import jax, jax.numpy as jnp
        import numpy as np
        DIM = 128
        HEADS = 8
        BS = 8
        N = 512
        NEG = -1000000000.0
        bs, n, dim = feats.shape
        feat_proj = (feats @ fc_w + fc_b).reshape(bs, n, HEADS, dim).transpose(0, 2, 1, 3)
        q = feat_proj @ q_w + q_b
        k = feat_proj @ k_w + k_b
        logits = q + jnp.swapaxes(k, -1, -2)
        masked = logits + (1.0 - adj_mat[:, None]) * NEG
        masked = jax.nn.leaky_relu(masked, negative_slope=0.01)
        attn = jax.nn.softmax(masked, axis=-1)
        out = attn @ feat_proj
        out = out.transpose(0, 2, 1, 3).reshape(bs, n, HEADS * dim)
        out = out @ fp_w + fp_b + feats
        return jax.nn.sigmoid(out)

    def _L1_gnn_ref(x, adjacency, epsilon, W1, b1, rms_weight, W2, b2):
        import jax, jax.numpy as jnp
        import numpy as np
        B, N, D, H = (8, 1024, 128, 512)
        RMS_EPS = 1e-06

        def _rmsnorm(h, w, eps=RMS_EPS):
            var = jnp.mean(jnp.square(h), axis=-1, keepdims=True)
            return h * jax.lax.rsqrt(var + eps) * w
        neighbor_sum = jnp.einsum('bnm,bmd->bnd', adjacency, x)
        agg = epsilon * x + neighbor_sum
        h = jnp.einsum('bnd,dh->bnh', agg, W1) + b1
        h = jax.nn.silu(_rmsnorm(h, rms_weight))
        out = jnp.einsum('bnh,hd->bnd', h, W2) + b2
        return out

    def _L2_gnn_ref(x, adj, eps, W1, b1, W2, b2):
        import jax, jax.numpy as jnp
        import numpy as np
        D_IN = 128
        D_HID = 256
        aggregated = jnp.einsum('bnm,bmd->bnd', adj, x)
        h = (1.0 + eps) * x + aggregated
        h = jax.nn.relu(h @ W1 + b1)
        return h @ W2 + b2

    def _L3_gnn_ref(x, adj, W_t, b_t, W_h, theta):
        import jax, jax.numpy as jnp
        import numpy as np
        B, N, D = (4, 2048, 128)
        DENSITY = 0.02
        in_degrees = jnp.sum(adj, axis=-1)
        norm = jnp.power(in_degrees + 1e-06, -0.5)[..., None]
        f_hom = jnp.einsum('bnd,de->bne', x, theta) * norm
        f_hom = jnp.einsum('bnm,bmd->bnd', adj, f_hom) * norm
        f_het = jnp.einsum('bnd,de->bne', x, W_h)
        gate = jax.nn.sigmoid(jnp.einsum('bnd,de->bne', x, W_t) + b_t)
        out = gate * f_hom + (1.0 - gate) * f_het
        return jax.nn.elu(out)
    x = _layernorm(x + _L0_gnn_ref(x, adj, L0_gnn_fc_w, L0_gnn_fc_b, L0_gnn_q_w, L0_gnn_q_b, L0_gnn_k_w, L0_gnn_k_b, L0_gnn_fp_w, L0_gnn_fp_b), axis=-1)
    x = _layernorm(x + _L1_gnn_ref(x, adj, L1_gnn_epsilon, L1_gnn_W1, L1_gnn_b1, L1_gnn_rms_weight, L1_gnn_W2, L1_gnn_b2), axis=-1)
    x = _layernorm(x + _L2_gnn_ref(x, adj, L2_gnn_eps, L2_gnn_W1, L2_gnn_b1, L2_gnn_W2, L2_gnn_b2), axis=-1)
    x = _layernorm(x + _L3_gnn_ref(x, adj, L3_gnn_W_t, L3_gnn_b_t, L3_gnn_W_h, L3_gnn_theta), axis=-1)
    return x

_drawn_inputs = setup_inputs


def setup_inputs(seed=0):
    import zlib

    import numpy as np

    out = dict(_drawn_inputs(seed))
    spreads = {'L0_gnn_fc_b': (0.0, 0.282),
     'L0_gnn_fp_b': (0.0, 0.294),
     'L1_gnn_b1': (0.0, 0.1),
     'L1_gnn_rms_weight': (1.0, 0.2),
     'L1_gnn_b2': (0.0, 0.1)}
    factors = {'L0_gnn_q_w': 3.031, 'L2_gnn_b1': 3.231, 'L3_gnn_b_t': 8.0}
    for name, (base, spread) in spreads.items():
        noise = np.random.default_rng([zlib.crc32(name.encode()), seed]).standard_normal(out[name].shape)
        drawn = base * np.exp(spread * noise) if base else spread * noise
        out[name] = jnp.asarray(drawn.astype(out[name].dtype))
    for name, factor in factors.items():
        out[name] = (out[name] * factor).astype(out[name].dtype)
    return out
```

```python
from contextlib import ExitStack

import concourse.bass as bass
from concourse import mybir

F32 = mybir.dt.float32
ALU = mybir.AluOpType
ACT = mybir.ActivationFunctionType
AX_X = mybir.AxisListType.X

P = 128
QUAD = 4
NEG = 1.0e9
SLOPE = 0.01
LN_EPS = 1e-5
RMS_EPS = 1e-6
DEG_EPS = 1e-6


def unit(it, per, offset, count):
    n = it * per + offset
    if isinstance(n, int) and not 0 <= n < count:
        return None
    return n


def wait(eng, sem, count):
    if isinstance(count, int) and count <= 0:
        return
    eng.wait_ge(sem, count)


def cap(count, most):
    return min(count, most) if isinstance(count, int) else count


def spread_loop(eng, slot, per, first, loop_from, loop_to, last):
    for it in range(first, loop_from):
        for c in range(per):
            slot(it, c)
    with eng.Fori(loop_from, loop_to) as it:
        for c in range(per):
            slot(it, c)
    for it in range(loop_to, last):
        for c in range(per):
            slot(it, c)


class Core:

    def __init__(self, nc, ctx):
        self.nc, self.ctx, self.count = nc, ctx, 0

    def sb(self, name, shape, ctx=None, dtype=F32):
        return (ctx or self.ctx).enter_context(self.nc.sbuf_tensor(name, shape, dtype))

    def psum(self, name, shape, ctx):
        return ctx.enter_context(self.nc.psum_tensor(name, shape, F32))

    def sem(self, name):
        return self.ctx.enter_context(self.nc.semaphore(name))


def start_loads(k, loads, loaded, sp, queue):
    for dst, src in loads[queue::2]:
        sp.dma_start(dst, src).then_inc(loaded, 16)


def prepare_attention(k, w):
    nc, H = k.nc, k.heads
    with ExitStack() as ctx:
        fc = k.sb("fc", [P, H, P], ctx)
        fp = k.sb("fp", [P, H, P], ctx)
        fc_t = k.sb("fc_t", [P, H, P], ctx)
        fcb = k.sb("fcb", [P, H], ctx)
        qkw = k.sb("qkw", [P, 2], ctx)
        qkb = k.sb("qkb", [P, 2], ctx)
        fpb = k.sb("fpb", [P, 1], ctx)
        turn_ps = k.psum("fc_turn_ps", [P, H, P], ctx)
        fold_ps = k.psum("fold_ps", [P, H, P], ctx)
        qk_ps = k.psum("qk_ps", [P, 512], ctx)
        bias_ps = k.psum("bias_ps", [P, 512], ctx)
        loaded, turned, copied = k.sem("weights0_loaded"), k.sem("fc_turned"), k.sem("fc_copied")
        multiplied = k.sem("fc_multiplied")
        loads = [
            (fc[:, :, :], w["L0_gnn_fc_w"].rearrange("d (h e) -> d h e", h=H)),
            (k.eye[:, :], w["eye"]),
            (fp[:, :, :], w["L0_gnn_fp_w"].rearrange("(h d) e -> d h e", h=H)),
            (fcb[:, :], w["L0_gnn_fc_b"]),
            (qkw[:, 0:1], w["L0_gnn_q_w"]),
            (qkw[:, 1:2], w["L0_gnn_k_w"]),
            (qkb[:, 0:1], w["L0_gnn_q_b"].partition_broadcast(P)),
            (qkb[:, 1:2], w["L0_gnn_k_b"].partition_broadcast(P)),
            (fpb[:, :], w["L0_gnn_fp_b"]),
        ]
        with nc.Block() as block:
            @block.sync
            def _(sp):
                start_loads(k, loads, loaded, sp, 0)

            @block.scalar
            def _(act):
                start_loads(k, loads, loaded, act, 1)

            @block.gpsimd
            def _(pool):
                pool.memset(k.minus_half[:, :], -0.5)
                pool.memset(k.bn[:, :, :], 0.0).then_inc(k.always, 1)

            @block.tensor
            def _(pe):
                pe.wait_ge(loaded, 16 * len(loads))
                for h in range(H):
                    mm = pe.transpose(turn_ps[:, h, :], fc[:, h, :], k.eye[:, :])
                mm.then_inc(turned, 1)
                pe.wait_ge(copied, 1)
                for h in range(H):
                    pe.matmul(fold_ps[:, h, :], fc_t[:, h, :], fp[:, h, :], start=True, stop=True)
                for h in range(H):
                    pe.matmul(qk_ps[:, 2 * h:2 * h + 2], fc_t[:, h, :], qkw[:, :], start=True, stop=True)
                for h in range(H):
                    pe.matmul(qk_ps[:, 2 * H + 2 * h:2 * H + 2 * h + 2], fcb[:, h:h + 1].to_broadcast([P, P]),
                              qkw[:, :], start=True, stop=True)
                for h in range(H):
                    mm = pe.matmul(bias_ps[:, 0:1], fp[:, h, :], fcb[:, h:h + 1], start=(h == 0), stop=(h == H - 1))
                mm.then_inc(multiplied, 1)

            @block.vector
            def _(dve):
                dve.wait_ge(turned, 1)
                dve.tensor_copy(fc_t[:, :, :], turn_ps[:, :, :]).then_inc(copied, 1)
                dve.wait_ge(multiplied, 1)
                dve.tensor_copy(k.fold[:, :, :], fold_ps[:, :, :])
                dve.tensor_copy(k.wqk[:, :, :], qk_ps[:, 0:2 * H].rearrange("d (h t) -> d t h", t=2))
                dve.tensor_tensor(k.qk_bias[:, :, :], qk_ps[:, 2 * H:4 * H].rearrange("d (h t) -> d t h", t=2),
                                  qkb[:, :].unsqueeze(2).to_broadcast([P, 2, H]), ALU.add)
                dve.tensor_tensor(k.out_bias[:, :], bias_ps[:, 0:1], fpb[:, :], ALU.add)


def prepare_mlps(k, w):
    nc, HC = k.nc, k.hid1
    with ExitStack() as ctx:
        w1_t = k.sb("w1_t", [P, HC, P], ctx)
        eps1 = k.sb("eps1", [P, 1], ctx)
        eps2 = k.sb("eps2", [P, 1], ctx)
        eps2p = k.sb("eps2p", [P, 1], ctx)
        turn_ps = k.psum("w1_turn_ps", [P, HC, P], ctx)
        gram_ps = k.psum("w1_gram_ps", [P, 512], ctx)
        loaded, turned, copied = k.sem("weights1_loaded"), k.sem("w1_turned"), k.sem("w1_copied")
        multiplied, one_added = k.sem("w1_multiplied"), k.sem("one_added")
        loads = [
            (k.w1[:, :, :], w["L1_gnn_W1"].rearrange("d (c h) -> d c h", c=HC)),
            (k.b1[:, :], w["L1_gnn_b1"]),
            (k.w2[:, :, :], w["L1_gnn_W2"].rearrange("(c h) d -> h c d", c=HC)),
            (k.rmsw[:, :], w["L1_gnn_rms_weight"]),
            (k.b2[:, :], w["L1_gnn_b2"]),
            (eps1[:, :], w["L1_gnn_epsilon"].partition_broadcast(P)),
            (k.v1[:, :, :], w["L2_gnn_W1"].rearrange("d (c h) -> d c h", c=k.hid2)),
            (k.c1[:, :], w["L2_gnn_b1"]),
            (k.v2[:, :, :], w["L2_gnn_W2"].rearrange("(c h) d -> h c d", c=k.hid2)),
            (k.c2[:, :], w["L2_gnn_b2"]),
            (eps2[:, :], w["L2_gnn_eps"].partition_broadcast(P)),
            (k.w_t[:, :], w["L3_gnn_W_t"]),
            (k.b_t[:, :], w["L3_gnn_b_t"]),
            (k.w_h[:, :], w["L3_gnn_W_h"]),
            (k.theta[:, :], w["L3_gnn_theta"]),
        ]
        with nc.Block() as block:
            @block.sync
            def _(sp):
                start_loads(k, loads, loaded, sp, 0)

            @block.scalar
            def _(act):
                start_loads(k, loads, loaded, act, 1)

            @block.gpsimd
            def _(pool):
                pool.memset(k.ones[:, :], 1.0 / (HC * P))

            @block.tensor
            def _(pe):
                pe.wait_ge(loaded, 16 * len(loads))
                for c in range(HC):
                    mm = pe.transpose(turn_ps[:, c, :], k.w1[:, c, :], k.eye[:, :])
                mm.then_inc(turned, 1)
                pe.wait_ge(copied, 1)
                for c in range(HC):
                    pe.matmul(gram_ps[:, 0:P], w1_t[:, c, :], w1_t[:, c, :], start=(c == 0), stop=(c == HC - 1))
                for c in range(HC):
                    pe.matmul(gram_ps[:, P:P + 1], w1_t[:, c, :], k.b1[:, c:c + 1], start=(c == 0),
                              stop=(c == HC - 1))
                for c in range(HC):
                    mm = pe.matmul(gram_ps[:, P + 1:P + 2], k.b1[:, c:c + 1].to_broadcast([P, P]),
                                   k.b1[:, c:c + 1], start=(c == 0), stop=(c == HC - 1))
                mm.then_inc(multiplied, 1)

            @block.vector
            def _(dve):
                dve.wait_ge(turned, 1)
                dve.tensor_copy(w1_t[:, :, :], turn_ps[:, :, :]).then_inc(copied, 1)
                dve.wait_ge(loaded, 16 * len(loads))
                dve.tensor_scalar(eps2p[:, :], eps2[:, :], 1.0, None, ALU.add).then_inc(one_added, 1)
                dve.tensor_scalar(k.diag1[:, :], k.eye[:, :], eps1[:, 0:1], None, ALU.mult)
                dve.wait_ge(one_added, 1)
                dve.tensor_scalar(k.diag2[:, :], k.eye[:, :], eps2p[:, 0:1], None, ALU.mult)
                dve.wait_ge(multiplied, 1)
                dve.tensor_copy(k.gram[:, :], gram_ps[:, 0:P])
                dve.tensor_scalar(k.gram_bias[:, :], gram_ps[:, P:P + 1], 2.0, None, ALU.mult)
                dve.tensor_scalar(k.square_bias[:, :], gram_ps[:, P + 1:P + 2], 1.0 / (HC * P), RMS_EPS,
                                  ALU.mult, ALU.add)


def norm_sems(k, layer):
    return {n: k.sem(f"{n}_{layer}") for n in ("summed", "stats", "moments", "var", "rstd", "x_next")}


def norm_statistics(dve, k, s, y, g):
    dve.wait_ge(s["summed"], g + 1)
    for q in range(QUAD):
        last = dve.bn_stats(k.bn[:, q, :], y[:, q, :])
    last.then_inc(s["stats"], 1)
    dve.wait_ge(k.always, 1)
    dve.wait_ge(s["stats"], g + 1)
    for q in range(QUAD):
        last = dve.bn_aggr(k.mv[:, q, :], k.bn[:, q, :])
    last.then_inc(s["moments"], 1)
    dve.wait_ge(s["moments"], g + 1)
    wait(dve, s["rstd"], g)
    dve.tensor_scalar(k.var[:, :], k.mv[:, :, 1], LN_EPS, None, ALU.add).then_inc(s["var"], 1)


def norm_root(pool, k, s, g):
    pool.wait_ge(s["var"], g + 1)
    wait(pool, s["x_next"], g)
    pool.tensor_tensor(k.rstd[:, :], k.var[:, :], k.minus_half[:, :], ALU.pow).then_inc(s["rstd"], 1)


def norm_apply(dve, k, s, y, g):
    dve.wait_ge(s["rstd"], g + 1)
    for q in range(QUAD):
        last = dve.tensor_scalar(k.x[:, bass.ds(g * QUAD + q, 1), :].rearrange("p a d -> p (a d)"), y[:, q, :],
                                 k.mv[:, q, 0:1], k.rstd[:, q:q + 1], ALU.subtract, ALU.mult)
    last.then_inc(s["x_next"], 1)


def group_of(t, g):
    return t[:, bass.ds(g * QUAD, QUAD), :]


def attention(k, x_dram, adj_dram):
    nc, H = k.nc, k.heads
    GROUPS, GRAPHS = k.groups, k.graphs
    x_view = x_dram.rearrange("b n d -> n b d")
    adj_view = adj_dram.rearrange("b n m -> n b m")
    with ExitStack() as ctx:
        xin = k.sb("xin", [P, QUAD, P], ctx)
        ain = k.sb("ain", [P, 2, QUAD, P], ctx)
        val = k.sb("val", [P, 2, QUAD, P], ctx)
        x_t = k.sb("x_t", [P, QUAD, P], ctx)
        qk = k.sb("qk", [P, 2, QUAD, 2, H], ctx)
        score = k.sb("score", [P, 4, H, P], ctx)
        probs_t = k.sb("probs_t", [P, 2, H, P], ctx)
        mixed = k.sb("mixed", [P, 2, H, QUAD, P], ctx)
        neg_max = k.sb("neg_max", [P, 2, H], ctx)
        total = k.sb("total", [P, 2, H], ctx)
        recip = k.sb("recip", [P, 2, H], ctx)
        out_t = k.sb("out_t", [P, QUAD, P], ctx)
        y = k.sb("y0", [P, QUAD, P], ctx)
        key_ps = k.psum("key_ps", [P, H, P], ctx)
        turn_ps = k.psum("turn_ps", [P, H, P], ctx)
        mix_ps = k.psum("mix_ps", [P, H, P], ctx)
        out_ps = k.psum("out_ps", [P, QUAD, P], ctx)
        misc_ps = k.psum("misc_ps", [P, 512], ctx)
        quad_ps = misc_ps[:, :].rearrange("p (q n) -> p q n", q=QUAD)

        x_loaded = k.sem("x_loaded")
        adj_loaded = [k.sem(f"adj_loaded{i}") for i in range(2)]
        val_loaded = [k.sem(f"val_loaded{i}") for i in range(2)]
        all_x_loaded = k.sem("all_x_loaded")
        adj_turned, adj_copied = k.sem("adj_turned"), k.sem("adj_copied")
        x_turned, x_copied = k.sem("x_turned"), k.sem("x_copied")
        qk_made, qk_copied, mask_made = k.sem("qk_made"), k.sem("qk_copied"), k.sem("mask_made")
        degree_summed = k.sem("degree_summed")
        keys_spread, query_added = k.sem("keys_spread"), k.sem("query_added")
        scores_made, scores_leaky = k.sem("scores_made"), k.sem("scores_leaky")
        max_found, exp_made, recip_made = k.sem("max_found"), k.sem("exp_made"), k.sem("recip_made")
        probs_made, probs_turned, probs_copied = k.sem("probs_made"), k.sem("probs_turned"), k.sem("probs_copied")
        mix_made, mix_copied = k.sem("mix_made"), k.sem("mix_copied")
        out_made, out_copied, out_turned = k.sem("out_made"), k.sem("out_copied"), k.sem("out_turned")
        feats_added, tanh_made, sigmoid_made = k.sem("feats_added"), k.sem("tanh_made"), k.sem("sigmoid_made")
        norm = norm_sems(k, 0)
        PER = 2 * QUAD
        SPAN = dict(per=PER, first=-1, loop_from=2, loop_to=GRAPHS // PER - 1, last=GRAPHS // PER + 2)

        with nc.Block() as block:
            @block.sync
            def _(sp):
                def load(it, j):
                    g = unit(it, 2, j, GROUPS)
                    wait(sp, query_added, QUAD * (g - 1))
                    sp.dma_start(ain[:, j], group_of(adj_view, g)).then_inc(adj_loaded[j], 16)
                    wait(sp, x_turned, g)
                    sp.dma_start(xin[:, :, :], group_of(x_view, g)).then_inc(x_loaded, 16)
                    wait(sp, mix_made, QUAD * (g - 1))
                    sp.dma_start(val[:, j], group_of(x_view, g)).then_inc(val_loaded[j], 16)

                for j in range(2):
                    load(0, j)
                for part in range(4):
                    n = GRAPHS // 4
                    sp.dma_start(k.x[:, part * n:(part + 1) * n, :],
                                 x_view[:, part * n:(part + 1) * n, :]).then_inc(all_x_loaded, 16)
                for j in range(2):
                    load(1, j)
                with sp.Fori(2, GROUPS // 2) as it:
                    for j in range(2):
                        load(it, j)

            @block.tensor
            def _(pe):
                def slot(it, c):
                    b = unit(it, PER, c - 2, GRAPHS)
                    if b is not None:
                        pe.wait_ge(probs_made, b + 1)
                        wait(pe, probs_copied, b)
                        for h in range(H):
                            mm = pe.transpose(turn_ps[:, h, :], score[:, (c - 2) % 4, h, :], k.eye[:, :])
                        mm.then_inc(probs_turned, 1)
                    g = unit(it, 2, c // QUAD + 1, GROUPS)
                    j = (c // QUAD + 1) % 2
                    if c % QUAD == 0 and g is not None:
                        pe.wait_ge(adj_loaded[j], 16 * (it + (c // QUAD + 1) // 2 + 1))
                        wait(pe, feats_added, g - 3)
                        for q in range(QUAD):
                            mm = pe.transpose(quad_ps[:, q, :], ain[:, j, q, :], k.eye[:, :])
                        mm.then_inc(adj_turned, 1)
                    if c % QUAD == 1 and g is not None:
                        pe.wait_ge(x_loaded, 16 * (g + 1))
                        pe.wait_ge(adj_copied, g + 1)
                        for q in range(QUAD):
                            mm = pe.transpose(quad_ps[:, q, :], xin[:, q, :], k.eye[:, :])
                        mm.then_inc(x_turned, 1)
                    if c % QUAD == 2 and g is not None:
                        pe.wait_ge(x_copied, g + 1)
                        for q in range(QUAD):
                            mm = pe.matmul(misc_ps[:, 2 * H * q:2 * H * (q + 1)], x_t[:, q, :],
                                           k.wqk[:, :, :].rearrange("d t h -> d (t h)"), start=True, stop=True)
                        mm.then_inc(qk_made, 1)
                    g = unit(it, 2, (c - 11) // QUAD, GROUPS)
                    if c % QUAD == 3 and g is not None:
                        pe.wait_ge(out_copied, g + 1)
                        pe.wait_ge(qk_copied, cap(g + 4, GROUPS))
                        for q in range(QUAD):
                            mm = pe.transpose(quad_ps[:, q, :], out_t[:, q, :], k.eye[:, :])
                        mm.then_inc(out_turned, 1)
                    g = unit(it, 2, (c - 7) // QUAD, GROUPS)
                    part = (c - 7) % QUAD
                    if g is not None:
                        if part == 0:
                            pe.wait_ge(mix_copied, QUAD * (g + 1))
                            wait(pe, out_copied, g)
                        for h in range(part * H // QUAD, (part + 1) * H // QUAD):
                            mm = pe.matmul(out_ps[:, :, :], k.fold[:, h, :], mixed[:, ((c - 7) // QUAD) % 2, h, :, :],
                                           start=(h == 0), stop=(h == H - 1))
                        if part == QUAD - 1:
                            mm.then_inc(out_made, 1)
                    b = unit(it, PER, c + 1, GRAPHS)
                    if b is not None:
                        pe.wait_ge(qk_copied, unit(it, 2, (c + 1) // QUAD, GROUPS) + 1)
                        wait(pe, scores_made, b)
                        for h in range(H):
                            mm = pe.transpose(key_ps[:, h, :],
                                              qk[:, ((c + 1) // QUAD) % 2, (c + 1) % QUAD, 1, h:h + 1].to_broadcast([P, P]),
                                              k.eye[:, :])
                        mm.then_inc(keys_spread, 1)
                    b = unit(it, PER, c - 2, GRAPHS)
                    if b is not None:
                        j = ((c - 2) // QUAD) % 2
                        pe.wait_ge(val_loaded[j], 16 * (it + (c - 2) // QUAD // 2 + 1))
                        pe.wait_ge(probs_copied, b + 1)
                        wait(pe, mix_copied, b)
                        for half in range(2):
                            hs = slice(half * H // 2, (half + 1) * H // 2)
                            mm = pe.matmul(mix_ps[:, hs, :], val[:, j, (c - 2) % QUAD, :], probs_t[:, c % 2, hs, :],
                                           start=True, stop=True)
                        mm.then_inc(mix_made, 1)

                spread_loop(pe, slot, **SPAN)

            @block.scalar
            def _(act):
                def slot(it, c):
                    b = unit(it, PER, c - 2, GRAPHS)
                    if b is not None:
                        act.wait_ge(probs_turned, b + 1)
                        wait(act, mix_made, b - 1)
                        act.activation(probs_t[:, c % 2], turn_ps[:, :, :], ACT.Copy).then_inc(probs_copied, 1)
                    b = unit(it, PER, c - 3, GRAPHS)
                    if b is not None:
                        act.wait_ge(mix_made, b + 1)
                        if (c - 3) % QUAD == 0:
                            wait(act, out_made, unit(it, 2, (c - 3) // QUAD, GROUPS) - 1)
                        act.activation(mixed[:, ((c - 3) // QUAD) % 2, :, (c - 3) % QUAD, :], mix_ps[:, :, :],
                                       ACT.Copy).then_inc(mix_copied, 1)
                    g = unit(it, 2, c // QUAD + 1, GROUPS)
                    if c % QUAD == 0 and g is not None:
                        act.wait_ge(adj_turned, g + 1)
                        act.activation(group_of(k.adj_t, g), quad_ps, ACT.Copy).then_inc(adj_copied, 1)
                    if c % QUAD == 1 and g is not None:
                        act.wait_ge(x_turned, g + 1)
                        wait(act, qk_made, g)
                        act.activation(x_t[:, :, :], quad_ps, ACT.Copy).then_inc(x_copied, 1)
                    g = unit(it, 2, (c - 12) // QUAD, GROUPS)
                    if c % QUAD == 0 and g is not None:
                        act.wait_ge(feats_added, g + 1)
                        act.activation(y[:, :, :], y[:, :, :], ACT.Tanh, scale=0.5).then_inc(tanh_made, 1)
                    g = unit(it, 2, (c - 10) // QUAD, GROUPS)
                    if c % QUAD == 2 and g is not None:
                        act.wait_ge(out_made, g + 1)
                        wait(act, out_turned, g)
                        act.activation(out_t[:, :, :], out_ps[:, :, :], ACT.Identity,
                                       bias=k.out_bias[:, 0:1]).then_inc(out_copied, 1)
                    b = unit(it, PER, c, GRAPHS)
                    if b is not None:
                        act.wait_ge(max_found, b + 1)
                        wait(act, recip_made, b - 1)
                        for h in range(H):
                            e = act.activation(score[:, c % 4, h, :], score[:, c % 4, h, :], ACT.Exp,
                                               bias=neg_max[:, c % 2, h:h + 1], accum_out=total[:, c % 2, h:h + 1])
                        e.then_inc(exp_made, 1)

                spread_loop(act, slot, **SPAN)

            @block.vector
            def _(dve):
                def slot(it, c):
                    b = unit(it, PER, c, GRAPHS)
                    if b is not None:
                        dve.wait_ge(keys_spread, b + 1)
                        dve.wait_ge(query_added, b + 1)
                        dve.tensor_tensor(score[:, c % 4], key_ps[:, :, :], score[:, c % 4], ALU.add)\
                           .then_inc(scores_made, 1)
                        dve.wait_ge(scores_made, b + 1)
                        dve.scalar_tensor_tensor(out=score[:, c % 4], in0=score[:, c % 4], scalar=SLOPE,
                                                 in1=score[:, c % 4], op0=ALU.mult, op1=ALU.max)\
                           .then_inc(scores_leaky, 1)
                    before = unit(it, PER, c - 1, GRAPHS)
                    if before is not None:
                        dve.wait_ge(exp_made, before + 1)
                        wait(dve, probs_made, before - 1)
                        dve.reciprocal(recip[:, (c - 1) % 2, :], total[:, (c - 1) % 2, :]).then_inc(recip_made, 1)
                    if b is not None:
                        dve.wait_ge(scores_leaky, b + 1)
                        wait(dve, exp_made, b - 1)
                        dve.tensor_reduce(neg_max[:, c % 2, :], score[:, c % 4], AX_X, ALU.max, negate=True)\
                           .then_inc(max_found, 1)
                    g = unit(it, 2, c // QUAD + 1, GROUPS)
                    j = (c // QUAD + 1) % 2
                    if c % QUAD == 0 and g is not None:
                        dve.wait_ge(adj_loaded[j], 16 * (it + (c // QUAD + 1) // 2 + 1))
                        dve.tensor_reduce(k.degree[:, bass.ds(g * QUAD, QUAD)], ain[:, j], AX_X, ALU.add)\
                           .then_inc(degree_summed, 1)
                        dve.wait_ge(degree_summed, g + 1)
                        dve.wait_ge(adj_turned, g + 1)
                        dve.tensor_scalar(ain[:, j], ain[:, j], 1.0, NEG, ALU.subtract, ALU.mult)\
                           .then_inc(mask_made, 1)
                    if c % QUAD == 2 and g is not None:
                        dve.wait_ge(qk_made, g + 1)
                        dve.tensor_tensor(qk[:, j].rearrange("p q t h -> p q (t h)"),
                                          misc_ps[:, 0:2 * H * QUAD].rearrange("p (q m) -> p q m", q=QUAD),
                                          k.qk_bias[:, :, :].rearrange("p t h -> p (t h)").unsqueeze(1)
                                          .to_broadcast([P, QUAD, 2 * H]), ALU.add).then_inc(qk_copied, 1)
                    g = unit(it, 2, (c - 11) // QUAD, GROUPS)
                    if c % QUAD == 3 and g is not None:
                        dve.wait_ge(out_turned, g + 1)
                        dve.wait_ge(all_x_loaded, 64)
                        wait(dve, norm["x_next"], g)
                        dve.tensor_tensor(y[:, :, :], quad_ps, group_of(k.x, g), ALU.add).then_inc(feats_added, 1)
                    g = unit(it, 2, (c - 13) // QUAD, GROUPS)
                    if c % QUAD == 1 and g is not None:
                        dve.wait_ge(tanh_made, g + 1)
                        dve.tensor_scalar(y[:, :, :], y[:, :, :], 0.5, 0.5, ALU.mult, ALU.add)\
                           .then_inc(sigmoid_made, 1)
                        dve.wait_ge(sigmoid_made, g + 1)
                        dve.tensor_tensor(y[:, :, :], y[:, :, :], group_of(k.x, g), ALU.add)\
                           .then_inc(norm["summed"], 1)
                        norm_statistics(dve, k, norm, y, g)
                    g = unit(it, 2, (c - 14) // QUAD, GROUPS)
                    if c % QUAD == 2 and g is not None:
                        norm_apply(dve, k, norm, y, g)

                spread_loop(dve, slot, **SPAN)
                dve.tensor_scalar(k.degree[:, :], k.degree[:, :], DEG_EPS, None, ALU.add)

            @block.gpsimd
            def _(pool):
                def slot(it, c):
                    b = unit(it, PER, c + 1, GRAPHS)
                    if b is not None:
                        g = unit(it, 2, (c + 1) // QUAD, GROUPS)
                        j = ((c + 1) // QUAD) % 2
                        pool.wait_ge(mask_made, g + 1)
                        pool.wait_ge(qk_copied, g + 1)
                        wait(pool, probs_turned, b - 3)
                        pool.tensor_tensor(score[:, (c + 1) % 4],
                                           ain[:, j, (c + 1) % QUAD, :].unsqueeze(1).to_broadcast([P, H, P]),
                                           qk[:, j, (c + 1) % QUAD, 0, :].unsqueeze(2).to_broadcast([P, H, P]),
                                           ALU.add).then_inc(query_added, 1)
                    g = unit(it, 2, (c - 14) // QUAD, GROUPS)
                    if c % QUAD == 2 and g is not None:
                        norm_root(pool, k, norm, g)
                    b = unit(it, PER, c - 1, GRAPHS)
                    if b is not None:
                        pool.wait_ge(recip_made, b + 1)
                        pool.tensor_tensor(score[:, (c - 1) % 4], score[:, (c - 1) % 4],
                                           recip[:, (c - 1) % 2, :].unsqueeze(2).to_broadcast([P, H, P]),
                                           ALU.mult).then_inc(probs_made, 1)

                spread_loop(pool, slot, **SPAN)


def rms_mlp(k):
    nc, HC, GROUPS = k.nc, k.hid1, k.groups
    with ExitStack() as ctx:
        xs = k.sb("xs1", [P, 2, QUAD, P], ctx)
        adj = k.sb("adj1", [P, 2, QUAD, P], ctx)
        agg = k.sb("agg1", [P, 2, QUAD * P], ctx)
        prod = k.sb("prod", [P, QUAD * P], ctx)
        root_in = k.sb("root_in", [P, QUAD], ctx)
        root = k.sb("root", [P, QUAD], ctx)
        scale = k.sb("scale", [P, QUAD * P], ctx)
        hid = k.sb("hid1", [P, 2, HC, QUAD * P], ctx)
        out_t = k.sb("out_t1", [P, QUAD * P], ctx)
        y = k.sb("y1", [P, QUAD, P], ctx)
        agg_ps = k.psum("agg_ps", [P, QUAD * P], ctx)
        gram_ps = k.psum("gram_ps", [P, QUAD * P], ctx)
        root_ps = k.psum("root_ps", [P, QUAD * P], ctx)
        hid_ps = k.psum("hid_ps", [P, 2, QUAD * P], ctx)
        out_ps = k.psum("out_ps1", [P, QUAD * P], ctx)
        back_ps = k.psum("back_ps", [P, QUAD, P], ctx)
        x_copied, diag_added = k.sem("x_copied1"), k.sem("diag_added1")
        agg_made, agg_copied = k.sem("agg_made1"), k.sem("agg_copied1")
        gram_made, prod_made = k.sem("gram_made"), k.sem("prod_made")
        squares_summed, root_asked, root_made = k.sem("squares_summed"), k.sem("root_asked"), k.sem("root_made")
        root_spread, root_copied = k.sem("root_spread"), k.sem("root_copied")
        hid_made, hid_scaled, hid_silu = k.sem("hid_made1"), k.sem("hid_scaled"), k.sem("hid_silu")
        out_made, out_copied, out_turned = k.sem("out_made1"), k.sem("out_copied1"), k.sem("out_turned1")
        norm = norm_sems(k, 1)
        SPAN = dict(per=2, first=-1, loop_from=3, loop_to=GROUPS // 2 - 1, last=GROUPS // 2 + 3)

        with nc.Block() as block:
            @block.tensor
            def _(pe):
                def hidden(it, c, chunk):
                    g = unit(it, 2, c - 1, GROUPS)
                    if g is None:
                        return
                    pe.wait_ge(agg_copied, g + 1)
                    wait(pe, hid_scaled, HC * g + chunk - 1)
                    pe.matmul(hid_ps[:, chunk % 2, :], k.w1[:, chunk, :], agg[:, (c - 1) % 2, :],
                              start=True, stop=True).then_inc(hid_made, 1)

                def output(it, c, chunk):
                    g = unit(it, 2, c - 2, GROUPS)
                    if g is None:
                        return
                    pe.wait_ge(hid_silu, HC * g + chunk + 1)
                    if chunk == 0:
                        wait(pe, out_copied, g)
                    mm = pe.matmul(out_ps[:, :], k.w2[:, chunk, :], hid[:, c % 2, chunk, :],
                                   start=(chunk == 0), stop=(chunk == HC - 1))
                    if chunk == HC - 1:
                        mm.then_inc(out_made, 1)

                def slot(it, c):
                    hidden(it, c, 0)
                    g = unit(it, 2, c, GROUPS)
                    if g is not None:
                        pe.wait_ge(x_copied, g + 1)
                        pe.wait_ge(diag_added, g + 1)
                        wait(pe, agg_copied, g)
                        for q in range(QUAD):
                            mm = pe.matmul(agg_ps[:, q * P:(q + 1) * P], xs[:, c % 2, q, :], adj[:, c % 2, q, :],
                                           start=True, stop=True)
                        mm.then_inc(agg_made, 1)
                    hidden(it, c, 1)
                    output(it, c, 0)
                    if g is not None:
                        pe.wait_ge(agg_copied, g + 1)
                        wait(pe, prod_made, g)
                        pe.matmul(gram_ps[:, :], k.gram[:, :], agg[:, c % 2, :], start=True, stop=True)\
                          .then_inc(gram_made, 1)
                    hidden(it, c, 2)
                    output(it, c, 1)
                    if g is not None:
                        pe.wait_ge(prod_made, g + 1)
                        wait(pe, root_copied, g)
                        for q in range(QUAD):
                            mm = pe.matmul(root_ps[:, q:q + 1], prod[:, q * P:(q + 1) * P], k.ones[:, :],
                                           start=True, stop=True)
                        mm.then_inc(squares_summed, 1)
                    hidden(it, c, 3)
                    output(it, c, 2)
                    if g is not None:
                        pe.wait_ge(root_made, g + 1)
                        for q in range(QUAD):
                            mm = pe.transpose(root_ps[:, q * P:(q + 1) * P], root[:, q:q + 1].to_broadcast([P, P]),
                                              k.eye[:, :])
                        mm.then_inc(root_spread, 1)
                    back = unit(it, 2, c - 3, GROUPS)
                    if back is not None:
                        pe.wait_ge(out_copied, back + 1)
                        wait(pe, norm["summed"], back)
                        for q in range(QUAD):
                            mm = pe.transpose(back_ps[:, q, :], out_t[:, q * P:(q + 1) * P], k.eye[:, :])
                        mm.then_inc(out_turned, 1)
                    output(it, c, 3)

                spread_loop(pe, slot, **SPAN)

            @block.scalar
            def _(act):
                def silu(it, c, chunk):
                    g = unit(it, 2, c - 1, GROUPS)
                    if g is None:
                        return
                    act.wait_ge(hid_scaled, HC * g + chunk + 1)
                    h = hid[:, (c - 1) % 2, chunk, :]
                    act.activation(h, h, ACT.Silu, scale=k.rmsw[:, chunk:chunk + 1]).then_inc(hid_silu, 1)

                def slot(it, c):
                    g = unit(it, 2, c - 3, GROUPS)
                    if g is not None:
                        act.wait_ge(out_made, g + 1)
                        wait(act, out_turned, g)
                        act.activation(out_t[:, :], out_ps[:, :], ACT.Identity, bias=k.b2[:, 0:1])\
                           .then_inc(out_copied, 1)
                    silu(it, c, 0)
                    g = unit(it, 2, c, GROUPS)
                    if g is not None:
                        act.wait_ge(agg_made, g + 1)
                        wait(act, hid_made, HC * (g - 1))
                        wait(act, prod_made, g - 1)
                        act.activation(agg[:, c % 2, :], agg_ps[:, :], ACT.Copy).then_inc(agg_copied, 1)
                    for chunk in range(1, HC):
                        silu(it, c, chunk)
                    if g is not None:
                        act.wait_ge(root_spread, g + 1)
                        wait(act, hid_scaled, HC * g)
                        act.activation(scale[:, :], root_ps[:, :], ACT.Copy).then_inc(root_copied, 1)

                spread_loop(act, slot, **SPAN)

            @block.vector
            def _(dve):
                def scaled(it, c, chunk):
                    g = unit(it, 2, c - 1, GROUPS)
                    if g is None:
                        return
                    dve.wait_ge(hid_made, HC * g + chunk + 1)
                    if chunk == 0:
                        dve.wait_ge(root_copied, g + 1)
                        wait(dve, out_made, g - 1)
                    dve.scalar_tensor_tensor(out=hid[:, (c - 1) % 2, chunk, :], in0=hid_ps[:, chunk % 2, :],
                                             scalar=k.b1[:, chunk:chunk + 1], in1=scale[:, :],
                                             op0=ALU.add, op1=ALU.mult).then_inc(hid_scaled, 1)

                def slot(it, c):
                    g = unit(it, 2, c - 4, GROUPS)
                    if g is not None:
                        norm_apply(dve, k, norm, y, g)
                    scaled(it, c, 0)
                    scaled(it, c, 1)
                    g = unit(it, 2, c, GROUPS)
                    if g is not None:
                        dve.wait_ge(gram_made, g + 1)
                        wait(dve, squares_summed, g)
                        dve.scalar_tensor_tensor(out=prod[:, :], in0=gram_ps[:, :], scalar=k.gram_bias[:, 0:1],
                                                 in1=agg[:, c % 2, :], op0=ALU.add, op1=ALU.mult)\
                           .then_inc(prod_made, 1)
                    n = unit(it, 2, c + 1, GROUPS)
                    if n is not None:
                        wait(dve, agg_made, n - 1)
                        dve.tensor_copy(xs[:, (c + 1) % 2], group_of(k.x, n)).then_inc(x_copied, 1)
                    scaled(it, c, 2)
                    if g is not None:
                        dve.wait_ge(squares_summed, g + 1)
                        wait(dve, root_made, g)
                        dve.tensor_scalar(root_in[:, :], root_ps[:, 0:QUAD], k.square_bias[:, 0:1], RMS_EPS,
                                          ALU.add, ALU.max).then_inc(root_asked, 1)
                    scaled(it, c, 3)
                    g = unit(it, 2, c - 3, GROUPS)
                    if g is not None:
                        dve.wait_ge(out_turned, g + 1)
                        wait(dve, norm["x_next"], g)
                        dve.tensor_tensor(y[:, :, :], back_ps[:, :, :], group_of(k.x, g), ALU.add)\
                           .then_inc(norm["summed"], 1)
                        norm_statistics(dve, k, norm, y, g)

                spread_loop(dve, slot, **SPAN)

            @block.gpsimd
            def _(pool):
                def slot(it, c):
                    n = unit(it, 2, c + 1, GROUPS)
                    if n is not None:
                        wait(pool, agg_made, n - 1)
                        pool.tensor_tensor(adj[:, (c + 1) % 2], group_of(k.adj_t, n),
                                           k.diag1[:, :].unsqueeze(1).to_broadcast([P, QUAD, P]), ALU.add)\
                            .then_inc(diag_added, 1)
                    g = unit(it, 2, c, GROUPS)
                    if g is not None:
                        pool.wait_ge(root_asked, g + 1)
                        wait(pool, root_spread, g)
                        pool.tensor_tensor(root[:, :], root_in[:, :], k.minus_half[:, :], ALU.pow)\
                            .then_inc(root_made, 1)
                    g = unit(it, 2, c - 3, GROUPS)
                    if g is not None:
                        norm_root(pool, k, norm, g)

                spread_loop(pool, slot, **SPAN)


def relu_mlp(k):
    nc, HC, GROUPS = k.nc, k.hid2, k.groups
    with ExitStack() as ctx:
        xs = k.sb("xs2", [P, 2, QUAD, P], ctx)
        adj = k.sb("adj2", [P, 2, QUAD, P], ctx)
        agg = k.sb("agg2", [P, 2, QUAD * P], ctx)
        hid = k.sb("hid2", [P, 2, HC, QUAD * P], ctx)
        out_t = k.sb("out_t2", [P, 2, QUAD * P], ctx)
        y = k.sb("y2", [P, QUAD, P], ctx)
        agg_ps = k.psum("agg_ps2", [P, QUAD * P], ctx)
        hid_ps = k.psum("hid_ps2", [P, HC, QUAD * P], ctx)
        out_ps = k.psum("out_ps2", [P, QUAD * P], ctx)
        back_ps = k.psum("back_ps2", [P, QUAD, P], ctx)
        x_copied, diag_added = k.sem("x_copied2"), k.sem("diag_added2")
        agg_made, agg_copied = k.sem("agg_made2"), k.sem("agg_copied2")
        hid_made, hid_relu = k.sem("hid_made2"), k.sem("hid_relu2")
        out_made, out_copied, out_turned = k.sem("out_made2"), k.sem("out_copied2"), k.sem("out_turned2")
        norm = norm_sems(k, 2)
        SPAN = dict(per=2, first=-1, loop_from=3, loop_to=GROUPS // 2 - 1, last=GROUPS // 2 + 3)

        with nc.Block() as block:
            @block.tensor
            def _(pe):
                def slot(it, c):
                    g = unit(it, 2, c, GROUPS)
                    if g is not None:
                        pe.wait_ge(x_copied, g + 1)
                        pe.wait_ge(diag_added, g + 1)
                        wait(pe, agg_copied, g)
                        for q in range(QUAD):
                            mm = pe.matmul(agg_ps[:, q * P:(q + 1) * P], xs[:, c % 2, q, :], adj[:, c % 2, q, :],
                                           start=True, stop=True)
                        mm.then_inc(agg_made, 1)
                    g = unit(it, 2, c - 1, GROUPS)
                    if g is not None:
                        pe.wait_ge(agg_copied, g + 1)
                        for chunk in range(HC):
                            wait(pe, hid_relu, HC * (g - 1) + chunk + 1)
                            pe.matmul(hid_ps[:, chunk, :], k.v1[:, chunk, :], agg[:, (c - 1) % 2, :],
                                      start=True, stop=True).then_inc(hid_made, 1)
                    g = unit(it, 2, c - 2, GROUPS)
                    if g is not None:
                        wait(pe, out_copied, g)
                        for chunk in range(HC):
                            pe.wait_ge(hid_relu, HC * g + chunk + 1)
                            mm = pe.matmul(out_ps[:, :], k.v2[:, chunk, :], hid[:, c % 2, chunk, :],
                                           start=(chunk == 0), stop=(chunk == HC - 1))
                        mm.then_inc(out_made, 1)
                    g = unit(it, 2, c - 3, GROUPS)
                    if g is not None:
                        pe.wait_ge(out_copied, g + 1)
                        wait(pe, norm["summed"], g)
                        for q in range(QUAD):
                            mm = pe.transpose(back_ps[:, q, :], out_t[:, (c - 3) % 2, q * P:(q + 1) * P], k.eye[:, :])
                        mm.then_inc(out_turned, 1)

                spread_loop(pe, slot, **SPAN)

            @block.scalar
            def _(act):
                def slot(it, c):
                    g = unit(it, 2, c - 3, GROUPS)
                    if g is not None:
                        act.wait_ge(out_made, g + 1)
                        wait(act, out_turned, g - 1)
                        act.activation(out_t[:, (c - 3) % 2, :], out_ps[:, :], ACT.Identity, bias=k.c2[:, 0:1])\
                           .then_inc(out_copied, 1)
                    g = unit(it, 2, c, GROUPS)
                    if g is not None:
                        act.wait_ge(agg_made, g + 1)
                        wait(act, hid_made, HC * (g - 1))
                        act.activation(agg[:, c % 2, :], agg_ps[:, :], ACT.Copy).then_inc(agg_copied, 1)
                    g = unit(it, 2, c - 1, GROUPS)
                    if g is not None:
                        wait(act, out_made, g - 1)
                        for chunk in range(HC):
                            act.wait_ge(hid_made, HC * g + chunk + 1)
                            act.activation(hid[:, (c - 1) % 2, chunk, :], hid_ps[:, chunk, :], ACT.Relu,
                                           bias=k.c1[:, chunk:chunk + 1]).then_inc(hid_relu, 1)

                spread_loop(act, slot, **SPAN)

            @block.vector
            def _(dve):
                def slot(it, c):
                    n = unit(it, 2, c + 1, GROUPS)
                    if n is not None:
                        wait(dve, agg_made, n - 1)
                        dve.tensor_copy(xs[:, (c + 1) % 2], group_of(k.x, n)).then_inc(x_copied, 1)
                    g = unit(it, 2, c - 5, GROUPS)
                    if g is not None:
                        norm_apply(dve, k, norm, y, g)
                    g = unit(it, 2, c - 4, GROUPS)
                    if g is not None:
                        dve.wait_ge(out_turned, g + 1)
                        wait(dve, norm["x_next"], g)
                        dve.tensor_tensor(y[:, :, :], back_ps[:, :, :], group_of(k.x, g), ALU.add)\
                           .then_inc(norm["summed"], 1)
                        norm_statistics(dve, k, norm, y, g)

                spread_loop(dve, slot, **SPAN)

            @block.gpsimd
            def _(pool):
                def slot(it, c):
                    n = unit(it, 2, c + 1, GROUPS)
                    if n is not None:
                        wait(pool, agg_made, n - 1)
                        pool.tensor_tensor(adj[:, (c + 1) % 2], group_of(k.adj_t, n),
                                           k.diag2[:, :].unsqueeze(1).to_broadcast([P, QUAD, P]), ALU.add)\
                            .then_inc(diag_added, 1)
                    g = unit(it, 2, c - 4, GROUPS)
                    if g is not None:
                        norm_root(pool, k, norm, g)

                spread_loop(pool, slot, **SPAN)


def gated_highway(k, out_dram):
    nc, GROUPS = k.nc, k.groups
    out_view = out_dram.rearrange("b n d -> n b d")
    W = QUAD * P
    with ExitStack() as ctx:
        xs = k.sb("xs3", [P, 2, QUAD, P], ctx)
        x_t = k.sb("x_t3", [P, 2, W], ctx)
        feat = k.sb("feat", [P, 2, QUAD, P], ctx)
        root = k.sb("root3", [P, 2, QUAD], ctx)
        root_t = k.sb("root_t", [P, 2, W], ctx)
        het = k.sb("het", [P, 2, W], ctx)
        gate = k.sb("gate", [P, 2, W], ctx)
        mix = k.sb("mix", [P, W], ctx)
        neg = k.sb("neg", [P, W], ctx)
        elu = k.sb("elu", [P, W], ctx)
        y = k.sb("y3", [P, QUAD, P], ctx)
        half_bias = k.sb("half_bias", [P, 1], ctx)
        turn_ps = k.psum("turn_ps3", [P, W], ctx)
        feat_ps = k.psum("feat_ps", [P, QUAD, P], ctx)
        het_ps = k.psum("het_ps", [P, W], ctx)
        gate_ps = k.psum("gate_ps", [P, W], ctx)
        hom_ps = k.psum("hom_ps", [P, W], ctx)
        back_ps = k.psum("back_ps3", [P, QUAD, P], ctx)
        x_copied, x_turned, x_t_copied = k.sem("x_copied3"), k.sem("x_turned3"), k.sem("x_t_copied3")
        feat_made, feat_scaled = k.sem("feat_made"), k.sem("feat_scaled")
        het_made, het_copied, gate_made, gate_tanh = k.sem("het_made"), k.sem("het_copied"), k.sem("gate_made"), k.sem("gate_tanh")
        root_made, root_spread, root_copied = k.sem("root_made3"), k.sem("root_spread3"), k.sem("root_copied3")
        hom_made, hom_scaled, differ = k.sem("hom_made"), k.sem("hom_scaled"), k.sem("differ")
        gated, mixed, neg_made, exp_made = k.sem("gated"), k.sem("mixed3"), k.sem("neg_made"), k.sem("exp_made3")
        elu_made, elu_turned, half_made = k.sem("elu_made"), k.sem("elu_turned"), k.sem("half_made")
        stored = k.sem("stored")
        norm = norm_sems(k, 3)
        SPAN = dict(per=2, first=-1, loop_from=3, loop_to=GROUPS // 2 - 1, last=GROUPS // 2 + 3)

        with nc.Block() as block:
            @block.tensor
            def _(pe):
                def slot(it, c):
                    p = c % 2
                    g = unit(it, 2, c, GROUPS)
                    if g is not None:
                        pe.wait_ge(x_copied, g + 1)
                        wait(pe, root_copied, g)
                        for q in range(QUAD):
                            mm = pe.transpose(turn_ps[:, q * P:(q + 1) * P], xs[:, p, q, :], k.eye[:, :])
                        mm.then_inc(x_turned, 1)
                    b = unit(it, 2, c - 1, GROUPS)
                    if b is not None:
                        pe.wait_ge(feat_scaled, b + 1)
                        wait(pe, hom_scaled, b)
                        for q in range(QUAD):
                            mm = pe.matmul(hom_ps[:, q * P:(q + 1) * P], feat[:, (c - 1) % 2, q, :],
                                           k.adj_t[:, bass.ds(b * QUAD + q, 1), :].rearrange("p a n -> p (a n)"),
                                           start=True, stop=True)
                        mm.then_inc(hom_made, 1)
                    b = unit(it, 2, c - 2, GROUPS)
                    if b is not None:
                        pe.wait_ge(elu_made, b + 1)
                        wait(pe, norm["summed"], b)
                        for q in range(QUAD):
                            mm = pe.transpose(back_ps[:, q, :], elu[:, q * P:(q + 1) * P], k.eye[:, :])
                        mm.then_inc(elu_turned, 1)
                    if g is not None:
                        pe.wait_ge(x_t_copied, g + 1)
                        wait(pe, feat_scaled, g)
                        for q in range(QUAD):
                            mm = pe.matmul(feat_ps[:, q, :], x_t[:, p, q * P:(q + 1) * P], k.theta[:, :],
                                           start=True, stop=True)
                        mm.then_inc(feat_made, 1)
                        wait(pe, het_copied, g)
                        pe.matmul(het_ps[:, :], k.w_h[:, :], x_t[:, p, :], start=True, stop=True).then_inc(het_made, 1)
                        wait(pe, gate_tanh, g)
                        pe.matmul(gate_ps[:, :], k.w_t[:, :], x_t[:, p, :], start=True, stop=True)\
                          .then_inc(gate_made, 1)
                        pe.wait_ge(root_made, g + 1)
                        for q in range(QUAD):
                            mm = pe.transpose(turn_ps[:, q * P:(q + 1) * P],
                                              root[:, p, q:q + 1].to_broadcast([P, P]), k.eye[:, :])
                        mm.then_inc(root_spread, 1)

                spread_loop(pe, slot, **SPAN)

            @block.scalar
            def _(act):
                def slot(it, c):
                    p = c % 2
                    g = unit(it, 2, c, GROUPS)
                    if g is not None:
                        act.wait_ge(x_turned, g + 1)
                        wait(act, gate_made, g - 1)
                        act.activation(x_t[:, p, :], turn_ps[:, :], ACT.Copy).then_inc(x_t_copied, 1)
                        act.wait_ge(het_made, g + 1)
                        wait(act, mixed, g - 1)
                        act.activation(het[:, p, :], het_ps[:, :], ACT.Copy).then_inc(het_copied, 1)
                        act.wait_ge(gate_made, g + 1)
                        act.wait_ge(half_made, 1)
                        act.activation(gate[:, p, :], gate_ps[:, :], ACT.Tanh, scale=0.5, bias=half_bias[:, 0:1])\
                           .then_inc(gate_tanh, 1)
                        act.wait_ge(root_spread, g + 1)
                        wait(act, hom_scaled, g - 1)
                        act.activation(root_t[:, p, :], turn_ps[:, :], ACT.Copy).then_inc(root_copied, 1)
                    b = unit(it, 2, c - 1, GROUPS)
                    if b is not None:
                        act.wait_ge(mixed, b + 1)
                        wait(act, elu_made, b)
                        act.activation(neg[:, :], mix[:, :], ACT.Relu, scale=-1.0).then_inc(neg_made, 1)
                        act.wait_ge(neg_made, b + 1)
                        act.activation(neg[:, :], neg[:, :], ACT.Exp, scale=-1.0).then_inc(exp_made, 1)

                spread_loop(act, slot, **SPAN)

            @block.vector
            def _(dve):
                def slot(it, c):
                    b = unit(it, 2, c - 2, GROUPS)
                    if b is not None:
                        dve.wait_ge(exp_made, b + 1)
                        wait(dve, elu_turned, b)
                        dve.scalar_tensor_tensor(out=elu[:, :], in0=neg[:, :], scalar=1.0, in1=mix[:, :],
                                                 op0=ALU.subtract, op1=ALU.max).then_inc(elu_made, 1)
                    n = unit(it, 2, c + 1, GROUPS)
                    if n is not None:
                        wait(dve, x_turned, n - 1)
                        dve.tensor_copy(xs[:, (c + 1) % 2], group_of(k.x, n)).then_inc(x_copied, 1)
                    a = unit(it, 2, c - 1, GROUPS)
                    if a is not None:
                        dve.wait_ge(hom_made, a + 1)
                        dve.wait_ge(root_copied, a + 1)
                        wait(dve, elu_made, a)
                        dve.tensor_tensor(mix[:, :], hom_ps[:, :], root_t[:, (c - 1) % 2, :], ALU.mult)\
                           .then_inc(hom_scaled, 1)
                    g = unit(it, 2, c, GROUPS)
                    if g is not None:
                        dve.wait_ge(feat_made, g + 1)
                        dve.wait_ge(root_made, g + 1)
                        wait(dve, hom_made, g - 1)
                        dve.tensor_tensor(feat[:, c % 2], feat_ps[:, :, :],
                                          root[:, c % 2, :].unsqueeze(2).to_broadcast([P, QUAD, P]), ALU.mult)\
                           .then_inc(feat_scaled, 1)
                    if b is not None:
                        dve.wait_ge(elu_turned, b + 1)
                        wait(dve, norm["x_next"], b)
                        dve.tensor_tensor(y[:, :, :], back_ps[:, :, :], group_of(k.x, b), ALU.add)\
                           .then_inc(norm["summed"], 1)
                        norm_statistics(dve, k, norm, y, b)
                    if a is not None:
                        dve.wait_ge(differ, a + 1)
                        dve.wait_ge(gate_tanh, a + 1)
                        dve.scalar_tensor_tensor(out=mix[:, :], in0=gate[:, (c - 1) % 2, :], scalar=1.0,
                                                 in1=mix[:, :], op0=ALU.add, op1=ALU.mult).then_inc(gated, 1)
                        dve.wait_ge(gated, a + 1)
                        dve.scalar_tensor_tensor(out=mix[:, :], in0=mix[:, :], scalar=0.5,
                                                 in1=het[:, (c - 1) % 2, :], op0=ALU.mult, op1=ALU.add)\
                           .then_inc(mixed, 1)
                    if b is not None:
                        norm_apply(dve, k, norm, y, b)

                dve.tensor_scalar(half_bias[:, :], k.b_t[:, :], 0.5, None, ALU.mult).then_inc(half_made, 1)
                spread_loop(dve, slot, **SPAN)

            @block.gpsimd
            def _(pool):
                def slot(it, c):
                    n = unit(it, 2, c + 1, GROUPS)
                    if n is not None:
                        wait(pool, root_spread, n - 1)
                        wait(pool, feat_scaled, n - 1)
                        pool.tensor_tensor(root[:, (c + 1) % 2, :], k.degree[:, bass.ds(n * QUAD, QUAD)],
                                           k.minus_half[:, :], ALU.pow).then_inc(root_made, 1)
                    a = unit(it, 2, c - 1, GROUPS)
                    if a is not None:
                        pool.wait_ge(hom_scaled, a + 1)
                        pool.wait_ge(het_copied, a + 1)
                        pool.tensor_tensor(mix[:, :], mix[:, :], het[:, (c - 1) % 2, :], ALU.subtract)\
                            .then_inc(differ, 1)
                    b = unit(it, 2, c - 2, GROUPS)
                    if b is not None:
                        norm_root(pool, k, norm, b)

                spread_loop(pool, slot, **SPAN)

            @block.sync
            def _(sp):
                with sp.Fori(0, GROUPS) as g:
                    sp.wait_ge(norm["x_next"], g + 1)
                    sp.dma_start(group_of(out_view, g), group_of(k.x, g)).then_inc(stored, 16)
                sp.wait_ge(stored, 16 * GROUPS)


def four_layers(nc, w, out):
    with ExitStack() as ctx:
        k = Core(nc, ctx)
        k.graphs = w["x"].shape[0]
        k.groups = k.graphs // QUAD
        k.heads = w["L0_gnn_fc_w"].shape[1] // P
        k.hid1 = w["L1_gnn_W1"].shape[1] // P
        k.hid2 = w["L2_gnn_W1"].shape[1] // P
        H = k.heads
        k.x = k.sb("x_all", [P, k.graphs, P])
        k.adj_t = k.sb("adj_t_all", [P, k.graphs, P])
        k.degree = k.sb("degree", [P, k.graphs])
        k.eye = k.sb("eye_sb", [P, P])
        k.minus_half = k.sb("minus_half", [P, QUAD])
        k.bn, k.mv = k.sb("bn", [P, QUAD, 6]), k.sb("mv", [P, QUAD, 2])
        k.var, k.rstd = k.sb("var", [P, QUAD]), k.sb("rstd", [P, QUAD])
        k.always = k.sem("always")
        with ExitStack() as weights:
            k.fold = k.sb("fold", [P, H, P], weights)
            k.wqk = k.sb("wqk", [P, 2, H], weights)
            k.qk_bias = k.sb("qk_bias", [P, 2, H], weights)
            k.out_bias = k.sb("out_bias", [P, 1], weights)
            prepare_attention(k, w)
            attention(k, w["x"], w["adj"])
        k.ones = k.sb("ones", [P, 1])
        k.w1, k.b1, k.rmsw = k.sb("w1", [P, k.hid1, P]), k.sb("b1", [P, k.hid1]), k.sb("rmsw", [P, k.hid1])
        k.w2, k.b2 = k.sb("w2", [P, k.hid1, P]), k.sb("b2", [P, 1])
        k.gram, k.gram_bias = k.sb("gram", [P, P]), k.sb("gram_bias", [P, 1])
        k.square_bias = k.sb("square_bias", [P, 1])
        k.diag1, k.diag2 = k.sb("diag1", [P, P]), k.sb("diag2", [P, P])
        k.v1, k.c1 = k.sb("v1", [P, k.hid2, P]), k.sb("c1", [P, k.hid2])
        k.v2, k.c2 = k.sb("v2", [P, k.hid2, P]), k.sb("c2", [P, 1])
        k.w_t, k.b_t = k.sb("w_t", [P, P]), k.sb("b_t", [P, 1])
        k.w_h, k.theta = k.sb("w_h", [P, P]), k.sb("theta", [P, P])
        prepare_mlps(k, w)
        rms_mlp(k)
        relu_mlp(k)
        gated_highway(k, out)


_INS = ['x', 'adj', 'L0_gnn_fc_w', 'L0_gnn_fc_b', 'L0_gnn_q_w', 'L0_gnn_q_b', 'L0_gnn_k_w', 'L0_gnn_k_b',
        'L0_gnn_fp_w', 'L0_gnn_fp_b', 'L1_gnn_epsilon', 'L1_gnn_W1', 'L1_gnn_b1', 'L1_gnn_rms_weight', 'L1_gnn_W2',
        'L1_gnn_b2', 'L2_gnn_eps', 'L2_gnn_W1', 'L2_gnn_b1', 'L2_gnn_W2', 'L2_gnn_b2', 'L3_gnn_W_t', 'L3_gnn_b_t',
        'L3_gnn_W_h', 'L3_gnn_theta']

_BY_PARTITION = ['L0_gnn_fc_b', 'L0_gnn_fp_b', 'L1_gnn_b1', 'L1_gnn_rms_weight', 'L1_gnn_b2', 'L2_gnn_b1',
                 'L2_gnn_b2', 'L3_gnn_b_t']


def kernel(**inputs):
    import numpy as _np
    import concourse.bacc as _bacc
    from concourse import mybir as _mybir
    from concourse.bass_utils import run_bass_kernel_spmd as _run

    nc = _bacc.Bacc("TRN2", target_bir_lowering=False, num_devices=1)
    arrays, args = {}, {}
    for name in _INS:
        a = _np.asarray(inputs[name])
        if name in _BY_PARTITION:
            a = a.reshape(-1, P).T
        a = _np.ascontiguousarray(a.reshape(1) if a.ndim == 0 else a)
        arrays[f"in_{name}"] = a
        args[name] = nc.dram_tensor(f"in_{name}", a.shape, _mybir.dt.from_np(a.dtype), kind="ExternalInput").ap()
    arrays["in_eye"] = _np.eye(P, dtype=_np.float32)
    args["eye"] = nc.dram_tensor("in_eye", (P, P), _mybir.dt.float32, kind="ExternalInput").ap()
    out = nc.dram_tensor("out_0", inputs["x"].shape, _mybir.dt.float32, kind="ExternalOutput").ap()
    four_layers(nc, args, out)
    r = _run(nc, [arrays], core_ids=[0])
    return r.results[0]["out_0"]
```

```python
from contextlib import ExitStack

import concourse.bass as bass
from concourse import mybir

F32 = mybir.dt.float32
ALU = mybir.AluOpType
ACT = mybir.ActivationFunctionType
AX_X = mybir.AxisListType.X

P = 128
QUAD = 4
NEG = 1.0e9
SLOPE = 0.01
LN_EPS = 1e-5
RMS_EPS = 1e-6
DEG_EPS = 1e-6


def unit(it, per, offset, count):
    n = it * per + offset
    if isinstance(n, int) and not 0 <= n < count:
        return None
    return n


def wait(eng, sem, count):
    if isinstance(count, int) and count <= 0:
        return
    eng.wait_ge(sem, count)


def cap(count, most):
    return min(count, most) if isinstance(count, int) else count


def spread_loop(eng, slot, per, first, loop_from, loop_to, last):
    for it in range(first, loop_from):
        for c in range(per):
            slot(it, c)
    with eng.Fori(loop_from, loop_to) as it:
        for c in range(per):
            slot(it, c)
    for it in range(loop_to, last):
        for c in range(per):
            slot(it, c)


class Core:

    def __init__(self, nc, ctx):
        self.nc, self.ctx, self.count = nc, ctx, 0

    def sb(self, name, shape, ctx=None, dtype=F32):
        return (ctx or self.ctx).enter_context(self.nc.sbuf_tensor(name, shape, dtype))

    def psum(self, name, shape, ctx):
        return ctx.enter_context(self.nc.psum_tensor(name, shape, F32))

    def sem(self, name):
        return self.ctx.enter_context(self.nc.semaphore(name))


def start_loads(k, loads, loaded, sp, queue):
    for dst, src in loads[queue::2]:
        sp.dma_start(dst, src).then_inc(loaded, 16)


def prepare_attention(k, w):
    nc, H = k.nc, k.heads
    with ExitStack() as ctx:
        fc = k.sb("fc", [P, H, P], ctx)
        fp = k.sb("fp", [P, H, P], ctx)
        fc_t = k.sb("fc_t", [P, H, P], ctx)
        fcb = k.sb("fcb", [P, H], ctx)
        qkw = k.sb("qkw", [P, 2], ctx)
        qkb = k.sb("qkb", [P, 2], ctx)
        fpb = k.sb("fpb", [P, 1], ctx)
        turn_ps = k.psum("fc_turn_ps", [P, H, P], ctx)
        fold_ps = k.psum("fold_ps", [P, H, P], ctx)
        qk_ps = k.psum("qk_ps", [P, 512], ctx)
        bias_ps = k.psum("bias_ps", [P, 512], ctx)
        loaded, turned, copied = k.sem("weights0_loaded"), k.sem("fc_turned"), k.sem("fc_copied")
        multiplied = k.sem("fc_multiplied")
        loads = [
            (fc[:, :, :], w["L0_gnn_fc_w"].rearrange("d (h e) -> d h e", h=H)),
            (k.eye[:, :], w["eye"]),
            (fp[:, :, :], w["L0_gnn_fp_w"].rearrange("(h d) e -> d h e", h=H)),
            (fcb[:, :], w["L0_gnn_fc_b"]),
            (qkw[:, 0:1], w["L0_gnn_q_w"]),
            (qkw[:, 1:2], w["L0_gnn_k_w"]),
            (qkb[:, 0:1], w["L0_gnn_q_b"].partition_broadcast(P)),
            (qkb[:, 1:2], w["L0_gnn_k_b"].partition_broadcast(P)),
            (fpb[:, :], w["L0_gnn_fp_b"]),
        ]
        with nc.Block() as block:
            @block.sync
            def _(sp):
                start_loads(k, loads, loaded, sp, 0)

            @block.scalar
            def _(act):
                start_loads(k, loads, loaded, act, 1)

            @block.gpsimd
            def _(pool):
                pool.memset(k.minus_half[:, :], -0.5)
                pool.memset(k.bn[:, :, :], 0.0).then_inc(k.always, 1)

            @block.tensor
            def _(pe):
                pe.wait_ge(loaded, 16 * len(loads))
                for h in range(H):
                    mm = pe.transpose(turn_ps[:, h, :], fc[:, h, :], k.eye[:, :])
                mm.then_inc(turned, 1)
                pe.wait_ge(copied, 1)
                for h in range(H):
                    pe.matmul(fold_ps[:, h, :], fc_t[:, h, :], fp[:, h, :], start=True, stop=True)
                for h in range(H):
                    pe.matmul(qk_ps[:, 2 * h:2 * h + 2], fc_t[:, h, :], qkw[:, :], start=True, stop=True)
                for h in range(H):
                    pe.matmul(qk_ps[:, 2 * H + 2 * h:2 * H + 2 * h + 2], fcb[:, h:h + 1].to_broadcast([P, P]),
                              qkw[:, :], start=True, stop=True)
                for h in range(H):
                    mm = pe.matmul(bias_ps[:, 0:1], fp[:, h, :], fcb[:, h:h + 1], start=(h == 0), stop=(h == H - 1))
                mm.then_inc(multiplied, 1)

            @block.vector
            def _(dve):
                dve.wait_ge(turned, 1)
                dve.tensor_copy(fc_t[:, :, :], turn_ps[:, :, :]).then_inc(copied, 1)
                dve.wait_ge(multiplied, 1)
                dve.tensor_copy(k.fold[:, :, :], fold_ps[:, :, :])
                dve.tensor_copy(k.wqk[:, :, :], qk_ps[:, 0:2 * H].rearrange("d (h t) -> d t h", t=2))
                dve.tensor_tensor(k.qk_bias[:, :, :], qk_ps[:, 2 * H:4 * H].rearrange("d (h t) -> d t h", t=2),
                                  qkb[:, :].unsqueeze(2).to_broadcast([P, 2, H]), ALU.add)
                dve.tensor_tensor(k.out_bias[:, :], bias_ps[:, 0:1], fpb[:, :], ALU.add)


def prepare_mlps(k, w):
    nc, HC = k.nc, k.hid1
    with ExitStack() as ctx:
        w1_t = k.sb("w1_t", [P, HC, P], ctx)
        eps1 = k.sb("eps1", [P, 1], ctx)
        eps2 = k.sb("eps2", [P, 1], ctx)
        eps2p = k.sb("eps2p", [P, 1], ctx)
        turn_ps = k.psum("w1_turn_ps", [P, HC, P], ctx)
        gram_ps = k.psum("w1_gram_ps", [P, 512], ctx)
        loaded, turned, copied = k.sem("weights1_loaded"), k.sem("w1_turned"), k.sem("w1_copied")
        multiplied, one_added = k.sem("w1_multiplied"), k.sem("one_added")
        loads = [
            (k.w1[:, :, :], w["L1_gnn_W1"].rearrange("d (c h) -> d c h", c=HC)),
            (k.b1[:, :], w["L1_gnn_b1"]),
            (k.w2[:, :, :], w["L1_gnn_W2"].rearrange("(c h) d -> h c d", c=HC)),
            (k.rmsw[:, :], w["L1_gnn_rms_weight"]),
            (k.b2[:, :], w["L1_gnn_b2"]),
            (eps1[:, :], w["L1_gnn_epsilon"].partition_broadcast(P)),
            (k.v1[:, :, :], w["L2_gnn_W1"].rearrange("d (c h) -> d c h", c=k.hid2)),
            (k.c1[:, :], w["L2_gnn_b1"]),
            (k.v2[:, :, :], w["L2_gnn_W2"].rearrange("(c h) d -> h c d", c=k.hid2)),
            (k.c2[:, :], w["L2_gnn_b2"]),
            (eps2[:, :], w["L2_gnn_eps"].partition_broadcast(P)),
            (k.w_ht[:, 0, :], w["L3_gnn_W_h"]),
            (k.w_ht[:, 1, :], w["L3_gnn_W_t"]),
            (k.b_t[:, :], w["L3_gnn_b_t"].unsqueeze(0)),
            (k.theta[:, :], w["L3_gnn_theta"]),
        ]
        with nc.Block() as block:
            @block.sync
            def _(sp):
                start_loads(k, loads, loaded, sp, 0)

            @block.scalar
            def _(act):
                start_loads(k, loads, loaded, act, 1)

            @block.gpsimd
            def _(pool):
                pool.memset(k.ones[:, :], 1.0 / (HC * P))
                pool.memset(k.one_row[:, :], 1.0)
                pool.tensor_tensor(k.root[:, :], k.degree[:, :], k.minus_half[:, 0:1].to_broadcast([P, k.graphs]),
                                   ALU.pow)

            @block.tensor
            def _(pe):
                pe.wait_ge(loaded, 16 * len(loads))
                for c in range(HC):
                    mm = pe.transpose(turn_ps[:, c, :], k.w1[:, c, :], k.eye[:, :])
                mm.then_inc(turned, 1)
                pe.wait_ge(copied, 1)
                for c in range(HC):
                    pe.matmul(gram_ps[:, 0:P], w1_t[:, c, :], w1_t[:, c, :], start=(c == 0), stop=(c == HC - 1))
                for c in range(HC):
                    pe.matmul(gram_ps[:, P:P + 1], w1_t[:, c, :], k.b1[:, c:c + 1], start=(c == 0),
                              stop=(c == HC - 1))
                for c in range(HC):
                    mm = pe.matmul(gram_ps[:, P + 1:P + 2], k.b1[:, c:c + 1].to_broadcast([P, P]),
                                   k.b1[:, c:c + 1], start=(c == 0), stop=(c == HC - 1))
                mm.then_inc(multiplied, 1)

            @block.vector
            def _(dve):
                dve.wait_ge(turned, 1)
                dve.tensor_copy(w1_t[:, :, :], turn_ps[:, :, :]).then_inc(copied, 1)
                dve.wait_ge(loaded, 16 * len(loads))
                dve.tensor_scalar(eps2p[:, :], eps2[:, :], 1.0, None, ALU.add).then_inc(one_added, 1)
                dve.tensor_scalar(k.diag1[:, :], k.eye[:, :], eps1[:, 0:1], None, ALU.mult)
                dve.wait_ge(one_added, 1)
                dve.tensor_scalar(k.diag2[:, :], k.eye[:, :], eps2p[:, 0:1], None, ALU.mult)
                dve.wait_ge(multiplied, 1)
                dve.tensor_copy(k.gram[:, :], gram_ps[:, 0:P])
                dve.tensor_scalar(k.gram_bias[:, :], gram_ps[:, P:P + 1], 2.0, None, ALU.mult)
                dve.tensor_scalar(k.square_bias[:, :], gram_ps[:, P + 1:P + 2], 1.0 / (HC * P), RMS_EPS,
                                  ALU.mult, ALU.add)


def norm_sems(k, layer):
    return {n: k.sem(f"{n}_{layer}") for n in ("summed", "stats", "moments", "var", "rstd", "x_next")}


def norm_statistics(dve, k, s, y, g):
    dve.wait_ge(s["summed"], g + 1)
    for q in range(QUAD):
        last = dve.bn_stats(k.bn[:, q, :], y[:, q, :])
    last.then_inc(s["stats"], 1)
    dve.wait_ge(k.always, 1)
    dve.wait_ge(s["stats"], g + 1)
    for q in range(QUAD):
        last = dve.bn_aggr(k.mv[:, q, :], k.bn[:, q, :])
    last.then_inc(s["moments"], 1)
    dve.wait_ge(s["moments"], g + 1)
    wait(dve, s["rstd"], g)
    dve.tensor_scalar(k.var[:, :], k.mv[:, :, 1], LN_EPS, None, ALU.add).then_inc(s["var"], 1)


def norm_root(pool, k, s, g):
    pool.wait_ge(s["var"], g + 1)
    wait(pool, s["x_next"], g)
    pool.tensor_tensor(k.rstd[:, :], k.var[:, :], k.minus_half[:, :], ALU.pow).then_inc(s["rstd"], 1)


def norm_apply(dve, k, s, y, g):
    dve.wait_ge(s["rstd"], g + 1)
    for q in range(QUAD):
        last = dve.tensor_scalar(k.x[:, bass.ds(g * QUAD + q, 1), :].rearrange("p a d -> p (a d)"), y[:, q, :],
                                 k.mv[:, q, 0:1], k.rstd[:, q:q + 1], ALU.subtract, ALU.mult)
    last.then_inc(s["x_next"], 1)


def group_of(t, g):
    return t[:, bass.ds(g * QUAD, QUAD), :]


def attention(k, x_dram, adj_dram):
    nc, H = k.nc, k.heads
    GROUPS, GRAPHS = k.groups, k.graphs
    x_view = x_dram.rearrange("b n d -> n b d")
    adj_view = adj_dram.rearrange("b n m -> n b m")
    with ExitStack() as ctx:
        xin = k.sb("xin", [P, QUAD, P], ctx)
        ain = k.sb("ain", [P, 2, QUAD, P], ctx)
        val = k.sb("val", [P, 2, QUAD, P], ctx)
        x_t = k.sb("x_t", [P, QUAD, P], ctx)
        qk = k.sb("qk", [P, 2, QUAD, 2, H], ctx)
        score = k.sb("score", [P, 4, H, P], ctx)
        probs_t = k.sb("probs_t", [P, 2, H, P], ctx)
        mixed = k.sb("mixed", [P, 2, H, QUAD, P], ctx)
        neg_max = k.sb("neg_max", [P, 2, H], ctx)
        total = k.sb("total", [P, 2, H], ctx)
        recip = k.sb("recip", [P, 2, H], ctx)
        out_t = k.sb("out_t", [P, QUAD, P], ctx)
        y = k.sb("y0", [P, QUAD, P], ctx)
        key_ps = k.psum("key_ps", [P, H, P], ctx)
        turn_ps = k.psum("turn_ps", [P, H, P], ctx)
        mix_ps = k.psum("mix_ps", [P, H, P], ctx)
        out_ps = k.psum("out_ps", [P, QUAD, P], ctx)
        misc_ps = k.psum("misc_ps", [P, 512], ctx)
        quad_ps = misc_ps[:, :].rearrange("p (q n) -> p q n", q=QUAD)

        x_loaded = k.sem("x_loaded")
        adj_loaded = [k.sem(f"adj_loaded{i}") for i in range(2)]
        val_loaded = [k.sem(f"val_loaded{i}") for i in range(2)]
        all_x_loaded = k.sem("all_x_loaded")
        adj_turned, adj_copied = k.sem("adj_turned"), k.sem("adj_copied")
        x_turned, x_copied = k.sem("x_turned"), k.sem("x_copied")
        qk_made, qk_copied, mask_made = k.sem("qk_made"), k.sem("qk_copied"), k.sem("mask_made")
        degree_summed = k.sem("degree_summed")
        keys_spread, query_added = k.sem("keys_spread"), k.sem("query_added")
        scores_made, scores_leaky = k.sem("scores_made"), k.sem("scores_leaky")
        max_found, exp_made, recip_made = k.sem("max_found"), k.sem("exp_made"), k.sem("recip_made")
        probs_made, probs_turned, probs_copied = k.sem("probs_made"), k.sem("probs_turned"), k.sem("probs_copied")
        mix_made, mix_copied = k.sem("mix_made"), k.sem("mix_copied")
        out_made, out_copied, out_turned = k.sem("out_made"), k.sem("out_copied"), k.sem("out_turned")
        feats_added, tanh_made, sigmoid_made = k.sem("feats_added"), k.sem("tanh_made"), k.sem("sigmoid_made")
        norm = norm_sems(k, 0)
        PER = 2 * QUAD
        SPAN = dict(per=PER, first=-1, loop_from=2, loop_to=GRAPHS // PER - 1, last=GRAPHS // PER + 2)

        with nc.Block() as block:
            @block.sync
            def _(sp):
                def load(it, j):
                    g = unit(it, 2, j, GROUPS)
                    wait(sp, query_added, QUAD * (g - 1))
                    sp.dma_start(ain[:, j], group_of(adj_view, g)).then_inc(adj_loaded[j], 16)
                    wait(sp, x_turned, g)
                    sp.dma_start(xin[:, :, :], group_of(x_view, g)).then_inc(x_loaded, 16)
                    wait(sp, mix_made, QUAD * (g - 1))
                    sp.dma_start(val[:, j], group_of(x_view, g)).then_inc(val_loaded[j], 16)

                for j in range(2):
                    load(0, j)
                for part in range(4):
                    n = GRAPHS // 4
                    sp.dma_start(k.x[:, part * n:(part + 1) * n, :],
                                 x_view[:, part * n:(part + 1) * n, :]).then_inc(all_x_loaded, 16)
                for j in range(2):
                    load(1, j)
                with sp.Fori(2, GROUPS // 2) as it:
                    for j in range(2):
                        load(it, j)

            @block.tensor
            def _(pe):
                def slot(it, c):
                    b = unit(it, PER, c - 2, GRAPHS)
                    if b is not None:
                        pe.wait_ge(probs_made, b + 1)
                        wait(pe, probs_copied, b)
                        for h in range(H):
                            mm = pe.transpose(turn_ps[:, h, :], score[:, (c - 2) % 4, h, :], k.eye[:, :])
                        mm.then_inc(probs_turned, 1)
                    g = unit(it, 2, c // QUAD + 1, GROUPS)
                    j = (c // QUAD + 1) % 2
                    if c % QUAD == 0 and g is not None:
                        pe.wait_ge(adj_loaded[j], 16 * (it + (c // QUAD + 1) // 2 + 1))
                        wait(pe, feats_added, g - 3)
                        for q in range(QUAD):
                            mm = pe.transpose(quad_ps[:, q, :], ain[:, j, q, :], k.eye[:, :])
                        mm.then_inc(adj_turned, 1)
                    if c % QUAD == 1 and g is not None:
                        pe.wait_ge(x_loaded, 16 * (g + 1))
                        pe.wait_ge(adj_copied, g + 1)
                        for q in range(QUAD):
                            mm = pe.transpose(quad_ps[:, q, :], xin[:, q, :], k.eye[:, :])
                        mm.then_inc(x_turned, 1)
                    if c % QUAD == 2 and g is not None:
                        pe.wait_ge(x_copied, g + 1)
                        for q in range(QUAD):
                            mm = pe.matmul(misc_ps[:, 2 * H * q:2 * H * (q + 1)], x_t[:, q, :],
                                           k.wqk[:, :, :].rearrange("d t h -> d (t h)"), start=True, stop=True)
                        mm.then_inc(qk_made, 1)
                    g = unit(it, 2, (c - 11) // QUAD, GROUPS)
                    if c % QUAD == 3 and g is not None:
                        pe.wait_ge(out_copied, g + 1)
                        pe.wait_ge(qk_copied, cap(g + 4, GROUPS))
                        for q in range(QUAD):
                            mm = pe.transpose(quad_ps[:, q, :], out_t[:, q, :], k.eye[:, :])
                        mm.then_inc(out_turned, 1)
                    g = unit(it, 2, (c - 7) // QUAD, GROUPS)
                    part = (c - 7) % QUAD
                    if g is not None:
                        if part == 0:
                            pe.wait_ge(mix_copied, QUAD * (g + 1))
                            wait(pe, out_copied, g)
                        for h in range(part * H // QUAD, (part + 1) * H // QUAD):
                            mm = pe.matmul(out_ps[:, :, :], k.fold[:, h, :], mixed[:, ((c - 7) // QUAD) % 2, h, :, :],
                                           start=(h == 0), stop=(h == H - 1))
                        if part == QUAD - 1:
                            mm.then_inc(out_made, 1)
                    b = unit(it, PER, c + 1, GRAPHS)
                    if b is not None:
                        pe.wait_ge(qk_copied, unit(it, 2, (c + 1) // QUAD, GROUPS) + 1)
                        wait(pe, scores_made, b)
                        for h in range(H):
                            mm = pe.transpose(key_ps[:, h, :],
                                              qk[:, ((c + 1) // QUAD) % 2, (c + 1) % QUAD, 1, h:h + 1].to_broadcast([P, P]),
                                              k.eye[:, :])
                        mm.then_inc(keys_spread, 1)
                    b = unit(it, PER, c - 2, GRAPHS)
                    if b is not None:
                        j = ((c - 2) // QUAD) % 2
                        pe.wait_ge(val_loaded[j], 16 * (it + (c - 2) // QUAD // 2 + 1))
                        pe.wait_ge(probs_copied, b + 1)
                        wait(pe, mix_copied, b)
                        for half in range(2):
                            hs = slice(half * H // 2, (half + 1) * H // 2)
                            mm = pe.matmul(mix_ps[:, hs, :], val[:, j, (c - 2) % QUAD, :], probs_t[:, c % 2, hs, :],
                                           start=True, stop=True)
                        mm.then_inc(mix_made, 1)

                spread_loop(pe, slot, **SPAN)

            @block.scalar
            def _(act):
                def slot(it, c):
                    b = unit(it, PER, c - 2, GRAPHS)
                    if b is not None:
                        act.wait_ge(probs_turned, b + 1)
                        wait(act, mix_made, b - 1)
                        act.activation(probs_t[:, c % 2], turn_ps[:, :, :], ACT.Copy).then_inc(probs_copied, 1)
                    b = unit(it, PER, c - 3, GRAPHS)
                    if b is not None:
                        act.wait_ge(mix_made, b + 1)
                        if (c - 3) % QUAD == 0:
                            wait(act, out_made, unit(it, 2, (c - 3) // QUAD, GROUPS) - 1)
                        act.activation(mixed[:, ((c - 3) // QUAD) % 2, :, (c - 3) % QUAD, :], mix_ps[:, :, :],
                                       ACT.Copy).then_inc(mix_copied, 1)
                    g = unit(it, 2, c // QUAD + 1, GROUPS)
                    if c % QUAD == 0 and g is not None:
                        act.wait_ge(adj_turned, g + 1)
                        act.activation(group_of(k.adj_t, g), quad_ps, ACT.Copy).then_inc(adj_copied, 1)
                    if c % QUAD == 1 and g is not None:
                        act.wait_ge(x_turned, g + 1)
                        wait(act, qk_made, g)
                        act.activation(x_t[:, :, :], quad_ps, ACT.Copy).then_inc(x_copied, 1)
                    g = unit(it, 2, (c - 12) // QUAD, GROUPS)
                    if c % QUAD == 0 and g is not None:
                        act.wait_ge(feats_added, g + 1)
                        act.activation(y[:, :, :], y[:, :, :], ACT.Tanh, scale=0.5).then_inc(tanh_made, 1)
                    g = unit(it, 2, (c - 10) // QUAD, GROUPS)
                    if c % QUAD == 2 and g is not None:
                        act.wait_ge(out_made, g + 1)
                        wait(act, out_turned, g)
                        act.activation(out_t[:, :, :], out_ps[:, :, :], ACT.Identity,
                                       bias=k.out_bias[:, 0:1]).then_inc(out_copied, 1)
                    b = unit(it, PER, c, GRAPHS)
                    if b is not None:
                        act.wait_ge(max_found, b + 1)
                        wait(act, recip_made, b - 1)
                        for h in range(H):
                            e = act.activation(score[:, c % 4, h, :], score[:, c % 4, h, :], ACT.Exp,
                                               bias=neg_max[:, c % 2, h:h + 1], accum_out=total[:, c % 2, h:h + 1])
                        e.then_inc(exp_made, 1)

                spread_loop(act, slot, **SPAN)

            @block.vector
            def _(dve):
                def slot(it, c):
                    b = unit(it, PER, c, GRAPHS)
                    if b is not None:
                        dve.wait_ge(keys_spread, b + 1)
                        dve.wait_ge(query_added, b + 1)
                        dve.tensor_tensor(score[:, c % 4], key_ps[:, :, :], score[:, c % 4], ALU.add)\
                           .then_inc(scores_made, 1)
                        dve.wait_ge(scores_made, b + 1)
                        dve.scalar_tensor_tensor(out=score[:, c % 4], in0=score[:, c % 4], scalar=SLOPE,
                                                 in1=score[:, c % 4], op0=ALU.mult, op1=ALU.max)\
                           .then_inc(scores_leaky, 1)
                    before = unit(it, PER, c - 1, GRAPHS)
                    if before is not None:
                        dve.wait_ge(exp_made, before + 1)
                        wait(dve, probs_made, before - 1)
                        dve.reciprocal(recip[:, (c - 1) % 2, :], total[:, (c - 1) % 2, :]).then_inc(recip_made, 1)
                    if b is not None:
                        dve.wait_ge(scores_leaky, b + 1)
                        wait(dve, exp_made, b - 1)
                        dve.tensor_reduce(neg_max[:, c % 2, :], score[:, c % 4], AX_X, ALU.max, negate=True)\
                           .then_inc(max_found, 1)
                    g = unit(it, 2, c // QUAD + 1, GROUPS)
                    j = (c // QUAD + 1) % 2
                    if c % QUAD == 0 and g is not None:
                        dve.wait_ge(adj_loaded[j], 16 * (it + (c // QUAD + 1) // 2 + 1))
                        dve.tensor_reduce(k.degree[:, bass.ds(g * QUAD, QUAD)], ain[:, j], AX_X, ALU.add)\
                           .then_inc(degree_summed, 1)
                        dve.wait_ge(degree_summed, g + 1)
                        dve.wait_ge(adj_turned, g + 1)
                        dve.tensor_scalar(ain[:, j], ain[:, j], 1.0, NEG, ALU.subtract, ALU.mult)\
                           .then_inc(mask_made, 1)
                    if c % QUAD == 2 and g is not None:
                        dve.wait_ge(qk_made, g + 1)
                        dve.tensor_tensor(qk[:, j].rearrange("p q t h -> p q (t h)"),
                                          misc_ps[:, 0:2 * H * QUAD].rearrange("p (q m) -> p q m", q=QUAD),
                                          k.qk_bias[:, :, :].rearrange("p t h -> p (t h)").unsqueeze(1)
                                          .to_broadcast([P, QUAD, 2 * H]), ALU.add).then_inc(qk_copied, 1)
                    g = unit(it, 2, (c - 11) // QUAD, GROUPS)
                    if c % QUAD == 3 and g is not None:
                        dve.wait_ge(out_turned, g + 1)
                        dve.wait_ge(all_x_loaded, 64)
                        wait(dve, norm["x_next"], g)
                        dve.tensor_tensor(y[:, :, :], quad_ps, group_of(k.x, g), ALU.add).then_inc(feats_added, 1)
                    g = unit(it, 2, (c - 13) // QUAD, GROUPS)
                    if c % QUAD == 1 and g is not None:
                        dve.wait_ge(tanh_made, g + 1)
                        dve.tensor_scalar(y[:, :, :], y[:, :, :], 0.5, 0.5, ALU.mult, ALU.add)\
                           .then_inc(sigmoid_made, 1)
                        dve.wait_ge(sigmoid_made, g + 1)
                        dve.tensor_tensor(y[:, :, :], y[:, :, :], group_of(k.x, g), ALU.add)\
                           .then_inc(norm["summed"], 1)
                        norm_statistics(dve, k, norm, y, g)
                    g = unit(it, 2, (c - 14) // QUAD, GROUPS)
                    if c % QUAD == 2 and g is not None:
                        norm_apply(dve, k, norm, y, g)

                spread_loop(dve, slot, **SPAN)
                dve.tensor_scalar(k.degree[:, :], k.degree[:, :], DEG_EPS, None, ALU.add)

            @block.gpsimd
            def _(pool):
                def slot(it, c):
                    b = unit(it, PER, c + 1, GRAPHS)
                    if b is not None:
                        g = unit(it, 2, (c + 1) // QUAD, GROUPS)
                        j = ((c + 1) // QUAD) % 2
                        pool.wait_ge(mask_made, g + 1)
                        pool.wait_ge(qk_copied, g + 1)
                        wait(pool, probs_turned, b - 3)
                        pool.tensor_tensor(score[:, (c + 1) % 4],
                                           ain[:, j, (c + 1) % QUAD, :].unsqueeze(1).to_broadcast([P, H, P]),
                                           qk[:, j, (c + 1) % QUAD, 0, :].unsqueeze(2).to_broadcast([P, H, P]),
                                           ALU.add).then_inc(query_added, 1)
                    g = unit(it, 2, (c - 14) // QUAD, GROUPS)
                    if c % QUAD == 2 and g is not None:
                        norm_root(pool, k, norm, g)
                    b = unit(it, PER, c - 1, GRAPHS)
                    if b is not None:
                        pool.wait_ge(recip_made, b + 1)
                        pool.tensor_tensor(score[:, (c - 1) % 4], score[:, (c - 1) % 4],
                                           recip[:, (c - 1) % 2, :].unsqueeze(2).to_broadcast([P, H, P]),
                                           ALU.mult).then_inc(probs_made, 1)

                spread_loop(pool, slot, **SPAN)


def rms_mlp(k):
    nc, HC, GROUPS = k.nc, k.hid1, k.groups
    with ExitStack() as ctx:
        xs = k.sb("xs1", [P, 2, QUAD, P], ctx)
        adj = k.sb("adj1", [P, 2, QUAD, P], ctx)
        agg = k.sb("agg1", [P, 2, QUAD * P], ctx)
        prod = k.sb("prod", [P, QUAD * P], ctx)
        root_in = k.sb("root_in", [P, QUAD], ctx)
        root = k.sb("root", [P, QUAD], ctx)
        scale = k.sb("scale", [P, QUAD * P], ctx)
        hid = k.sb("hid1", [P, 2, HC, QUAD * P], ctx)
        out_t = k.sb("out_t1", [P, QUAD * P], ctx)
        y = k.sb("y1", [P, QUAD, P], ctx)
        agg_ps = k.psum("agg_ps", [P, QUAD * P], ctx)
        gram_ps = k.psum("gram_ps", [P, QUAD * P], ctx)
        root_ps = k.psum("root_ps", [P, QUAD * P], ctx)
        hid_ps = k.psum("hid_ps", [P, 2, QUAD * P], ctx)
        out_ps = k.psum("out_ps1", [P, QUAD * P], ctx)
        back_ps = k.psum("back_ps", [P, QUAD, P], ctx)
        x_copied, diag_added = k.sem("x_copied1"), k.sem("diag_added1")
        agg_made, agg_copied = k.sem("agg_made1"), k.sem("agg_copied1")
        gram_made, prod_made = k.sem("gram_made"), k.sem("prod_made")
        squares_summed, root_asked, root_made = k.sem("squares_summed"), k.sem("root_asked"), k.sem("root_made")
        root_spread, root_copied = k.sem("root_spread"), k.sem("root_copied")
        hid_made, hid_scaled, hid_silu = k.sem("hid_made1"), k.sem("hid_scaled"), k.sem("hid_silu")
        out_made, out_copied, out_turned = k.sem("out_made1"), k.sem("out_copied1"), k.sem("out_turned1")
        norm = norm_sems(k, 1)
        SPAN = dict(per=2, first=-1, loop_from=3, loop_to=GROUPS // 2 - 1, last=GROUPS // 2 + 3)

        with nc.Block() as block:
            @block.tensor
            def _(pe):
                def hidden(it, c, chunk):
                    g = unit(it, 2, c - 1, GROUPS)
                    if g is None:
                        return
                    pe.wait_ge(agg_copied, g + 1)
                    wait(pe, hid_scaled, HC * g + chunk - 1)
                    pe.matmul(hid_ps[:, chunk % 2, :], k.w1[:, chunk, :], agg[:, (c - 1) % 2, :],
                              start=True, stop=True).then_inc(hid_made, 1)

                def output(it, c, chunk):
                    g = unit(it, 2, c - 2, GROUPS)
                    if g is None:
                        return
                    pe.wait_ge(hid_silu, HC * g + chunk + 1)
                    if chunk == 0:
                        wait(pe, out_copied, g)
                    mm = pe.matmul(out_ps[:, :], k.w2[:, chunk, :], hid[:, c % 2, chunk, :],
                                   start=(chunk == 0), stop=(chunk == HC - 1))
                    if chunk == HC - 1:
                        mm.then_inc(out_made, 1)

                def slot(it, c):
                    hidden(it, c, 0)
                    hidden(it, c, 1)
                    g = unit(it, 2, c, GROUPS)
                    if g is not None:
                        pe.wait_ge(x_copied, g + 1)
                        pe.wait_ge(diag_added, g + 1)
                        wait(pe, agg_copied, g)
                        for q in range(QUAD):
                            mm = pe.matmul(agg_ps[:, q * P:(q + 1) * P], xs[:, c % 2, q, :], adj[:, c % 2, q, :],
                                           start=True, stop=True)
                        mm.then_inc(agg_made, 1)
                    output(it, c, 0)
                    output(it, c, 1)
                    if g is not None:
                        pe.wait_ge(agg_copied, g + 1)
                        wait(pe, prod_made, g)
                        pe.matmul(gram_ps[:, :], k.gram[:, :], agg[:, c % 2, :], start=True, stop=True)\
                          .then_inc(gram_made, 1)
                    hidden(it, c, 2)
                    output(it, c, 2)
                    if g is not None:
                        pe.wait_ge(prod_made, g + 1)
                        wait(pe, root_copied, g)
                        for q in range(QUAD):
                            mm = pe.matmul(root_ps[:, q:q + 1], prod[:, q * P:(q + 1) * P], k.ones[:, :],
                                           start=True, stop=True)
                        mm.then_inc(squares_summed, 1)
                    hidden(it, c, 3)
                    output(it, c, 3)
                    if g is not None:
                        pe.wait_ge(root_made, g + 1)
                        for q in range(QUAD):
                            mm = pe.transpose(root_ps[:, q * P:(q + 1) * P], root[:, q:q + 1].to_broadcast([P, P]),
                                              k.eye[:, :])
                        mm.then_inc(root_spread, 1)
                    back = unit(it, 2, c - 3, GROUPS)
                    if back is not None:
                        pe.wait_ge(out_copied, back + 1)
                        wait(pe, norm["summed"], back)
                        for q in range(QUAD):
                            mm = pe.transpose(back_ps[:, q, :], out_t[:, q * P:(q + 1) * P], k.eye[:, :])
                        mm.then_inc(out_turned, 1)

                spread_loop(pe, slot, **SPAN)

            @block.scalar
            def _(act):
                def silu(it, c, chunk):
                    g = unit(it, 2, c - 1, GROUPS)
                    if g is None:
                        return
                    act.wait_ge(hid_scaled, HC * g + chunk + 1)
                    h = hid[:, (c - 1) % 2, chunk, :]
                    act.activation(h, h, ACT.Silu, scale=k.rmsw[:, chunk:chunk + 1]).then_inc(hid_silu, 1)

                def slot(it, c):
                    g = unit(it, 2, c - 3, GROUPS)
                    if g is not None:
                        act.wait_ge(out_made, g + 1)
                        wait(act, out_turned, g)
                        act.activation(out_t[:, :], out_ps[:, :], ACT.Identity, bias=k.b2[:, 0:1])\
                           .then_inc(out_copied, 1)
                    silu(it, c, 0)
                    g = unit(it, 2, c, GROUPS)
                    if g is not None:
                        act.wait_ge(agg_made, g + 1)
                        wait(act, hid_made, HC * (g - 1))
                        wait(act, prod_made, g - 1)
                        act.activation(agg[:, c % 2, :], agg_ps[:, :], ACT.Copy).then_inc(agg_copied, 1)
                    for chunk in range(1, HC):
                        silu(it, c, chunk)
                    if g is not None:
                        act.wait_ge(root_spread, g + 1)
                        wait(act, hid_scaled, HC * g)
                        act.activation(scale[:, :], root_ps[:, :], ACT.Copy).then_inc(root_copied, 1)

                spread_loop(act, slot, **SPAN)

            @block.vector
            def _(dve):
                def scaled(it, c, chunk):
                    g = unit(it, 2, c - 1, GROUPS)
                    if g is None:
                        return
                    dve.wait_ge(hid_made, HC * g + chunk + 1)
                    if chunk == 0:
                        dve.wait_ge(root_copied, g + 1)
                        wait(dve, out_made, g - 1)
                    dve.scalar_tensor_tensor(out=hid[:, (c - 1) % 2, chunk, :], in0=hid_ps[:, chunk % 2, :],
                                             scalar=k.b1[:, chunk:chunk + 1], in1=scale[:, :],
                                             op0=ALU.add, op1=ALU.mult).then_inc(hid_scaled, 1)

                def slot(it, c):
                    scaled(it, c, 0)
                    scaled(it, c, 1)
                    g = unit(it, 2, c - 4, GROUPS)
                    if g is not None:
                        norm_apply(dve, k, norm, y, g)
                    g = unit(it, 2, c, GROUPS)
                    if g is not None:
                        dve.wait_ge(gram_made, g + 1)
                        wait(dve, squares_summed, g)
                        dve.scalar_tensor_tensor(out=prod[:, :], in0=gram_ps[:, :], scalar=k.gram_bias[:, 0:1],
                                                 in1=agg[:, c % 2, :], op0=ALU.add, op1=ALU.mult)\
                           .then_inc(prod_made, 1)
                    n = unit(it, 2, c + 1, GROUPS)
                    if n is not None:
                        wait(dve, agg_made, n - 1)
                        dve.tensor_copy(xs[:, (c + 1) % 2], group_of(k.x, n)).then_inc(x_copied, 1)
                    scaled(it, c, 2)
                    if g is not None:
                        dve.wait_ge(squares_summed, g + 1)
                        wait(dve, root_made, g)
                        dve.tensor_scalar(root_in[:, :], root_ps[:, 0:QUAD], k.square_bias[:, 0:1], RMS_EPS,
                                          ALU.add, ALU.max).then_inc(root_asked, 1)
                    scaled(it, c, 3)
                    g = unit(it, 2, c - 3, GROUPS)
                    if g is not None:
                        dve.wait_ge(out_turned, g + 1)
                        wait(dve, norm["x_next"], g)
                        dve.tensor_tensor(y[:, :, :], back_ps[:, :, :], group_of(k.x, g), ALU.add)\
                           .then_inc(norm["summed"], 1)
                        norm_statistics(dve, k, norm, y, g)

                spread_loop(dve, slot, **SPAN)

            @block.gpsimd
            def _(pool):
                def slot(it, c):
                    n = unit(it, 2, c + 1, GROUPS)
                    if n is not None:
                        wait(pool, agg_made, n - 1)
                        pool.tensor_tensor(adj[:, (c + 1) % 2], group_of(k.adj_t, n),
                                           k.diag1[:, :].unsqueeze(1).to_broadcast([P, QUAD, P]), ALU.add)\
                            .then_inc(diag_added, 1)
                    g = unit(it, 2, c, GROUPS)
                    if g is not None:
                        pool.wait_ge(root_asked, g + 1)
                        wait(pool, root_spread, g)
                        pool.tensor_tensor(root[:, :], root_in[:, :], k.minus_half[:, :], ALU.pow)\
                            .then_inc(root_made, 1)
                    g = unit(it, 2, c - 3, GROUPS)
                    if g is not None:
                        norm_root(pool, k, norm, g)

                spread_loop(pool, slot, **SPAN)


def relu_mlp(k):
    nc, HC, GROUPS = k.nc, k.hid2, k.groups
    with ExitStack() as ctx:
        xs = k.sb("xs2", [P, 2, QUAD, P], ctx)
        adj = k.sb("adj2", [P, 2, QUAD, P], ctx)
        agg = k.sb("agg2", [P, 2, QUAD * P], ctx)
        hid = k.sb("hid2", [P, 2, HC, QUAD * P], ctx)
        out_t = k.sb("out_t2", [P, 2, QUAD * P], ctx)
        y = k.sb("y2", [P, QUAD, P], ctx)
        agg_ps = k.psum("agg_ps2", [P, QUAD * P], ctx)
        hid_ps = k.psum("hid_ps2", [P, HC, QUAD * P], ctx)
        out_ps = k.psum("out_ps2", [P, QUAD * P], ctx)
        back_ps = k.psum("back_ps2", [P, QUAD, P], ctx)
        x_copied, diag_added = k.sem("x_copied2"), k.sem("diag_added2")
        agg_made, agg_copied = k.sem("agg_made2"), k.sem("agg_copied2")
        hid_made, hid_relu = k.sem("hid_made2"), k.sem("hid_relu2")
        out_made, out_copied, out_turned = k.sem("out_made2"), k.sem("out_copied2"), k.sem("out_turned2")
        norm = norm_sems(k, 2)
        SPAN = dict(per=2, first=-1, loop_from=3, loop_to=GROUPS // 2 - 1, last=GROUPS // 2 + 3)

        with nc.Block() as block:
            @block.tensor
            def _(pe):
                def slot(it, c):
                    g = unit(it, 2, c, GROUPS)
                    if g is not None:
                        pe.wait_ge(x_copied, g + 1)
                        pe.wait_ge(diag_added, g + 1)
                        wait(pe, agg_copied, g)
                        for q in range(QUAD):
                            mm = pe.matmul(agg_ps[:, q * P:(q + 1) * P], xs[:, c % 2, q, :], adj[:, c % 2, q, :],
                                           start=True, stop=True)
                        mm.then_inc(agg_made, 1)
                    g = unit(it, 2, c - 1, GROUPS)
                    if g is not None:
                        pe.wait_ge(agg_copied, g + 1)
                        for chunk in range(HC):
                            wait(pe, hid_relu, HC * (g - 1) + chunk + 1)
                            pe.matmul(hid_ps[:, chunk, :], k.v1[:, chunk, :], agg[:, (c - 1) % 2, :],
                                      start=True, stop=True).then_inc(hid_made, 1)
                    g = unit(it, 2, c - 2, GROUPS)
                    if g is not None:
                        wait(pe, out_copied, g)
                        for chunk in range(HC):
                            pe.wait_ge(hid_relu, HC * g + chunk + 1)
                            mm = pe.matmul(out_ps[:, :], k.v2[:, chunk, :], hid[:, c % 2, chunk, :],
                                           start=(chunk == 0), stop=(chunk == HC - 1))
                        mm.then_inc(out_made, 1)
                    g = unit(it, 2, c - 3, GROUPS)
                    if g is not None:
                        pe.wait_ge(out_copied, g + 1)
                        wait(pe, norm["summed"], g)
                        for q in range(QUAD):
                            mm = pe.transpose(back_ps[:, q, :], out_t[:, (c - 3) % 2, q * P:(q + 1) * P], k.eye[:, :])
                        mm.then_inc(out_turned, 1)

                spread_loop(pe, slot, **SPAN)

            @block.scalar
            def _(act):
                def slot(it, c):
                    g = unit(it, 2, c - 3, GROUPS)
                    if g is not None:
                        act.wait_ge(out_made, g + 1)
                        wait(act, out_turned, g - 1)
                        act.activation(out_t[:, (c - 3) % 2, :], out_ps[:, :], ACT.Identity, bias=k.c2[:, 0:1])\
                           .then_inc(out_copied, 1)
                    g = unit(it, 2, c, GROUPS)
                    if g is not None:
                        act.wait_ge(agg_made, g + 1)
                        wait(act, hid_made, HC * (g - 1))
                        act.activation(agg[:, c % 2, :], agg_ps[:, :], ACT.Copy).then_inc(agg_copied, 1)
                    g = unit(it, 2, c - 1, GROUPS)
                    if g is not None:
                        wait(act, out_made, g - 1)
                        for chunk in range(HC):
                            act.wait_ge(hid_made, HC * g + chunk + 1)
                            act.activation(hid[:, (c - 1) % 2, chunk, :], hid_ps[:, chunk, :], ACT.Relu,
                                           bias=k.c1[:, chunk:chunk + 1]).then_inc(hid_relu, 1)

                spread_loop(act, slot, **SPAN)

            @block.vector
            def _(dve):
                def slot(it, c):
                    n = unit(it, 2, c + 1, GROUPS)
                    if n is not None:
                        wait(dve, agg_made, n - 1)
                        dve.tensor_copy(xs[:, (c + 1) % 2], group_of(k.x, n)).then_inc(x_copied, 1)
                    g = unit(it, 2, c - 5, GROUPS)
                    if g is not None:
                        norm_apply(dve, k, norm, y, g)
                    g = unit(it, 2, c - 4, GROUPS)
                    if g is not None:
                        dve.wait_ge(out_turned, g + 1)
                        wait(dve, norm["x_next"], g)
                        dve.tensor_tensor(y[:, :, :], back_ps[:, :, :], group_of(k.x, g), ALU.add)\
                           .then_inc(norm["summed"], 1)
                        norm_statistics(dve, k, norm, y, g)

                spread_loop(dve, slot, **SPAN)

            @block.gpsimd
            def _(pool):
                def slot(it, c):
                    n = unit(it, 2, c + 1, GROUPS)
                    if n is not None:
                        wait(pool, agg_made, n - 1)
                        pool.tensor_tensor(adj[:, (c + 1) % 2], group_of(k.adj_t, n),
                                           k.diag2[:, :].unsqueeze(1).to_broadcast([P, QUAD, P]), ALU.add)\
                            .then_inc(diag_added, 1)
                    g = unit(it, 2, c - 4, GROUPS)
                    if g is not None:
                        norm_root(pool, k, norm, g)

                spread_loop(pool, slot, **SPAN)


def gated_highway(k, out_dram):
    nc, GROUPS = k.nc, k.groups
    out_view = out_dram.rearrange("b n d -> n b d")
    with ExitStack() as ctx:
        quads = lambda name, ring: k.sb(name, [P, ring, QUAD, P], ctx)
        xs, x_t = quads("xs3", 2), quads("x_t3", 2)
        adj = quads("adj3", 2)
        feat = quads("feat", 2)
        het = quads("het", 2)
        gate = quads("gate", 2)
        mix, neg, elu, y = quads("mix", 2), quads("neg", 2), quads("elu", 1), quads("y3", 4)
        rstd, shift = k.sb("rstd3", [P, 2, QUAD], ctx), k.sb("shift3", [P, 2, QUAD], ctx)
        turn_ps = k.psum("turn_ps3", [P, QUAD, P], ctx)
        feat_ps = k.psum("feat_ps", [P, QUAD, P], ctx)
        pair_ps = k.psum("pair_ps", [P, 2, QUAD, 2, P], ctx)
        hom_ps = k.psum("hom_ps", [P, 2, QUAD, P], ctx)
        x_copied, x_turned, x_t_copied = k.sem("x_copied3"), k.sem("x_turned3"), k.sem("x_t_copied3")
        feat_made, feat_scaled, adj_copied = k.sem("feat_made"), k.sem("feat_scaled"), k.sem("adj_copied3")
        pair_made, het_copied, gate_tanh = k.sem("pair_made"), k.sem("het_copied"), k.sem("gate_tanh")
        hom_made, differ, gated, mixed = k.sem("hom_made"), k.sem("differ"), k.sem("gated"), k.sem("mixed3")
        neg_made, exp_made, elu_made = k.sem("neg_made"), k.sem("exp_made3"), k.sem("elu_made")
        stored = k.sem("stored")
        norm = norm_sems(k, 3)
        norm["shift"] = k.sem("shift_3")
        SPAN = dict(per=4, first=-1, loop_from=2, loop_to=GROUPS // 4 - 1, last=GROUPS // 4 + 2)

        with nc.Block() as block:
            @block.tensor
            def _(pe):
                def slot(it, c):
                    p = c % 2
                    g = unit(it, 4, c, GROUPS)
                    if g is not None:
                        pe.wait_ge(x_copied, g + 1)
                        wait(pe, x_t_copied, g)
                        for q in range(QUAD):
                            mm = pe.transpose(turn_ps[:, q, :], xs[:, p, q, :], k.eye[:, :])
                        mm.then_inc(x_turned, 1)
                    b = unit(it, 4, c - 1, GROUPS)
                    if b is not None:
                        pe.wait_ge(adj_copied, b + 1)
                        pe.wait_ge(feat_scaled, b + 1)
                        wait(pe, differ, b - 1)
                        for q in range(QUAD):
                            mm = pe.matmul(hom_ps[:, 1 - p, q, :], adj[:, 1 - p, q, :], feat[:, 1 - p, q, :],
                                           start=True, stop=True)
                        mm.then_inc(hom_made, 1)
                    if g is not None:
                        pe.wait_ge(x_t_copied, g + 1)
                        wait(pe, feat_scaled, g)
                        for q in range(QUAD):
                            mm = pe.matmul(feat_ps[:, q, :], x_t[:, p, q, :], k.theta[:, :], start=True, stop=True)
                        mm.then_inc(feat_made, 1)
                        wait(pe, gate_tanh, g - 1)
                        for q in range(QUAD):
                            pe.matmul(pair_ps[:, p, q], x_t[:, p, q, :], k.w_ht[:, :, :], start=True, stop=False)
                            mm = pe.matmul(pair_ps[:, p, q, 1, :], k.one_row[:, :], k.b_t[:, :],
                                           start=False, stop=True)
                        mm.then_inc(pair_made, 1)

                spread_loop(pe, slot, **SPAN)

            @block.scalar
            def _(act):
                def slot(it, c):
                    p = c % 2
                    g = unit(it, 4, c, GROUPS)
                    if g is not None:
                        act.wait_ge(x_turned, g + 1)
                        wait(act, pair_made, g - 1)
                        act.activation(x_t[:, p], turn_ps[:, :, :], ACT.Copy).then_inc(x_t_copied, 1)
                    b = unit(it, 4, c - 1, GROUPS)
                    if b is not None:
                        act.wait_ge(pair_made, b + 1)
                        wait(act, mixed, b - 1)
                        act.activation(het[:, 1 - p], pair_ps[:, 1 - p, :, 0, :], ACT.Copy).then_inc(het_copied, 1)
                        act.activation(gate[:, 1 - p], pair_ps[:, 1 - p, :, 1, :], ACT.Tanh, scale=0.5)\
                           .then_inc(gate_tanh, 1)
                    b = unit(it, 4, c - 2, GROUPS)
                    if b is not None:
                        act.wait_ge(mixed, b + 1)
                        wait(act, elu_made, b - 1)
                        act.activation(neg[:, p], mix[:, p], ACT.Relu, scale=-1.0).then_inc(neg_made, 1)
                    if b is not None:
                        act.wait_ge(neg_made, b + 1)
                        act.activation(neg[:, p], neg[:, p], ACT.Exp, scale=-1.0).then_inc(exp_made, 1)
                    b = unit(it, 4, c - 5, GROUPS)
                    if b is not None:
                        act.wait_ge(norm["shift"], b + 1)
                        for q in range(QUAD):
                            last = act.activation(
                                k.x[:, bass.ds(b * QUAD + q, 1), :].rearrange("p a d -> p (a d)"), y[:, (c + 3) % 4, q, :],
                                ACT.Identity, scale=rstd[:, 1 - p, q:q + 1], bias=shift[:, 1 - p, q:q + 1])
                        last.then_inc(norm["x_next"], 1)
                    n = unit(it, 4, c + 1, GROUPS)
                    if n is not None:
                        wait(act, x_turned, n - 1)
                        act.activation(xs[:, 1 - p], group_of(k.x, n), ACT.Copy).then_inc(x_copied, 1)

                spread_loop(act, slot, **SPAN)

            @block.vector
            def _(dve):
                def slot(it, c):
                    p = c % 2
                    d = unit(it, 4, c - 4, GROUPS)
                    if d is not None:
                        norm_statistics(dve, k, norm, y[:, c % 4], d)
                    a = unit(it, 4, c - 1, GROUPS)
                    if a is not None:
                        dve.wait_ge(hom_made, a + 1)
                        dve.wait_ge(het_copied, a + 1)
                        wait(dve, elu_made, a - 1)
                        for q in range(QUAD):
                            last = dve.scalar_tensor_tensor(
                                out=mix[:, 1 - p, q, :], in0=hom_ps[:, 1 - p, q, :],
                                scalar=k.root[:, bass.ds(a * QUAD + q, 1)], in1=het[:, 1 - p, q, :],
                                op0=ALU.mult, op1=ALU.subtract)
                        last.then_inc(differ, 1)
                    g = unit(it, 4, c, GROUPS)
                    if g is not None:
                        dve.wait_ge(feat_made, g + 1)
                        wait(dve, hom_made, g - 1)
                        dve.tensor_tensor(feat[:, p], feat_ps[:, :, :],
                                          k.root[:, bass.ds(g * QUAD, QUAD)].unsqueeze(2).to_broadcast([P, QUAD, P]),
                                          ALU.mult).then_inc(feat_scaled, 1)
                    if d is not None:
                        dve.wait_ge(norm["rstd"], d + 1)
                        wait(dve, norm["x_next"], d - 1)
                        dve.scalar_tensor_tensor(out=shift[:, p, :], in0=k.mv[:, :, 0], scalar=-1.0,
                                                 in1=rstd[:, p, :], op0=ALU.mult, op1=ALU.mult)\
                           .then_inc(norm["shift"], 1)
                    if a is not None:
                        dve.wait_ge(differ, a + 1)
                        dve.wait_ge(gate_tanh, a + 1)
                        dve.scalar_tensor_tensor(out=mix[:, 1 - p], in0=gate[:, 1 - p], scalar=1.0,
                                                 in1=mix[:, 1 - p], op0=ALU.add, op1=ALU.mult).then_inc(gated, 1)
                    b = unit(it, 4, c - 2, GROUPS)
                    if b is not None:
                        dve.wait_ge(exp_made, b + 1)
                        wait(dve, norm["summed"], b)
                        dve.scalar_tensor_tensor(out=elu[:, 0], in0=neg[:, p], scalar=1.0, in1=mix[:, p],
                                                 op0=ALU.subtract, op1=ALU.max).then_inc(elu_made, 1)
                    if a is not None:
                        dve.wait_ge(gated, a + 1)
                        dve.scalar_tensor_tensor(out=mix[:, 1 - p], in0=mix[:, 1 - p], scalar=0.5,
                                                 in1=het[:, 1 - p], op0=ALU.mult, op1=ALU.add).then_inc(mixed, 1)

                spread_loop(dve, slot, **SPAN)

            @block.gpsimd
            def _(pool):
                def slot(it, c):
                    p = c % 2
                    b = unit(it, 4, c - 4, GROUPS)
                    if b is not None:
                        pool.wait_ge(norm["var"], b + 1)
                        wait(pool, norm["x_next"], b - 1)
                        pool.tensor_tensor(rstd[:, p, :], k.var[:, :], k.minus_half[:, :], ALU.pow)\
                            .then_inc(norm["rstd"], 1)
                    n = unit(it, 4, c + 1, GROUPS)
                    if n is not None:
                        wait(pool, hom_made, n - 1)
                        pool.tensor_copy(adj[:, 1 - p], group_of(k.adj_t, n)).then_inc(adj_copied, 1)
                    b = unit(it, 4, c - 2, GROUPS)
                    if b is not None:
                        pool.wait_ge(elu_made, b + 1)
                        wait(pool, norm["x_next"], b - 3)
                        pool.tensor_tensor(y[:, (c + 2) % 4], elu[:, 0], group_of(k.x, b), ALU.add)\
                            .then_inc(norm["summed"], 1)

                spread_loop(pool, slot, **SPAN)

            @block.sync
            def _(sp):
                with sp.Fori(0, GROUPS) as g:
                    sp.wait_ge(norm["x_next"], g + 1)
                    sp.dma_start(group_of(out_view, g), group_of(k.x, g)).then_inc(stored, 16)
                sp.wait_ge(stored, 16 * GROUPS)


def four_layers(nc, w, out):
    with ExitStack() as ctx:
        k = Core(nc, ctx)
        k.graphs = w["x"].shape[0]
        k.groups = k.graphs // QUAD
        k.heads = w["L0_gnn_fc_w"].shape[1] // P
        k.hid1 = w["L1_gnn_W1"].shape[1] // P
        k.hid2 = w["L2_gnn_W1"].shape[1] // P
        H = k.heads
        k.x = k.sb("x_all", [P, k.graphs, P])
        k.adj_t = k.sb("adj_t_all", [P, k.graphs, P])
        k.degree, k.root = k.sb("degree", [P, k.graphs]), k.sb("degree_root", [P, k.graphs])
        k.eye = k.sb("eye_sb", [P, P])
        k.minus_half = k.sb("minus_half", [P, QUAD])
        k.bn, k.mv = k.sb("bn", [P, QUAD, 6]), k.sb("mv", [P, QUAD, 2])
        k.var, k.rstd = k.sb("var", [P, QUAD]), k.sb("rstd", [P, QUAD])
        k.always = k.sem("always")
        with ExitStack() as weights:
            k.fold = k.sb("fold", [P, H, P], weights)
            k.wqk = k.sb("wqk", [P, 2, H], weights)
            k.qk_bias = k.sb("qk_bias", [P, 2, H], weights)
            k.out_bias = k.sb("out_bias", [P, 1], weights)
            prepare_attention(k, w)
            attention(k, w["x"], w["adj"])
        k.ones = k.sb("ones", [P, 1])
        k.w1, k.b1, k.rmsw = k.sb("w1", [P, k.hid1, P]), k.sb("b1", [P, k.hid1]), k.sb("rmsw", [P, k.hid1])
        k.w2, k.b2 = k.sb("w2", [P, k.hid1, P]), k.sb("b2", [P, 1])
        k.gram, k.gram_bias = k.sb("gram", [P, P]), k.sb("gram_bias", [P, 1])
        k.square_bias = k.sb("square_bias", [P, 1])
        k.diag1, k.diag2 = k.sb("diag1", [P, P]), k.sb("diag2", [P, P])
        k.v1, k.c1 = k.sb("v1", [P, k.hid2, P]), k.sb("c1", [P, k.hid2])
        k.v2, k.c2 = k.sb("v2", [P, k.hid2, P]), k.sb("c2", [P, 1])
        k.w_ht, k.theta = k.sb("w_ht", [P, 2, P]), k.sb("theta", [P, P])
        k.b_t, k.one_row = k.sb("b_t", [1, P]), k.sb("one_row", [1, P])
        prepare_mlps(k, w)
        rms_mlp(k)
        relu_mlp(k)
        gated_highway(k, out)


_INS = ['x', 'adj', 'L0_gnn_fc_w', 'L0_gnn_fc_b', 'L0_gnn_q_w', 'L0_gnn_q_b', 'L0_gnn_k_w', 'L0_gnn_k_b',
        'L0_gnn_fp_w', 'L0_gnn_fp_b', 'L1_gnn_epsilon', 'L1_gnn_W1', 'L1_gnn_b1', 'L1_gnn_rms_weight', 'L1_gnn_W2',
        'L1_gnn_b2', 'L2_gnn_eps', 'L2_gnn_W1', 'L2_gnn_b1', 'L2_gnn_W2', 'L2_gnn_b2', 'L3_gnn_W_t', 'L3_gnn_b_t',
        'L3_gnn_W_h', 'L3_gnn_theta']

_BY_PARTITION = ['L0_gnn_fc_b', 'L0_gnn_fp_b', 'L1_gnn_b1', 'L1_gnn_rms_weight', 'L1_gnn_b2', 'L2_gnn_b1',
                 'L2_gnn_b2']


def kernel(**inputs):
    import numpy as _np
    import concourse.bacc as _bacc
    from concourse import mybir as _mybir
    from concourse.bass_utils import run_bass_kernel_spmd as _run

    nc = _bacc.Bacc("TRN2", target_bir_lowering=False, num_devices=1)
    arrays, args = {}, {}
    for name in _INS:
        a = _np.asarray(inputs[name])
        if name in _BY_PARTITION:
            a = a.reshape(-1, P).T
        a = _np.ascontiguousarray(a.reshape(1) if a.ndim == 0 else a)
        arrays[f"in_{name}"] = a
        args[name] = nc.dram_tensor(f"in_{name}", a.shape, _mybir.dt.from_np(a.dtype), kind="ExternalInput").ap()
    arrays["in_eye"] = _np.eye(P, dtype=_np.float32)
    args["eye"] = nc.dram_tensor("in_eye", (P, P), _mybir.dt.float32, kind="ExternalInput").ap()
    out = nc.dram_tensor("out_0", inputs["x"].shape, _mybir.dt.float32, kind="ExternalOutput").ap()
    four_layers(nc, args, out)
    r = _run(nc, [arrays], core_ids=[0])
    return r.results[0]["out_0"]
```

```python
from contextlib import ExitStack

import concourse.bass as bass
from concourse import mybir

F32 = mybir.dt.float32
F32R = mybir.dt.float32r
ALU = mybir.AluOpType
ACT = mybir.ActivationFunctionType
AX_X = mybir.AxisListType.X

P = 128
BANK = 512
QUAD = 4
NEG = 1.0e9
SLOPE = 0.01
LN_EPS = 1e-5
RMS_EPS = 1e-6
NORM_WORDS = 10 * QUAD
DEG_EPS = 1e-6


def unit(it, per, offset, count):
    n = it * per + offset
    if isinstance(n, int) and not 0 <= n < count:
        return None
    return n


def wait(eng, sem, count):
    if isinstance(count, int) and count <= 0:
        return
    eng.wait_ge(sem, count)


def cap(count, most):
    return min(count, most) if isinstance(count, int) else count


def run_layers(eng, layers):
    tail = []
    for slot, span in layers:
        head = [(it, c) for it in range(span["first"], span["loop_from"]) for c in range(span["per"])]
        done = 0
        for (it, c), after in zip(head, span["follows"] or [0] * len(head)):
            while done < len(tail) and done <= after:
                tail_slot, at = tail[done]
                tail_slot(*at)
                done += 1
            slot(it, c)
        for tail_slot, at in tail[done:]:
            tail_slot(*at)
        with eng.Fori(span["loop_from"], span["loop_to"]) as it:
            for c in range(span["per"]):
                slot(it, c)
        tail = [(slot, (it, c)) for it in range(span["loop_to"], span["last"]) for c in range(span["per"])]
    for tail_slot, at in tail:
        tail_slot(*at)


def after_last(eng, n, *signals):
    if isinstance(n, int) and n == 0:
        for sem, count in signals:
            eng.wait_ge(sem, count)


def wait_x(eng, k, norm, g):
    eng.wait_ge(norm["x_next"], g + 1 if isinstance(g, int) else k.groups)


class Region:

    def __init__(self, work, start, size, work_at=None):
        self.work, self.start, self.size, self.used, self.work_at = work, start, size, 0, work_at

    def again(self):
        return Region(self.work, self.start, self.size, self.work_at)

    def take(self, *shape):
        size = 1
        for n in shape:
            size *= n
        assert self.used + size <= self.size
        view = self.work[:, self.start + self.used:self.start + self.used + size]
        self.used += size
        names = "abcd"[:len(shape)]
        sizes = dict(zip(names[1:], shape[1:]))
        return view.rearrange(f"p ({' '.join(names)}) -> p {' '.join(names)}", **sizes) if len(shape) > 1 else view


class Core:

    def __init__(self, nc, ctx):
        self.nc, self.ctx = nc, ctx

    def sb(self, name, shape):
        return self.ctx.enter_context(self.nc.sbuf_tensor(name, shape, F32))

    def rounded_at(self, name, region, *shape):
        offset = region.work_at + 4 * (region.start + region.used)
        region.take(*shape)
        return self.nc.alloc_sbuf_tensor_at(name, [P, *shape], F32, offset=offset)

    def sem(self, name):
        return self.ctx.enter_context(self.nc.semaphore(name))

    def bank(self, first, *shape):
        return Region(self.psum, first * BANK, self.psum_words - first * BANK).take(*shape)


def start_loads(loads, loaded, queue):
    for dst, src in loads:
        queue.dma_start(dst, src).then_inc(loaded, 16)


def prepare_attention(k, w):
    H = k.heads
    space = k.mixed_b.again()
    fc, fc_t = space.take(H, P), space.take(H, P)
    fp = space.take(H, P + 2)
    fcb, qkw, qkb = space.take(H), space.take(2), space.take(2)
    fpb = space.take(1)
    eps1, eps2 = space.take(1), space.take(1)
    PER_BANK = BANK // (P + 2)
    banks = [(b, range(b * PER_BANK, min((b + 1) * PER_BANK, H))) for b in range(-(-H // PER_BANK))]
    turn_ps, fold_ps, small_ps, bias_ps = k.bank(2, H, P), k.bank(4, len(banks), BANK), k.bank(0, BANK), k.bank(6, BANK)
    loaded, small_loaded = k.sem("weights0_loaded"), k.sem("small_weights_loaded")
    later_loaded = k.sem("later_weights_loaded")
    turned, copied, spread = k.sem("fc_turned"), k.sem("fc_copied"), k.sem("qkw_spread")
    multiplied, bias_multiplied = k.sem("fc_multiplied"), k.sem("bias_multiplied")
    scalar_loads = [
        (qkw[:, 0:1], w["L0_gnn_q_w"]),
        (qkw[:, 1:2], w["L0_gnn_k_w"]),
        (fcb[:, :], w["L0_gnn_fc_b"]),
    ]
    later_loads = [
        (qkb[:, 0:1], w["L0_gnn_q_b"].partition_broadcast(P)),
        (qkb[:, 1:2], w["L0_gnn_k_b"].partition_broadcast(P)),
        (fpb[:, :], w["L0_gnn_fp_b"]),
        (eps1[:, :], w["L1_gnn_epsilon"].partition_broadcast(P)),
        (eps2[:, :], w["L2_gnn_eps"].partition_broadcast(P)),
        (k.b1[:, :], w["L1_gnn_b1"]),
        (k.rmsw[:, :], w["L1_gnn_rms_weight"]),
        (k.b2[:, :], w["L1_gnn_b2"]),
        (k.c1[:, :], w["L2_gnn_b1"]),
        (k.c2[:, :], w["L2_gnn_b2"]),
    ]
    SMALL_LOADED, LATER_LOADED = 16 * len(scalar_loads), 16 * len(later_loads)

    def sync(sp):
        start_loads([(fc[:, :, :], w["L0_gnn_fc_w"].rearrange("d (h e) -> d h e", h=H)),
                     (fp[:, :, 0:P], w["L0_gnn_fp_w"].rearrange("(h d) e -> d h e", h=H))], loaded, sp)

    def scalar(act):
        start_loads([(k.eye[:, :], w["eye"])], loaded, act)
        start_loads(scalar_loads, small_loaded, act)
        start_loads(later_loads, later_loaded, act)
        act.wait_ge(later_loaded, LATER_LOADED)

    def gpsimd(pool):
        pool.memset(k.minus_half[:, :], -0.5).then_inc(k.constants_set, 1)
        pool.memset(k.ones[:, :], 1.0 / (k.hid1 * P)).then_inc(k.constants_set, 1)
        pool.memset(k.norm_words[:, :], 0.0).then_inc(k.always, 1)
        pool.wait_ge(k.constants_set, 2)

    def tensor(pe):
        pe.wait_ge(loaded, 16 * 3)
        for h in range(H):
            mm = pe.transpose(turn_ps[:, h, :], fc[:, h, :], k.eye[:, :])
        mm.then_inc(turned, 1)
        pe.wait_ge(spread, 1)
        pe.wait_ge(small_loaded, SMALL_LOADED)
        for t in range(2):
            pe.matmul(small_ps[:, t * H:(t + 1) * H], qkw[:, t:t + 1].to_broadcast([P, P]), fcb[:, :],
                      start=True, stop=True)
        pe.wait_ge(copied, 1)
        for b, heads in banks:
            for i, h in enumerate(heads):
                mm = pe.matmul(fold_ps[:, b, i * (P + 2):(i + 1) * (P + 2)], fc_t[:, h, :], fp[:, h, :],
                               start=True, stop=True)
        mm.then_inc(multiplied, 1)

    def multiply_bias(pe):
        pe.wait_ge(later_loaded, LATER_LOADED)
        pe.wait_ge(k.folded, 2 + len(banks))
        for h in range(H):
            mm = pe.matmul(bias_ps[:, 0:1], fp[:, h, 0:P], fcb[:, h:h + 1], start=(h == 0), stop=(h == H - 1))
        mm.then_inc(bias_multiplied, 1)

    def vector(dve):
        dve.wait_ge(small_loaded, SMALL_LOADED)
        dve.wait_ge(loaded, 16 * 3)
        dve.tensor_copy(fp[:, :, P:P + 2], qkw[:, :].unsqueeze(1).to_broadcast([P, H, 2])).then_inc(spread, 1)
        dve.wait_ge(turned, 1)
        dve.tensor_copy(fc_t[:, :, :], turn_ps[:, :, :]).then_inc(copied, 1)
        dve.wait_ge(later_loaded, LATER_LOADED)
        dve.tensor_scalar(k.diag1[:, :], k.eye[:, :], eps1[:, 0:1], None, ALU.mult).then_inc(k.folded, 1)
        dve.tensor_scalar(k.scale2[:, :], eps2[:, :], 1.0, None, ALU.add).then_inc(k.folded, 1)
        dve.wait_ge(multiplied, 1)
        for b, heads in banks:
            view = fold_ps[:, b, 0:len(heads) * (P + 2)].rearrange("p (h e) -> p h e", h=len(heads))
            dve.tensor_copy(k.wqk[:, :, heads[0]:heads[-1] + 1].rearrange("p t h -> p h t"), view[:, :, P:P + 2])\
               .then_inc(k.qk_folded, 1)
        dve.tensor_tensor(k.qk_bias[:, :, :], small_ps[:, 0:2 * H].rearrange("d (t h) -> d t h", t=2),
                          qkb[:, :].unsqueeze(2).to_broadcast([P, 2, H]), ALU.add).then_inc(k.qk_folded, 1)
        for b, heads in banks:
            view = fold_ps[:, b, 0:len(heads) * (P + 2)].rearrange("p (h e) -> p h e", h=len(heads))
            dve.tensor_copy(k.fold[:, heads[0]:heads[-1] + 1, :], view[:, :, 0:P]).then_inc(k.folded, 1)
        dve.wait_ge(k.qk_folded, k.QK_FOLDED)

    def add_bias(dve):
        dve.wait_ge(bias_multiplied, 1)
        dve.tensor_tensor(k.out_bias[:, :], bias_ps[:, 0:1], fpb[:, :], ALU.add).then_inc(k.folded, 1)

    k.QK_FOLDED, k.FOLDED = 1 + len(banks), 3 + len(banks)
    return dict(sync=sync, scalar=scalar, gpsimd=gpsimd, tensor=tensor, vector=vector,
                multiply_bias=multiply_bias, add_bias=add_bias)


def prepare_mlps(k, w, before):
    HC = k.hid1
    w1_t = k.x_t_space.again().take(HC, P)
    turn_ps, gram_ps = k.bank(1, HC, P), k.bank(2, BANK)
    w1_loaded, w2_loaded = k.sem("w1_loaded"), k.sem("w2_loaded")
    turned, copied, multiplied = k.sem("w1_turned"), k.sem("w1_copied"), k.sem("w1_multiplied")
    w2_loads = [
        (k.w2[:, :, :], w["L1_gnn_W2"].rearrange("(c h) d -> h c d", c=HC)),
        (k.v1[:, :, :], w["L2_gnn_W1"].rearrange("d (c h) -> d c h", c=k.hid2)),
        (k.v2[:, :, :], w["L2_gnn_W2"].rearrange("(c h) d -> h c d", c=k.hid2)),
    ]
    gate_loads = [
        (k.w_ht[:, 0, :], w["L3_gnn_W_h"]),
        (k.w_ht[:, 1, :], w["L3_gnn_W_t"]),
        (k.b_t[0:1, :], w["L3_gnn_b_t"].unsqueeze(0)),
        (k.theta[:, :], w["L3_gnn_theta"]),
    ]
    k.GATE_LOADED = 16 * len(gate_loads)

    def sync(sp):
        sp.wait_ge(before["x_turned"], k.groups)
        start_loads([(k.w1[:, :, :], w["L1_gnn_W1"].rearrange("d (c h) -> d c h", c=HC))], w1_loaded, sp)
        sp.wait_ge(before["query_added"], k.graphs)
        start_loads(w2_loads, w2_loaded, sp)
        sp.wait_ge(before["mix_made"], k.graphs)
        start_loads(gate_loads, k.gate_loaded, sp)

    def set_row(pool):
        pool.wait_ge(before["mix_made"], k.graphs)
        pool.memset(k.one_row[0:1, :], 1.0).then_inc(k.row_set, 1)

    def turn(pe):
        pe.wait_ge(w1_loaded, 16)
        pe.wait_ge(before["scores_made"], k.graphs)
        for c in range(HC):
            mm = pe.transpose(turn_ps[:, c, :], k.w1[:, c, :], k.eye[:, :])
        mm.then_inc(turned, 1)

    def multiply(pe):
        pe.wait_ge(copied, 1)
        pe.wait_ge(before["probs_copied"], k.graphs)
        for c in range(HC):
            pe.matmul(gram_ps[:, 0:P], w1_t[:, c, :], w1_t[:, c, :], start=(c == 0), stop=(c == HC - 1))
        for c in range(HC):
            pe.matmul(gram_ps[:, P:P + 1], w1_t[:, c, :], k.b1[:, c:c + 1], start=(c == 0),
                      stop=(c == HC - 1))
        for c in range(HC):
            mm = pe.matmul(gram_ps[:, P + 1:P + 2], k.b1[:, c:c + 1].to_broadcast([P, P]),
                           k.b1[:, c:c + 1], start=(c == 0), stop=(c == HC - 1))
        mm.then_inc(multiplied, 1)

    def copy_turned(dve):
        dve.wait_ge(turned, 1)
        dve.wait_ge(before["qk_made"], k.groups)
        dve.wait_ge(before["mix_made"], k.graphs)
        dve.tensor_copy(w1_t[:, :, :], turn_ps[:, :, :]).then_inc(copied, 1)
        dve.tensor_scalar(k.diag2[:, :], k.eye[:, :], k.scale2[:, 0:1], None, ALU.mult)\
           .then_inc(k.diag2_made, 1)

    def copy_gram(dve):
        dve.wait_ge(multiplied, 1)
        dve.tensor_copy(k.gram[:, :], gram_ps[:, 0:P]).then_inc(k.gram_ready, 1)
        dve.tensor_scalar(k.gram_bias[:, :], gram_ps[:, P:P + 1], 2.0, None, ALU.mult).then_inc(k.gram_ready, 1)
        dve.tensor_scalar(k.square_bias[:, :], gram_ps[:, P + 1:P + 2], 1.0 / (HC * P), RMS_EPS,
                          ALU.mult, ALU.add).then_inc(k.gram_ready, 1)
        dve.wait_ge(k.gram_ready, 3)

    def split(dve):
        dve.wait_ge(before["out_made"], k.groups)
        dve.tensor_copy(rounded(k.w1_hi[:, :, :]), k.w1[:, :, :]).then_inc(k.hi_made, 1)
        dve.wait_ge(k.hi_made, 1)
        dve.tensor_tensor(rounded(k.w1_lo[:, :, :]), k.w1[:, :, :], k.w1_hi[:, :, :], ALU.subtract)\
           .then_inc(k.split_made, 1)
        dve.wait_ge(k.split_made, 1)
        dve.wait_ge(w2_loaded, 16 * len(w2_loads))
        dve.tensor_copy(rounded(k.v1_hi[:, :, :]), k.v1[:, :, :]).then_inc(k.hi_made, 1)
        dve.wait_ge(k.hi_made, 2)
        dve.tensor_tensor(rounded(k.v1_lo[:, :, :]), k.v1[:, :, :], k.v1_hi[:, :, :], ALU.subtract)\
           .then_inc(k.split_made, 1)

    return dict(sync=sync, set_row=set_row, turn=turn, multiply=multiply, copy_turned=copy_turned,
                copy_gram=copy_gram, split=split, w2_loaded=w2_loaded, W2_LOADED=16 * len(w2_loads))


def norm_of(k, layer):
    start = layer * NORM_WORDS
    part = lambda first, size: k.norm_words[:, start + first:start + first + size]
    return dict(
        bn=part(0, 6 * QUAD).rearrange("p (q s) -> p q s", q=QUAD),
        mv=part(6 * QUAD, 2 * QUAD).rearrange("p (q s) -> p q s", q=QUAD),
        var=part(8 * QUAD, QUAD), rstd=part(9 * QUAD, QUAD),
        **{n: k.sem(f"{n}_{layer}") for n in ("summed", "stats", "moments", "var_made", "rstd_made", "x_next")})


def norm_statistics(dve, k, norm, y, g):
    dve.wait_ge(norm["summed"], g + 1)
    for q in range(QUAD):
        last = dve.bn_stats(norm["bn"][:, q, :], y[:, q, :])
    last.then_inc(norm["stats"], 1)
    dve.wait_ge(k.always, 1)
    dve.wait_ge(norm["stats"], g + 1)
    for q in range(QUAD):
        last = dve.bn_aggr(norm["mv"][:, q, :], norm["bn"][:, q, :])
    last.then_inc(norm["moments"], 1)
    dve.wait_ge(norm["moments"], g + 1)
    wait(dve, norm["rstd_made"], g)
    dve.tensor_scalar(norm["var"][:, :], norm["mv"][:, :, 1], LN_EPS, None, ALU.add).then_inc(norm["var_made"], 1)


def norm_root(pool, k, norm, g):
    pool.wait_ge(norm["var_made"], g + 1)
    wait(pool, norm["x_next"], g)
    pool.tensor_tensor(norm["rstd"][:, :], norm["var"][:, :], k.minus_half[:, :], ALU.pow)\
        .then_inc(norm["rstd_made"], 1)


def norm_apply(dve, k, norm, y, g):
    dve.wait_ge(norm["rstd_made"], g + 1)
    for q in range(QUAD):
        last = dve.tensor_scalar(k.x[:, bass.ds(g * QUAD + q, 1), :].rearrange("p a d -> p (a d)"), y[:, q, :],
                                 norm["mv"][:, q, 0:1], norm["rstd"][:, q:q + 1], ALU.subtract, ALU.mult)
    last.then_inc(norm["x_next"], 1)


def rounded(t):
    return t.bitcast(F32R)


def split_matmul(pe, out, left_hi, left_lo, right_hi, right_lo):
    pe.matmul(out, rounded(left_hi), rounded(right_hi), start=True, stop=False)
    pe.matmul(out, rounded(left_hi), rounded(right_lo), start=False, stop=False)
    return pe.matmul(out, rounded(left_lo), rounded(right_hi), start=False, stop=True)


def group_of(t, g):
    return t[:, bass.ds(g * QUAD, QUAD), :]


def attention(k, x_dram, adj_dram, prepare):
    H, GROUPS, GRAPHS = k.heads, k.groups, k.graphs
    x_view = x_dram.rearrange("b n d -> n b d")
    adj_view = adj_dram.rearrange("b n m -> n b m")
    xin = k.xin_space.take(QUAD, P)
    ain = k.ain_space.take(2, QUAD, P)
    val = k.val_space.take(2, QUAD, P)
    x_t = k.x_t_space.take(QUAD, P)
    score = k.score_space.take(4, H, P)
    probs_t = k.probs_space.take(2, H, P)
    mixed = k.mixed_space.take(2, H, QUAD * P)\
             .rearrange("p r h (q n) -> p r h q n", q=QUAD)
    out_t, y = k.out_space.take(QUAD, P), k.out_space.take(QUAD, P)
    qk = k.qk_space.take(2, QUAD, 2 * H).rearrange("p r q (t h) -> p r q t h", t=2)
    neg_max, total, recip = k.qk_space.take(2, H), k.qk_space.take(2, H), k.qk_space.take(2, H)
    key_ps, turn_ps, mix_ps = k.bank(0, H, P), k.bank(2, H, P), k.bank(4, H, P)
    out_ps = k.bank(6, QUAD, P)
    misc_ps, quad_ps = k.bank(7, BANK), k.bank(7, QUAD, P)
    adj_loaded = [k.sem(f"adj_loaded{i}") for i in range(2)]
    val_loaded = [k.sem(f"val_loaded{i}") for i in range(2)]
    x_loaded, all_x_loaded = k.sem("x_loaded"), k.sem("all_x_loaded")
    adj_turned, adj_copied = k.sem("adj_turned"), k.sem("adj_copied")
    x_turned, x_copied = k.sem("x_turned"), k.sem("x_copied")
    qk_made, qk_copied, mask_made = k.sem("qk_made"), k.sem("qk_copied"), k.sem("mask_made")
    degree_summed = k.sem("degree_summed")
    keys_spread, query_added = k.sem("keys_spread"), k.sem("query_added")
    scores_made, scores_leaky = k.sem("scores_made"), k.sem("scores_leaky")
    max_found, exp_made, recip_made = k.sem("max_found"), k.sem("exp_made"), k.sem("recip_made")
    probs_made, probs_turned, probs_copied = k.sem("probs_made"), k.sem("probs_turned"), k.sem("probs_copied")
    mix_made, mix_copied = k.sem("mix_made"), k.sem("mix_copied")
    out_made, out_copied, out_turned = k.sem("out_made"), k.sem("out_copied"), k.sem("out_turned")
    feats_added, tanh_made, sigmoid_made = k.sem("feats_added"), k.sem("tanh_made"), k.sem("sigmoid_made")
    degree_added = k.sem("degree_added")
    norm = norm_of(k, 0)
    PER = 2 * QUAD
    span = dict(per=PER, first=-1, loop_from=2, loop_to=GRAPHS // PER - 1, last=GRAPHS // PER + 2,
                           follows=None)

    def sync(sp):
        def load(it, j):
            g = unit(it, 2, j, GROUPS)
            wait(sp, query_added, QUAD * (g - 1))
            sp.dma_start(ain[:, j], group_of(adj_view, g)).then_inc(adj_loaded[j], 16)
            wait(sp, x_turned, g)
            sp.dma_start(xin[:, :, :], group_of(x_view, g)).then_inc(x_loaded, 16)
            wait(sp, mix_made, QUAD * (g - 1))
            sp.dma_start(val[:, j], group_of(x_view, g)).then_inc(val_loaded[j], 16)

        for j in range(2):
            load(0, j)
        for part in range(4):
            n = GRAPHS // 4
            sp.dma_start(k.x[:, part * n:(part + 1) * n, :],
                         x_view[:, part * n:(part + 1) * n, :]).then_inc(all_x_loaded, 16)
        for j in range(2):
            load(1, j)
        with sp.Fori(2, GROUPS // 2) as it:
            for j in range(2):
                load(it, j)

    def tensor(pe):
        def slot(it, c):
            if isinstance(it, int) and (it, c) == (0, 1):
                prepare["multiply_bias"](pe)
            b = unit(it, PER, c - 2, GRAPHS)
            if b is not None:
                pe.wait_ge(probs_made, b + 1)
                wait(pe, probs_copied, b)
                for h in range(H):
                    mm = pe.transpose(turn_ps[:, h, :], score[:, (c - 2) % 4, h, :], k.eye[:, :])
                mm.then_inc(probs_turned, 1)
            g = unit(it, 2, c // QUAD + 1, GROUPS)
            j = (c // QUAD + 1) % 2
            if c % QUAD == 0 and g is not None:
                pe.wait_ge(adj_loaded[j], 16 * (it + (c // QUAD + 1) // 2 + 1))
                wait(pe, feats_added, g - 3)
                for q in range(QUAD):
                    mm = pe.transpose(quad_ps[:, q, :], ain[:, j, q, :], k.eye[:, :])
                mm.then_inc(adj_turned, 1)
            if c % QUAD == 1 and g is not None:
                pe.wait_ge(x_loaded, 16 * (g + 1))
                pe.wait_ge(adj_copied, g + 1)
                for q in range(QUAD):
                    mm = pe.transpose(quad_ps[:, q, :], xin[:, q, :], k.eye[:, :])
                mm.then_inc(x_turned, 1)
            if c % QUAD == 2 and g is not None:
                pe.wait_ge(x_copied, g + 1)
                after_last(pe, g, (k.qk_folded, k.QK_FOLDED))
                for q in range(QUAD):
                    mm = pe.matmul(misc_ps[:, 2 * H * q:2 * H * (q + 1)], x_t[:, q, :],
                                   k.wqk[:, :, :].rearrange("d t h -> d (t h)"), start=True, stop=True)
                mm.then_inc(qk_made, 1)
            g = unit(it, 2, (c - 11) // QUAD, GROUPS)
            if c % QUAD == 3 and g is not None:
                pe.wait_ge(out_copied, g + 1)
                pe.wait_ge(qk_copied, cap(g + 4, GROUPS))
                for q in range(QUAD):
                    mm = pe.transpose(quad_ps[:, q, :], out_t[:, q, :], k.eye[:, :])
                mm.then_inc(out_turned, 1)
            g = unit(it, 2, (c - 7) // QUAD, GROUPS)
            part = (c - 7) % QUAD
            if g is not None:
                if part == 0:
                    after_last(pe, g, (k.folded, k.FOLDED))
                    pe.wait_ge(mix_copied, QUAD * (g + 1))
                    wait(pe, out_copied, g)
                for h in range(part * H // QUAD, (part + 1) * H // QUAD):
                    mm = pe.matmul(out_ps[:, :, :], k.fold[:, h, :], mixed[:, ((c - 7) // QUAD) % 2, h, :, :],
                                   start=(h == 0), stop=(h == H - 1))
                if part == QUAD - 1:
                    mm.then_inc(out_made, 1)
            b = unit(it, PER, c + 1, GRAPHS)
            if b is not None:
                pe.wait_ge(qk_copied, unit(it, 2, (c + 1) // QUAD, GROUPS) + 1)
                wait(pe, scores_made, b)
                for h in range(H):
                    mm = pe.transpose(key_ps[:, h, :],
                                      qk[:, ((c + 1) // QUAD) % 2, (c + 1) % QUAD, 1, h:h + 1].to_broadcast([P, P]),
                                      k.eye[:, :])
                mm.then_inc(keys_spread, 1)
            b = unit(it, PER, c - 2, GRAPHS)
            if b is not None:
                j = ((c - 2) // QUAD) % 2
                pe.wait_ge(val_loaded[j], 16 * (it + (c - 2) // QUAD // 2 + 1))
                pe.wait_ge(probs_copied, b + 1)
                wait(pe, mix_copied, b)
                for half in range(2):
                    hs = slice(half * H // 2, (half + 1) * H // 2)
                    mm = pe.matmul(mix_ps[:, hs, :], val[:, j, (c - 2) % QUAD, :], probs_t[:, c % 2, hs, :],
                                   start=True, stop=True)
                mm.then_inc(mix_made, 1)

        return slot

    def scalar(act):
        def slot(it, c):
            b = unit(it, PER, c - 2, GRAPHS)
            if b is not None:
                act.wait_ge(probs_turned, b + 1)
                wait(act, mix_made, b - 1)
                act.activation(probs_t[:, c % 2], turn_ps[:, :, :], ACT.Copy).then_inc(probs_copied, 1)
            b = unit(it, PER, c - 3, GRAPHS)
            if b is not None:
                act.wait_ge(mix_made, b + 1)
                if (c - 3) % QUAD == 0:
                    wait(act, out_made, unit(it, 2, (c - 3) // QUAD, GROUPS) - 1)
                act.activation(mixed[:, ((c - 3) // QUAD) % 2, :, (c - 3) % QUAD, :], mix_ps[:, :, :],
                               ACT.Copy).then_inc(mix_copied, 1)
            g = unit(it, 2, c // QUAD + 1, GROUPS)
            if c % QUAD == 0 and g is not None:
                act.wait_ge(adj_turned, g + 1)
                act.activation(group_of(k.adj_t, g), quad_ps, ACT.Copy).then_inc(adj_copied, 1)
            if c % QUAD == 1 and g is not None:
                act.wait_ge(x_turned, g + 1)
                wait(act, qk_made, g)
                act.activation(x_t[:, :, :], quad_ps, ACT.Copy).then_inc(x_copied, 1)
            g = unit(it, 2, (c - 12) // QUAD, GROUPS)
            if c % QUAD == 0 and g is not None:
                act.wait_ge(feats_added, g + 1)
                act.activation(y[:, :, :], y[:, :, :], ACT.Tanh, scale=0.5).then_inc(tanh_made, 1)
            g = unit(it, 2, (c - 10) // QUAD, GROUPS)
            if c % QUAD == 2 and g is not None:
                act.wait_ge(out_made, g + 1)
                after_last(act, g, (k.folded, k.FOLDED))
                wait(act, out_turned, g)
                act.activation(out_t[:, :, :], out_ps[:, :, :], ACT.Identity,
                               bias=k.out_bias[:, 0:1]).then_inc(out_copied, 1)
            b = unit(it, PER, c, GRAPHS)
            if b is not None:
                act.wait_ge(max_found, b + 1)
                wait(act, recip_made, b - 1)
                for h in range(H):
                    e = act.activation(score[:, c % 4, h, :], score[:, c % 4, h, :], ACT.Exp,
                                       bias=neg_max[:, c % 2, h:h + 1], accum_out=total[:, c % 2, h:h + 1])
                e.then_inc(exp_made, 1)

        return slot

    def vector(dve):
        def slot(it, c):
            if isinstance(it, int) and it * PER + c == GRAPHS:
                dve.wait_ge(degree_summed, GROUPS)
                dve.tensor_scalar(k.degree[:, :], k.degree[:, :], DEG_EPS, None, ALU.add).then_inc(degree_added, 1)
            if isinstance(it, int) and (it, c) == (0, 2):
                prepare["add_bias"](dve)
            b = unit(it, PER, c, GRAPHS)
            if b is not None:
                dve.wait_ge(keys_spread, b + 1)
                dve.wait_ge(query_added, b + 1)
                dve.tensor_tensor(score[:, c % 4], key_ps[:, :, :], score[:, c % 4], ALU.add)\
                   .then_inc(scores_made, 1)
                dve.wait_ge(scores_made, b + 1)
                dve.scalar_tensor_tensor(out=score[:, c % 4], in0=score[:, c % 4], scalar=SLOPE,
                                         in1=score[:, c % 4], op0=ALU.mult, op1=ALU.max)\
                   .then_inc(scores_leaky, 1)
            before = unit(it, PER, c - 1, GRAPHS)
            if before is not None:
                dve.wait_ge(exp_made, before + 1)
                wait(dve, probs_made, before - 1)
                dve.reciprocal(recip[:, (c - 1) % 2, :], total[:, (c - 1) % 2, :]).then_inc(recip_made, 1)
            if b is not None:
                dve.wait_ge(scores_leaky, b + 1)
                wait(dve, exp_made, b - 1)
                dve.tensor_reduce(neg_max[:, c % 2, :], score[:, c % 4], AX_X, ALU.max, negate=True)\
                   .then_inc(max_found, 1)
            g = unit(it, 2, c // QUAD + 1, GROUPS)
            j = (c // QUAD + 1) % 2
            if c % QUAD == 0 and g is not None:
                dve.wait_ge(adj_loaded[j], 16 * (it + (c // QUAD + 1) // 2 + 1))
                dve.tensor_reduce(k.degree[:, bass.ds(g * QUAD, QUAD)], ain[:, j], AX_X, ALU.add)\
                   .then_inc(degree_summed, 1)
                dve.wait_ge(degree_summed, g + 1)
                dve.wait_ge(adj_turned, g + 1)
                dve.tensor_scalar(ain[:, j], ain[:, j], 1.0, NEG, ALU.subtract, ALU.mult)\
                   .then_inc(mask_made, 1)
            if c % QUAD == 2 and g is not None:
                dve.wait_ge(qk_made, g + 1)
                dve.tensor_tensor(qk[:, j].rearrange("p q t h -> p q (t h)"),
                                  misc_ps[:, 0:2 * H * QUAD].rearrange("p (q m) -> p q m", q=QUAD),
                                  k.qk_bias[:, :, :].rearrange("p t h -> p (t h)").unsqueeze(1)
                                  .to_broadcast([P, QUAD, 2 * H]), ALU.add).then_inc(qk_copied, 1)
            g = unit(it, 2, (c - 11) // QUAD, GROUPS)
            if c % QUAD == 3 and g is not None:
                dve.wait_ge(out_turned, g + 1)
                dve.wait_ge(all_x_loaded, 64)
                wait(dve, norm["x_next"], g)
                dve.tensor_tensor(y[:, :, :], quad_ps, group_of(k.x, g), ALU.add).then_inc(feats_added, 1)
            g = unit(it, 2, (c - 13) // QUAD, GROUPS)
            if c % QUAD == 1 and g is not None:
                dve.wait_ge(tanh_made, g + 1)
                dve.tensor_scalar(y[:, :, :], y[:, :, :], 0.5, 0.5, ALU.mult, ALU.add)\
                   .then_inc(sigmoid_made, 1)
                dve.wait_ge(sigmoid_made, g + 1)
                dve.tensor_tensor(y[:, :, :], y[:, :, :], group_of(k.x, g), ALU.add)\
                   .then_inc(norm["summed"], 1)
                norm_statistics(dve, k, norm, y, g)
            g = unit(it, 2, (c - 14) // QUAD, GROUPS)
            if c % QUAD == 2 and g is not None:
                norm_apply(dve, k, norm, y, g)

        return slot

    def gpsimd(pool):
        def slot(it, c):
            b = unit(it, PER, c + 1, GRAPHS)
            if b is not None:
                g = unit(it, 2, (c + 1) // QUAD, GROUPS)
                j = ((c + 1) // QUAD) % 2
                pool.wait_ge(mask_made, g + 1)
                pool.wait_ge(qk_copied, g + 1)
                wait(pool, probs_turned, b - 3)
                pool.tensor_tensor(score[:, (c + 1) % 4],
                                   ain[:, j, (c + 1) % QUAD, :].unsqueeze(1).to_broadcast([P, H, P]),
                                   qk[:, j, (c + 1) % QUAD, 0, :].unsqueeze(2).to_broadcast([P, H, P]),
                                   ALU.add).then_inc(query_added, 1)
            g = unit(it, 2, (c - 14) // QUAD, GROUPS)
            if c % QUAD == 2 and g is not None:
                norm_root(pool, k, norm, g)
            b = unit(it, PER, c - 1, GRAPHS)
            if b is not None:
                pool.wait_ge(recip_made, b + 1)
                pool.tensor_tensor(score[:, (c - 1) % 4], score[:, (c - 1) % 4],
                                   recip[:, (c - 1) % 2, :].unsqueeze(2).to_broadcast([P, H, P]),
                                   ALU.mult).then_inc(probs_made, 1)

        return slot
    return dict(
        sync=sync, tensor=tensor, scalar=scalar, vector=vector, gpsimd=gpsimd, span=span, norm=norm, x_turned=x_turned,
        query_added=query_added, mix_made=mix_made, degree_added=degree_added, scores_made=scores_made,
        probs_copied=probs_copied, qk_made=qk_made, mix_copied=mix_copied, out_copied=out_copied,
        out_made=out_made, adj_copied=adj_copied)


def rms_mlp(k, before, prepare):
    HC, GROUPS = k.hid1, k.groups
    first = k.mixed_a.again()
    xs = first.take(2, QUAD, P)
    adj = first.take(2, QUAD, P)
    k.xs, k.adj = xs, adj
    agg = first.take(2, QUAD * P)
    prod = first.take(QUAD * P)
    agg_hi = k.rounded_at("agg_hi1", k.split1_space, 2, QUAD * P)
    agg_lo = k.rounded_at("agg_lo1", k.split1_space, 2, QUAD * P)
    scale = first.take(QUAD * P)
    hid = k.mixed_b.again().take(2, HC, QUAD * P)
    out_t = k.probs_space.again().take(QUAD * P)
    y = k.y1_space.take(QUAD, P)
    root_in, root = k.small_space.take(QUAD), k.small_space.take(QUAD)
    agg_ps, gram_ps, root_ps = k.bank(0, QUAD * P), k.bank(1, QUAD * P), k.bank(2, QUAD * P)
    hid_ps, out_ps, back_ps = k.bank(3, 2, QUAD * P), k.bank(5, QUAD * P), k.bank(6, QUAD, P)
    degree_rooted = k.sem("degree_rooted")
    agg_rounded, agg_split = k.sem("agg_rounded1"), k.sem("agg_split1")
    x_copied, diag_added = k.sem("x_copied1"), k.sem("diag_added1")
    agg_made, agg_copied = k.sem("agg_made1"), k.sem("agg_copied1")
    gram_made, prod_made = k.sem("gram_made"), k.sem("prod_made")
    squares_summed, root_asked, root_made = k.sem("squares_summed"), k.sem("root_asked"), k.sem("root_made")
    root_spread, root_copied = k.sem("root_spread"), k.sem("root_copied")
    hid_made, hid_scaled, hid_silu = k.sem("hid_made1"), k.sem("hid_scaled"), k.sem("hid_silu")
    out_made, out_copied, out_turned = k.sem("out_made1"), k.sem("out_copied1"), k.sem("out_turned1")
    norm = norm_of(k, 1)
    span = dict(per=2, first=-1, loop_from=3, loop_to=GROUPS // 2 - 1, last=GROUPS // 2 + 3,
                           follows=[10, 11, 13, 15, 17, 19, 21, 23])

    def tensor(pe):
        def hidden(it, c, chunk):
            g = unit(it, 2, c - 1, GROUPS)
            if g is None:
                return
            pe.wait_ge(agg_split, g + 1)
            after_last(pe, g, (k.split_made, 1))
            after_last(pe, g, (before["probs_copied"], k.graphs), (before["mix_copied"], k.graphs))
            wait(pe, hid_scaled, HC * g + chunk - 1)
            split_matmul(pe, hid_ps[:, chunk % 2, :], k.w1_hi[:, chunk, :], k.w1_lo[:, chunk, :],
                         agg_hi[:, (c - 1) % 2, :], agg_lo[:, (c - 1) % 2, :]).then_inc(hid_made, 1)

        def output(it, c, chunk):
            g = unit(it, 2, c - 2, GROUPS)
            if g is None:
                return
            pe.wait_ge(hid_silu, HC * g + chunk + 1)
            if chunk == 0:
                after_last(pe, g, (prepare["w2_loaded"], prepare["W2_LOADED"]))
                wait(pe, out_copied, g)
            mm = pe.matmul(out_ps[:, :], k.w2[:, chunk, :], hid[:, c % 2, chunk, :],
                           start=(chunk == 0), stop=(chunk == HC - 1))
            if chunk == HC - 1:
                mm.then_inc(out_made, 1)

        def slot(it, c):
            if isinstance(it, int) and (it, c) == (-1, 0):
                prepare["turn"](pe)
            if isinstance(it, int) and (it, c) == (-1, 1):
                prepare["multiply"](pe)
            hidden(it, c, 0)
            hidden(it, c, 1)
            g = unit(it, 2, c, GROUPS)
            if g is not None:
                pe.wait_ge(x_copied, g + 1)
                pe.wait_ge(diag_added, g + 1)
                after_last(pe, g, (before["scores_made"], k.graphs))
                wait(pe, agg_copied, g)
                for q in range(QUAD):
                    mm = pe.matmul(agg_ps[:, q * P:(q + 1) * P], xs[:, c % 2, q, :], adj[:, c % 2, q, :],
                                   start=True, stop=True)
                mm.then_inc(agg_made, 1)
            output(it, c, 0)
            output(it, c, 1)
            if g is not None:
                pe.wait_ge(agg_copied, g + 1)
                after_last(pe, g, (k.gram_ready, 3))
                wait(pe, prod_made, g)
                pe.matmul(gram_ps[:, :], k.gram[:, :], agg[:, c % 2, :], start=True, stop=True)\
                  .then_inc(gram_made, 1)
            hidden(it, c, 2)
            output(it, c, 2)
            if g is not None:
                pe.wait_ge(prod_made, g + 1)
                wait(pe, root_copied, g)
                for q in range(QUAD):
                    mm = pe.matmul(root_ps[:, q:q + 1], prod[:, q * P:(q + 1) * P], k.ones[:, :],
                                   start=True, stop=True)
                mm.then_inc(squares_summed, 1)
            hidden(it, c, 3)
            output(it, c, 3)
            if g is not None:
                pe.wait_ge(root_made, g + 1)
                for q in range(QUAD):
                    mm = pe.transpose(root_ps[:, q * P:(q + 1) * P], root[:, q:q + 1].to_broadcast([P, P]),
                                      k.eye[:, :])
                mm.then_inc(root_spread, 1)
            back = unit(it, 2, c - 3, GROUPS)
            if back is not None:
                pe.wait_ge(out_copied, back + 1)
                after_last(pe, back, (before["out_copied"], GROUPS))
                wait(pe, norm["summed"], back)
                for q in range(QUAD):
                    mm = pe.transpose(back_ps[:, q, :], out_t[:, q * P:(q + 1) * P], k.eye[:, :])
                mm.then_inc(out_turned, 1)

        return slot

    def scalar(act):
        def silu(it, c, chunk):
            g = unit(it, 2, c - 1, GROUPS)
            if g is None:
                return
            act.wait_ge(hid_scaled, HC * g + chunk + 1)
            h = hid[:, (c - 1) % 2, chunk, :]
            act.activation(h, h, ACT.Silu, scale=k.rmsw[:, chunk:chunk + 1]).then_inc(hid_silu, 1)

        def slot(it, c):
            g = unit(it, 2, c - 3, GROUPS)
            if g is not None:
                act.wait_ge(out_made, g + 1)
                after_last(act, g, (before["mix_made"], k.graphs))
                wait(act, out_turned, g)
                act.activation(out_t[:, :], out_ps[:, :], ACT.Identity, bias=k.b2[:, 0:1])\
                   .then_inc(out_copied, 1)
            g = unit(it, 2, c, GROUPS)
            if g is not None:
                act.wait_ge(agg_made, g + 1)
                after_last(act, g, (before["out_made"], GROUPS - 1))
                wait(act, agg_split, g - 1)
                wait(act, prod_made, g - 1)
                act.activation(agg[:, c % 2, :], agg_ps[:, :], ACT.Copy).then_inc(agg_copied, 1)
            for chunk in range(HC):
                silu(it, c, chunk)
            if g is not None:
                act.wait_ge(root_spread, g + 1)
                wait(act, hid_scaled, HC * g)
                act.activation(scale[:, :], root_ps[:, :], ACT.Copy).then_inc(root_copied, 1)

        return slot

    def vector(dve):
        def scaled(it, c, chunk):
            g = unit(it, 2, c - 1, GROUPS)
            if g is None:
                return
            dve.wait_ge(hid_made, HC * g + chunk + 1)
            if chunk == 0:
                dve.wait_ge(root_copied, g + 1)
                after_last(dve, g, (before["out_made"], GROUPS))
                wait(dve, out_made, g - 1)
            dve.scalar_tensor_tensor(out=hid[:, (c - 1) % 2, chunk, :], in0=hid_ps[:, chunk % 2, :],
                                     scalar=k.b1[:, chunk:chunk + 1], in1=scale[:, :],
                                     op0=ALU.add, op1=ALU.mult).then_inc(hid_scaled, 1)

        def slot(it, c):
            if isinstance(it, int) and (it, c) == (-1, 0):
                prepare["copy_turned"](dve)
            if isinstance(it, int) and (it, c) == (0, 0):
                prepare["copy_gram"](dve)
            if isinstance(it, int) and (it, c) == (0, 1):
                prepare["split"](dve)
            scaled(it, c, 0)
            scaled(it, c, 1)
            g = unit(it, 2, c, GROUPS)
            if g is not None:
                dve.wait_ge(gram_made, g + 1)
                wait(dve, squares_summed, g)
                dve.scalar_tensor_tensor(out=prod[:, :], in0=gram_ps[:, :], scalar=k.gram_bias[:, 0:1],
                                         in1=agg[:, c % 2, :], op0=ALU.add, op1=ALU.mult)\
                   .then_inc(prod_made, 1)
                dve.wait_ge(agg_copied, g + 1)
                after_last(dve, g, (before["probs_copied"], k.graphs))
                wait(dve, hid_made, HC * (g - 1))
                wait(dve, agg_split, g - 1)
                dve.tensor_copy(rounded(agg_hi[:, c % 2, :]), agg[:, c % 2, :]).then_inc(agg_rounded, 1)
            n = unit(it, 2, c + 1, GROUPS)
            if n is not None:
                wait_x(dve, k, before["norm"], n)
                after_last(dve, n, (before["out_made"], GROUPS - 1))
                wait(dve, agg_made, n - 1)
                dve.tensor_copy(xs[:, (c + 1) % 2], group_of(k.x, n)).then_inc(x_copied, 1)
            scaled(it, c, 2)
            if g is not None:
                dve.wait_ge(squares_summed, g + 1)
                wait(dve, root_made, g)
                dve.tensor_scalar(root_in[:, :], root_ps[:, 0:QUAD], k.square_bias[:, 0:1], RMS_EPS,
                                  ALU.add, ALU.max).then_inc(root_asked, 1)
            scaled(it, c, 3)
            g = unit(it, 2, c - 4, GROUPS)
            if g is not None:
                norm_apply(dve, k, norm, y, g)
            g = unit(it, 2, c - 3, GROUPS)
            if g is not None:
                dve.wait_ge(out_turned, g + 1)
                after_last(dve, g, (before["mix_made"], k.graphs))
                wait(dve, norm["x_next"], g)
                dve.tensor_tensor(y[:, :, :], back_ps[:, :, :], group_of(k.x, g), ALU.add)\
                   .then_inc(norm["summed"], 1)
                norm_statistics(dve, k, norm, y, g)

        return slot

    def gpsimd(pool):
        def slot(it, c):
            if isinstance(it, int) and (it, c) == (-1, 0):
                prepare["set_row"](pool)
            n = unit(it, 2, c + 1, GROUPS)
            if n is not None:
                after_last(pool, n, (before["out_made"], GROUPS - 1), (before["adj_copied"], GROUPS),
                           (k.folded, k.FOLDED))
                wait(pool, agg_made, n - 1)
                pool.tensor_tensor(adj[:, (c + 1) % 2], group_of(k.adj_t, n),
                                   k.diag1[:, :].unsqueeze(1).to_broadcast([P, QUAD, P]), ALU.add)\
                    .then_inc(diag_added, 1)
            g = unit(it, 2, c, GROUPS)
            if g is not None:
                pool.wait_ge(agg_rounded, g + 1)
                wait(pool, hid_made, HC * (g - 1))
                pool.tensor_tensor(rounded(agg_lo[:, c % 2, :]), agg[:, c % 2, :], agg_hi[:, c % 2, :],
                                   ALU.subtract).then_inc(agg_split, 1)
                pool.wait_ge(root_asked, g + 1)
                wait(pool, root_spread, g)
                pool.tensor_tensor(root[:, :], root_in[:, :], k.minus_half[:, :], ALU.pow)\
                    .then_inc(root_made, 1)
                after_last(pool, g, (before["degree_added"], 1))
                pool.tensor_tensor(k.root[:, bass.ds(g * QUAD, QUAD)], k.degree[:, bass.ds(g * QUAD, QUAD)],
                                   k.minus_half[:, :], ALU.pow).then_inc(degree_rooted, 1)
            g = unit(it, 2, c - 3, GROUPS)
            if g is not None:
                norm_root(pool, k, norm, g)

        return slot
    return dict(
        tensor=tensor, scalar=scalar, vector=vector, gpsimd=gpsimd, span=span, norm=norm, agg_made=agg_made,
        agg_copied=agg_copied, prod_made=prod_made, root_copied=root_copied, hid_scaled=hid_scaled,
        out_made=out_made, out_copied=out_copied, out_turned=out_turned, degree_rooted=degree_rooted,
        hid_made=hid_made, squares_summed=squares_summed)


def relu_mlp(k, before):
    HC, GROUPS = k.hid2, k.groups
    xs, adj = k.xs, k.adj
    space = k.score_space.again()
    agg_hi = k.rounded_at("agg_hi2", space, 2, QUAD * P)
    agg_lo = k.rounded_at("agg_lo2", k.out_space.again(), 2, QUAD * P)
    hid, out_t = space.take(2, HC, QUAD * P), space.take(2, QUAD * P)
    agg_split = k.sem("agg_split2")
    y = k.y2_space.take(2, QUAD, P)
    agg_ps = [k.bank(0, QUAD * P), k.bank(5, QUAD * P)]
    hid_ps, out_ps = k.bank(1, HC, QUAD * P), k.bank(3, QUAD * P)
    back_ps = k.bank(7, QUAD, P)
    x_copied, diag_added = k.sem("x_copied2"), k.sem("diag_added2")
    agg_made, agg_copied = k.sem("agg_made2"), k.sem("agg_copied2")
    hid_made, hid_relu = k.sem("hid_made2"), k.sem("hid_relu2")
    out_made, out_copied, out_turned = k.sem("out_made2"), k.sem("out_copied2"), k.sem("out_turned2")
    norm = norm_of(k, 2)
    span = dict(per=2, first=-1, loop_from=3, loop_to=GROUPS // 2 - 1, last=GROUPS // 2 + 3,
                           follows=[2, 2, 3, 4, 5, 6, 7, 7])

    def tensor(pe):
        def slot(it, c):
            g = unit(it, 2, c, GROUPS)
            if g is not None:
                pe.wait_ge(x_copied, g + 1)
                pe.wait_ge(diag_added, g + 1)
                after_last(pe, g, (before["agg_copied"], GROUPS))
                if isinstance(g, int) and g == 1:
                    pe.wait_ge(before["out_copied"], GROUPS)
                wait(pe, agg_split, g - 1)
                for q in range(QUAD):
                    mm = pe.matmul(agg_ps[c % 2][:, q * P:(q + 1) * P], xs[:, c % 2, q, :], adj[:, c % 2, q, :],
                                   start=True, stop=True)
                mm.then_inc(agg_made, 1)
            g = unit(it, 2, c - 1, GROUPS)
            if g is not None:
                pe.wait_ge(agg_split, g + 1)
                after_last(pe, g, (k.split_made, 2))
                after_last(pe, g, (before["prod_made"], GROUPS), (before["root_copied"], GROUPS))
                for chunk in range(HC):
                    wait(pe, hid_relu, HC * (g - 1) + chunk + 1)
                    split_matmul(pe, hid_ps[:, chunk, :], k.v1_hi[:, chunk, :], k.v1_lo[:, chunk, :],
                                 agg_hi[:, (c - 1) % 2, :], agg_lo[:, (c - 1) % 2, :]).then_inc(hid_made, 1)
            g = unit(it, 2, c - 2, GROUPS)
            if g is not None:
                after_last(pe, g, (before["hid_scaled"], k.hid1 * GROUPS))
                wait(pe, out_copied, g)
                for chunk in range(HC):
                    pe.wait_ge(hid_relu, HC * g + chunk + 1)
                    mm = pe.matmul(out_ps[:, :], k.v2[:, chunk, :], hid[:, c % 2, chunk, :],
                                   start=(chunk == 0), stop=(chunk == HC - 1))
                mm.then_inc(out_made, 1)
            g = unit(it, 2, c - 3, GROUPS)
            if g is not None:
                pe.wait_ge(out_copied, g + 1)
                wait(pe, norm["summed"], g)
                for q in range(QUAD):
                    mm = pe.transpose(back_ps[:, q, :], out_t[:, (c - 3) % 2, q * P:(q + 1) * P], k.eye[:, :])
                mm.then_inc(out_turned, 1)

        return slot

    def scalar(act):
        def slot(it, c):
            g = unit(it, 2, c - 3, GROUPS)
            if g is not None:
                act.wait_ge(out_made, g + 1)
                wait(act, out_turned, g - 1)
                act.activation(out_t[:, (c - 3) % 2, :], out_ps[:, :], ACT.Identity, bias=k.c2[:, 0:1])\
                   .then_inc(out_copied, 1)
            g = unit(it, 2, c, GROUPS)
            if g is not None:
                act.wait_ge(agg_made, g + 1)
                wait(act, hid_made, HC * (g - 1))
                act.activation(rounded(agg_hi[:, c % 2, :]), agg_ps[c % 2][:, :], ACT.Copy).then_inc(agg_copied, 1)
            g = unit(it, 2, c - 1, GROUPS)
            if g is not None:
                after_last(act, g, (before["hid_made"], k.hid1 * GROUPS))
                wait(act, out_made, g - 1)
                for chunk in range(HC):
                    act.wait_ge(hid_made, HC * g + chunk + 1)
                    act.activation(hid[:, (c - 1) % 2, chunk, :], hid_ps[:, chunk, :], ACT.Relu,
                                   bias=k.c1[:, chunk:chunk + 1]).then_inc(hid_relu, 1)

        return slot

    def vector(dve):
        def slot(it, c):
            b = unit(it, 2, c - 4, GROUPS)
            if b is not None:
                dve.wait_ge(out_turned, b + 1)
                wait(dve, norm["x_next"], b - 1)
                dve.tensor_tensor(y[:, c % 2], back_ps[:, :, :], group_of(k.x, b), ALU.add)\
                   .then_inc(norm["summed"], 1)
                norm_statistics(dve, k, norm, y[:, c % 2], b)
            g = unit(it, 2, c, GROUPS)
            if g is not None:
                dve.wait_ge(agg_copied, g + 1)
                wait(dve, hid_made, HC * (g - 1))
                dve.tensor_tensor(rounded(agg_lo[:, c % 2, :]), agg_ps[c % 2][:, :], agg_hi[:, c % 2, :], ALU.subtract)\
                   .then_inc(agg_split, 1)
            n = unit(it, 2, c + 1, GROUPS)
            if n is not None:
                wait_x(dve, k, before["norm"], n)
                after_last(dve, n, (before["agg_made"], GROUPS))
                wait(dve, agg_made, n - 1)
                dve.tensor_copy(xs[:, (c + 1) % 2], group_of(k.x, n)).then_inc(x_copied, 1)
            if b is not None:
                norm_apply(dve, k, norm, y[:, c % 2], b)

        return slot

    def gpsimd(pool):
        def slot(it, c):
            n = unit(it, 2, c + 1, GROUPS)
            if n is not None:
                after_last(pool, n, (before["agg_made"], GROUPS), (k.diag2_made, 1))
                wait(pool, agg_made, n - 1)
                pool.tensor_tensor(adj[:, (c + 1) % 2], group_of(k.adj_t, n),
                                   k.diag2[:, :].unsqueeze(1).to_broadcast([P, QUAD, P]), ALU.add)\
                    .then_inc(diag_added, 1)
            g = unit(it, 2, c - 4, GROUPS)
            if g is not None:
                norm_root(pool, k, norm, g)

        return slot
    return dict(
        tensor=tensor, scalar=scalar, vector=vector, gpsimd=gpsimd, span=span, norm=norm, agg_made=agg_made,
        agg_copied=agg_copied, agg_split=agg_split, hid_made=hid_made, hid_relu=hid_relu, out_copied=out_copied)


def gated_highway(k, out_dram, before, layer1):
    GROUPS = k.groups
    out_view = out_dram.rearrange("b n d -> n b d")
    xs, adj = k.xs, k.adj
    space = k.mixed_b.again()
    x_t = space.take(2, QUAD, P)
    feat = space.take(2, QUAD, P)
    het = space.take(2, QUAD, P)
    gate = space.take(2, QUAD, P)
    mix, neg = k.probs_space.again().take(2, QUAD, P), k.out_space.again().take(2, QUAD, P)
    elu, y = k.elu_space.take(QUAD, P), k.y3_space.take(4, QUAD, P)
    rstd, shift = k.small_space.take(2, QUAD), k.small_space.take(2, QUAD)
    turn_ps, feat_ps = k.bank(6, QUAD, P), k.bank(5, QUAD, P)
    pair_ps = k.bank(1, 2, QUAD, 2 * P).rearrange("p r q (t d) -> p r q t d", t=2)
    hom_ps = [k.bank(0, QUAD, P), k.bank(7, QUAD, P)]
    x_copied, x_turned, x_t_copied = k.sem("x_copied3"), k.sem("x_turned3"), k.sem("x_t_copied3")
    feat_made, feat_scaled, adj_copied = k.sem("feat_made"), k.sem("feat_scaled"), k.sem("adj_copied3")
    pair_made, het_copied, gate_tanh = k.sem("pair_made"), k.sem("het_copied"), k.sem("gate_tanh")
    hom_made, differ, gated, mixed = k.sem("hom_made"), k.sem("differ"), k.sem("gated"), k.sem("mixed3")
    neg_made, exp_made, elu_made = k.sem("neg_made"), k.sem("exp_made3"), k.sem("elu_made")
    stored = k.sem("stored")
    norm = norm_of(k, 3)
    norm["shift_made"] = k.sem("shift_3")
    span = dict(per=4, first=-1, loop_from=2, loop_to=GROUPS // 4 - 1, last=GROUPS // 4 + 2,
                           follows=[2, 2, 2, 2, 3, 4, 5, 6, 7, 7, 7, 7])

    def tensor(pe):
        def slot(it, c):
            p = c % 2
            g = unit(it, 4, c, GROUPS)
            if g is not None:
                pe.wait_ge(x_copied, g + 1)
                after_last(pe, g, (layer1["norm"]["summed"], GROUPS))
                wait(pe, x_t_copied, g)
                for q in range(QUAD):
                    mm = pe.transpose(turn_ps[:, q, :], xs[:, p, q, :], k.eye[:, :])
                mm.then_inc(x_turned, 1)
            b = unit(it, 4, c - 1, GROUPS)
            if b is not None:
                pe.wait_ge(adj_copied, b + 1)
                pe.wait_ge(feat_scaled, b + 1)
                after_last(pe, b, (before["agg_split"], GROUPS))
                if isinstance(b, int) and b == 1:
                    pe.wait_ge(before["norm"]["summed"], GROUPS)
                wait(pe, differ, b - 1)
                for q in range(QUAD):
                    mm = pe.matmul(hom_ps[1 - p][:, q, :], adj[:, 1 - p, q, :], feat[:, 1 - p, q, :],
                                   start=True, stop=True)
                mm.then_inc(hom_made, 1)
            if g is not None:
                pe.wait_ge(x_t_copied, g + 1)
                after_last(pe, g, (before["agg_split"], GROUPS), (k.gate_loaded, k.GATE_LOADED), (k.row_set, 1))
                wait(pe, feat_scaled, g)
                for q in range(QUAD):
                    mm = pe.matmul(feat_ps[:, q, :], x_t[:, p, q, :], k.theta[:, :], start=True, stop=True)
                mm.then_inc(feat_made, 1)
                after_last(pe, g, (before["hid_relu"], k.hid2 * GROUPS))
                if isinstance(g, int) and g == 1:
                    pe.wait_ge(before["out_copied"], GROUPS)
                wait(pe, gate_tanh, g - 1)
                for q in range(QUAD):
                    pe.matmul(pair_ps[:, p, q], x_t[:, p, q, :], k.w_ht[:, :, :], start=True, stop=False)
                    mm = pe.matmul(pair_ps[:, p, q, 1, :], k.one_row[0:1, :], k.b_t[0:1, :],
                                   start=False, stop=True)
                mm.then_inc(pair_made, 1)

        return slot

    def scalar(act):
        def slot(it, c):
            p = c % 2
            g = unit(it, 4, c, GROUPS)
            if g is not None:
                act.wait_ge(x_turned, g + 1)
                after_last(act, g, (layer1["out_made"], GROUPS))
                wait(act, pair_made, g - 1)
                act.activation(x_t[:, p], turn_ps[:, :, :], ACT.Copy).then_inc(x_t_copied, 1)
            b = unit(it, 4, c - 1, GROUPS)
            if b is not None:
                act.wait_ge(pair_made, b + 1)
                wait(act, mixed, b - 1)
                act.activation(het[:, 1 - p], pair_ps[:, 1 - p, :, 0, :], ACT.Copy).then_inc(het_copied, 1)
                act.activation(gate[:, 1 - p], pair_ps[:, 1 - p, :, 1, :], ACT.Tanh, scale=0.5)\
                   .then_inc(gate_tanh, 1)
            b = unit(it, 4, c - 2, GROUPS)
            if b is not None:
                act.wait_ge(mixed, b + 1)
                after_last(act, b, (before["hid_made"], k.hid2 * GROUPS))
                wait(act, elu_made, b - 1)
                act.activation(neg[:, p], mix[:, p], ACT.Relu, scale=-1.0).then_inc(neg_made, 1)
            n = unit(it, 4, c + 1, GROUPS)
            if n is not None:
                wait_x(act, k, before["norm"], n)
                after_last(act, n, (before["agg_made"], GROUPS))
                wait(act, x_turned, n - 1)
                act.activation(xs[:, 1 - p], group_of(k.x, n), ACT.Copy).then_inc(x_copied, 1)
            if b is not None:
                act.wait_ge(neg_made, b + 1)
                act.activation(neg[:, p], neg[:, p], ACT.Exp, scale=-1.0).then_inc(exp_made, 1)
            b = unit(it, 4, c - 5, GROUPS)
            if b is not None:
                act.wait_ge(norm["shift_made"], b + 1)
                for q in range(QUAD):
                    last = act.activation(
                        k.x[:, bass.ds(b * QUAD + q, 1), :].rearrange("p a d -> p (a d)"), y[:, (c + 3) % 4, q, :],
                        ACT.Identity, scale=rstd[:, 1 - p, q:q + 1], bias=shift[:, 1 - p, q:q + 1])
                last.then_inc(norm["x_next"], 1)

        return slot

    def vector(dve):
        def slot(it, c):
            p = c % 2
            d = unit(it, 4, c - 4, GROUPS)
            if d is not None:
                norm_statistics(dve, k, norm, y[:, c % 4], d)
            a = unit(it, 4, c - 1, GROUPS)
            if a is not None:
                dve.wait_ge(hom_made, a + 1)
                dve.wait_ge(het_copied, a + 1)
                wait(dve, elu_made, a - 1)
                for q in range(QUAD):
                    last = dve.scalar_tensor_tensor(
                        out=mix[:, 1 - p, q, :], in0=hom_ps[1 - p][:, q, :],
                        scalar=k.root[:, bass.ds(a * QUAD + q, 1)], in1=het[:, 1 - p, q, :],
                        op0=ALU.mult, op1=ALU.subtract)
                last.then_inc(differ, 1)
            g = unit(it, 4, c, GROUPS)
            if g is not None:
                dve.wait_ge(feat_made, g + 1)
                after_last(dve, g, (layer1["out_made"], GROUPS), (layer1["degree_rooted"], GROUPS))
                wait(dve, hom_made, g - 1)
                dve.tensor_tensor(feat[:, p], feat_ps[:, :, :],
                                  k.root[:, bass.ds(g * QUAD, QUAD)].unsqueeze(2).to_broadcast([P, QUAD, P]),
                                  ALU.mult).then_inc(feat_scaled, 1)
            if d is not None:
                dve.wait_ge(norm["rstd_made"], d + 1)
                wait(dve, norm["x_next"], d - 1)
                dve.scalar_tensor_tensor(out=shift[:, p, :], in0=norm["mv"][:, :, 0], scalar=-1.0,
                                         in1=rstd[:, p, :], op0=ALU.mult, op1=ALU.mult)\
                   .then_inc(norm["shift_made"], 1)
            if a is not None:
                dve.wait_ge(differ, a + 1)
                dve.wait_ge(gate_tanh, a + 1)
                dve.scalar_tensor_tensor(out=mix[:, 1 - p], in0=gate[:, 1 - p], scalar=1.0,
                                         in1=mix[:, 1 - p], op0=ALU.add, op1=ALU.mult).then_inc(gated, 1)
            b = unit(it, 4, c - 2, GROUPS)
            if b is not None:
                after_last(dve, b, (before["norm"]["x_next"], GROUPS))
                dve.wait_ge(exp_made, b + 1)
                wait(dve, norm["summed"], b)
                dve.scalar_tensor_tensor(out=elu[:, :, :], in0=neg[:, p], scalar=1.0, in1=mix[:, p],
                                         op0=ALU.subtract, op1=ALU.max).then_inc(elu_made, 1)
            if a is not None:
                dve.wait_ge(gated, a + 1)
                dve.scalar_tensor_tensor(out=mix[:, 1 - p], in0=mix[:, 1 - p], scalar=0.5,
                                         in1=het[:, 1 - p], op0=ALU.mult, op1=ALU.add).then_inc(mixed, 1)

        return slot

    def gpsimd(pool):
        def slot(it, c):
            p = c % 2
            b = unit(it, 4, c - 4, GROUPS)
            if b is not None:
                pool.wait_ge(norm["var_made"], b + 1)
                wait(pool, norm["x_next"], b - 1)
                pool.tensor_tensor(rstd[:, p, :], norm["var"][:, :], k.minus_half[:, :], ALU.pow)\
                    .then_inc(norm["rstd_made"], 1)
            n = unit(it, 4, c + 1, GROUPS)
            if n is not None:
                after_last(pool, n, (before["agg_made"], GROUPS))
                wait(pool, hom_made, n - 1)
                pool.tensor_copy(adj[:, 1 - p], group_of(k.adj_t, n)).then_inc(adj_copied, 1)
            b = unit(it, 4, c - 2, GROUPS)
            if b is not None:
                pool.wait_ge(elu_made, b + 1)
                wait(pool, norm["x_next"], b - 3)
                pool.tensor_tensor(y[:, (c + 2) % 4], elu[:, :, :], group_of(k.x, b), ALU.add)\
                    .then_inc(norm["summed"], 1)

        return slot

    def sync(sp):
        with sp.Fori(0, GROUPS) as g:
            sp.wait_ge(norm["x_next"], g + 1)
            sp.dma_start(group_of(out_view, g), group_of(k.x, g)).then_inc(stored, 16)
        sp.wait_ge(stored, 16 * GROUPS)
    return dict(sync=sync, tensor=tensor, scalar=scalar, vector=vector, gpsimd=gpsimd, span=span)


def lay_out(k):
    H = k.heads
    k.x = k.sb("x_all", [P, k.graphs, P])
    k.adj_t = k.sb("adj_t_all", [P, k.graphs, P])
    k.degree, k.root = k.sb("degree", [P, k.graphs]), k.sb("degree_root", [P, k.graphs])
    k.eye, k.diag1 = k.sb("eye_sb", [P, P]), k.sb("diag1", [P, P])
    k.minus_half, k.norm_words = k.sb("minus_half", [P, QUAD]), k.sb("norm_words", [P, 4 * NORM_WORDS])
    fold_at = -(-k.nc.sbuf_base // 32) * 32
    k.fold_space = Region(k.sb("fold", [P, H * P]), 0, H * P, fold_at)
    assert k.nc.sbuf_base == fold_at + 4 * H * P
    k.fold = k.fold_space.take(H, P)
    k.wqk, k.qk_bias = k.sb("wqk", [P, 2, H]), k.sb("qk_bias", [P, 2, H])
    k.out_bias = k.sb("out_bias", [P, 1])
    k.ones = k.sb("ones", [P, 1])
    k.b1, k.rmsw, k.b2 = k.sb("b1", [P, k.hid1]), k.sb("rmsw", [P, k.hid1]), k.sb("b2", [P, 1])
    k.c1, k.c2, k.scale2 = k.sb("c1", [P, k.hid2]), k.sb("c2", [P, 1]), k.sb("scale2", [P, 1])
    k.gram_bias, k.square_bias = k.sb("gram_bias", [P, 1]), k.sb("square_bias", [P, 1])

    sizes = dict(mixed=2 * H * QUAD * P, score=4 * H * P, probs=2 * H * P, ain=2 * QUAD * P, val=2 * QUAD * P,
                 xin=QUAD * P, x_t=QUAD * P, out=2 * QUAD * P, qk=4 * QUAD * H + 6 * H)
    work_at = -(-k.nc.sbuf_base // 32) * 32
    work, start, spaces = k.sb("work", [P, sum(sizes.values())]), 0, {}
    assert k.nc.sbuf_base == work_at + 4 * sum(sizes.values())
    for name, size in sizes.items():
        spaces[name] = Region(work, start, size, work_at)
        start += size
    k.mixed_space, k.score_space, k.probs_space = spaces["mixed"], spaces["score"], spaces["probs"]
    k.ain_space, k.val_space, k.xin_space = spaces["ain"], spaces["val"], spaces["xin"]
    k.x_t_space, k.out_space, k.qk_space = spaces["x_t"], spaces["out"], spaces["qk"]
    half = sizes["mixed"] // 2
    k.split1_space = Region(work, k.score_space.start + 2 * QUAD * P, k.hid2 * 2 * QUAD * P, work_at)
    k.mixed_a, k.mixed_b = Region(work, 0, half), Region(work, half, half)
    k.y3_space = Region(work, half // 2, half // 2)
    probs, row = k.probs_space.start, QUAD * P
    k.y1_space, k.y2_space = Region(work, probs + row, row), Region(work, probs + 2 * row, 2 * row)
    k.elu_space = Region(work, probs + 3 * row, row)

    k.w1 = k.xin_space.again().take(k.hid1, P)
    space = k.fold_space.again()
    k.w1_hi, k.w1_lo = k.rounded_at("w1_hi", space, k.hid1, P), k.rounded_at("w1_lo", space, k.hid1, P)
    space = k.xin_space.again()
    k.v1_hi, k.v1_lo = k.rounded_at("v1_hi", space, k.hid2, P), k.rounded_at("v1_lo", space, k.hid2, P)
    space = k.ain_space.again()
    k.w2, k.v1, k.v2 = space.take(k.hid1, P), space.take(k.hid2, P), space.take(k.hid2, P)
    space = k.val_space.again()
    k.w_ht, k.theta, k.gram, k.diag2 = space.take(2, P), space.take(P), space.take(P), space.take(P)
    k.b_t, k.one_row = space.take(P), space.take(P)
    k.small_space = Region(work, space.start + space.used, space.size - space.used)

    k.psum_words = 8 * BANK
    k.psum = k.ctx.enter_context(k.nc.psum_tensor("psum", [P, k.psum_words], F32))
    k.always, k.constants_set, k.folded = k.sem("always"), k.sem("constants_set"), k.sem("folded")
    k.qk_folded = k.sem("qk_folded")
    k.hi_made, k.split_made = k.sem("weights_hi_made"), k.sem("weights_split")
    k.diag2_made, k.gram_ready = k.sem("diag2_made"), k.sem("gram_ready")
    k.gate_loaded, k.row_set = k.sem("gate_loaded"), k.sem("row_set")


def four_layers(nc, w, out):
    with ExitStack() as ctx:
        k = Core(nc, ctx)
        k.graphs = w["x"].shape[0]
        k.groups = k.graphs // QUAD
        k.heads = w["L0_gnn_fc_w"].shape[1] // P
        k.hid1 = w["L1_gnn_W1"].shape[1] // P
        k.hid2 = w["L2_gnn_W1"].shape[1] // P
        lay_out(k)
        prepare0 = prepare_attention(k, w)
        layer0 = attention(k, w["x"], w["adj"], prepare0)
        prepare1 = prepare_mlps(k, w, layer0)
        layer1 = rms_mlp(k, layer0, prepare1)
        layer2 = relu_mlp(k, layer1)
        layer3 = gated_highway(k, out, layer2, layer1)
        layers = (layer0, layer1, layer2, layer3)
        with nc.Block() as block:
            @block.tensor
            def _(pe):
                prepare0["tensor"](pe)
                run_layers(pe, [(layer["tensor"](pe), layer["span"]) for layer in layers])

            @block.scalar
            def _(act):
                prepare0["scalar"](act)
                run_layers(act, [(layer["scalar"](act), layer["span"]) for layer in layers])

            @block.vector
            def _(dve):
                prepare0["vector"](dve)
                run_layers(dve, [(layer["vector"](dve), layer["span"]) for layer in layers])

            @block.gpsimd
            def _(pool):
                prepare0["gpsimd"](pool)
                run_layers(pool, [(layer["gpsimd"](pool), layer["span"]) for layer in layers])

            @block.sync
            def _(sp):
                prepare0["sync"](sp)
                layer0["sync"](sp)
                prepare1["sync"](sp)
                layer3["sync"](sp)


_INS = ['x', 'adj', 'L0_gnn_fc_w', 'L0_gnn_fc_b', 'L0_gnn_q_w', 'L0_gnn_q_b', 'L0_gnn_k_w', 'L0_gnn_k_b',
        'L0_gnn_fp_w', 'L0_gnn_fp_b', 'L1_gnn_epsilon', 'L1_gnn_W1', 'L1_gnn_b1', 'L1_gnn_rms_weight', 'L1_gnn_W2',
        'L1_gnn_b2', 'L2_gnn_eps', 'L2_gnn_W1', 'L2_gnn_b1', 'L2_gnn_W2', 'L2_gnn_b2', 'L3_gnn_W_t', 'L3_gnn_b_t',
        'L3_gnn_W_h', 'L3_gnn_theta']

_BY_PARTITION = ['L0_gnn_fc_b', 'L0_gnn_fp_b', 'L1_gnn_b1', 'L1_gnn_rms_weight', 'L1_gnn_b2', 'L2_gnn_b1',
                 'L2_gnn_b2']


def kernel(**inputs):
    import numpy as _np
    import concourse.bacc as _bacc
    from concourse import mybir as _mybir
    from concourse.bass_utils import run_bass_kernel_spmd as _run

    nc = _bacc.Bacc("TRN2", target_bir_lowering=False, num_devices=1)
    arrays, args = {}, {}
    for name in _INS:
        a = _np.asarray(inputs[name])
        if name in _BY_PARTITION:
            a = a.reshape(-1, P).T
        a = _np.ascontiguousarray(a.reshape(1) if a.ndim == 0 else a)
        arrays[f"in_{name}"] = a
        args[name] = nc.dram_tensor(f"in_{name}", a.shape, _mybir.dt.from_np(a.dtype), kind="ExternalInput").ap()
    arrays["in_eye"] = _np.eye(P, dtype=_np.float32)
    args["eye"] = nc.dram_tensor("in_eye", (P, P), _mybir.dt.float32, kind="ExternalInput").ap()
    out = nc.dram_tensor("out_0", inputs["x"].shape, _mybir.dt.float32, kind="ExternalOutput").ap()
    four_layers(nc, args, out)
    r = _run(nc, [arrays], core_ids=[0])
    return r.results[0]["out_0"]
```
